# Optimizing a Trainium2 kernel written in Bass

```python
import numpy as np
import jax
import jax.numpy as jnp

def _softmax(x, axis=-1):
    return jax.nn.softmax(x, axis=axis)

def _gelu(x):
    return jax.nn.gelu(x, approximate=True)

def _silu(x):
    return jax.nn.silu(x)

def _sigmoid(x):
    return jax.nn.sigmoid(x)

def _layernorm(x, axis=-1, eps=1e-05):
    m = jnp.mean(x, axis=axis, keepdims=True)
    v = jnp.var(x, axis=axis, keepdims=True)
    return (x - m) / jnp.sqrt(v + eps)

def _scatter_add(tgt, idx, src, axis=0):
    return tgt.at[idx].add(src)

def _segment_sum(src, seg, n):
    return jax.ops.segment_sum(src, seg, n)
kernel_name = 'mk_adaln_ffn_d2_seqx_r4_870a35'

def setup_inputs(seed: int=0):
    np.random.seed(seed)
    _w = jnp.asarray

    def _rec_inputs():
        import jax
        import jax.numpy as jnp
        _rk = jax.random.key(seed)
        x = -0.000125 + 0.9999 * jax.random.normal(jax.random.fold_in(_rk, 1), (4, 512, 512), jnp.float32)
        _lenS = 512 - jax.random.randint(jax.random.fold_in(_rk, 7), (4,), 0, max(1, 512 // 4) + 1, jnp.int32)
        _lenS2 = 512 - jax.random.randint(jax.random.fold_in(_rk, 8), (4,), 0, max(1, 512 // 4) + 1, jnp.int32)
        fside_BxSxS_0 = -1.52775e-05 + 0.999936 * jax.random.normal(jax.random.fold_in(_rk, 11), (4, 512, 512), jnp.float32)
        cond_512 = -5.03954e-05 + 1.00559 * jax.random.normal(jax.random.fold_in(_rk, 12), (4, 128), jnp.float32)
        return (x, fside_BxSxS_0, cond_512)
    x, fside_BxSxS_0, cond_512 = _rec_inputs()

    def _L0_cond_setup():
        import jax, jax.numpy as jnp
        from jax import lax
        import numpy as np
        B, T, C, TD = (8, 512, 512, 128)

        def _bi_wkv(r, k, v, w, u, time_emb):
            tf = jax.nn.sigmoid(jnp.sum(time_emb, axis=-1))[:, None, None]
            decay = jnp.exp(-jnp.exp(w.astype(jnp.float32)))[None, :] * (0.5 + 0.5 * tf[:, :, 0])
            kf = k.astype(jnp.float32)
            vf = v.astype(jnp.float32)
            ek = jnp.exp(jnp.minimum(kf, 30.0))
            ekv = ek * vf

            def step(carry, x):
                a, b = carry
                ekv_t, ek_t = x
                a = a * decay + ekv_t
                b = b * decay + ek_t
                return ((a, b), (a, b))
            ekv_t = jnp.swapaxes(ekv, 0, 1)
            ek_t = jnp.swapaxes(ek, 0, 1)
            init = (jnp.zeros_like(decay), jnp.zeros_like(decay))
            _, (nf, df) = lax.scan(step, init, (ekv_t, ek_t))
            _, (nb, db) = lax.scan(step, init, (ekv_t, ek_t), reverse=True)
            nf = jnp.swapaxes(nf, 0, 1)
            df = jnp.swapaxes(df, 0, 1)
            nb = jnp.swapaxes(nb, 0, 1)
            db = jnp.swapaxes(db, 0, 1)
            euk = jnp.exp(jnp.minimum(u.astype(jnp.float32)[None, None, :] + kf, 30.0))
            num = nf + nb - ekv + euk * vf
            den = df + db - ek + euk
            base = jax.nn.sigmoid(r.astype(jnp.float32)) * (num / jnp.maximum(den, 1e-08))
            out = base * (0.8 + 0.2 * tf)
            return out.astype(r.dtype)
        key = jax.random.key(seed)
        ks = jax.random.split(key, 6)
        return {'r': jax.random.normal(ks[0], (B, T, C), dtype=jnp.float32), 'k': jax.random.normal(ks[1], (B, T, C), dtype=jnp.float32), 'v': jax.random.normal(ks[2], (B, T, C), dtype=jnp.float32), 'w': jax.random.normal(ks[3], (C,), dtype=jnp.float32), 'u': jax.random.normal(ks[4], (C,), dtype=jnp.float32), 'time_emb': jax.random.normal(ks[5], (B, TD), dtype=jnp.float32)}
    _L0_cond_all = _L0_cond_setup()
    _L0_cond_in = {k: v for k, v in _L0_cond_all.items() if k in ('w', 'u')}
    del _L0_cond_all

    def _L0_ffn_setup():
        import jax, jax.numpy as jnp
        import numpy as np
        DIM = 512
        INTER = 352
        N_EXPERTS = 16
        TOP_K = 2
        N_SHARED = 2
        SHARED_INTER = N_SHARED * INTER

        def _swiglu(t, wa, wb, wo):
            h = jax.nn.silu(t @ wa.T) * (t @ wb.T)
            return h @ wo.T
        key = jax.random.key(seed)
        ks = jax.random.split(key, 9)
        s = 0.02
        return {'x': jax.random.normal(ks[0], (4, 512, DIM), dtype=jnp.float32), 'gate_w': jax.random.normal(ks[1], (N_EXPERTS, DIM), dtype=jnp.float32) * s, 'w1': jax.random.normal(ks[2], (N_EXPERTS, INTER, DIM), dtype=jnp.float32) * s, 'w2': jax.random.normal(ks[3], (N_EXPERTS, DIM, INTER), dtype=jnp.float32) * s, 'w3': jax.random.normal(ks[4], (N_EXPERTS, INTER, DIM), dtype=jnp.float32) * s, 'sw1': jax.random.normal(ks[5], (SHARED_INTER, DIM), dtype=jnp.float32) * s, 'sw2': jax.random.normal(ks[6], (DIM, SHARED_INTER), dtype=jnp.float32) * s, 'sw3': jax.random.normal(ks[7], (SHARED_INTER, DIM), dtype=jnp.float32) * s}
    _L0_ffn_all = _L0_ffn_setup()
    _L0_ffn_in = {k: v for k, v in _L0_ffn_all.items() if k in ('gate_w', 'w1', 'w2', 'w3', 'sw1', 'sw2', 'sw3')}
    del _L0_ffn_all

    def _L1_cond_setup():
        import jax, jax.numpy as jnp
        from jax import lax
        import numpy as np
        B, T, C, TD = (8, 512, 512, 128)

        def _bi_wkv(r, k, v, w, u, time_emb):
            tf = jax.nn.sigmoid(jnp.sum(time_emb, axis=-1))[:, None, None]
            decay = jnp.exp(-jnp.exp(w.astype(jnp.float32)))[None, :] * (0.5 + 0.5 * tf[:, :, 0])
            kf = k.astype(jnp.float32)
            vf = v.astype(jnp.float32)
            ek = jnp.exp(jnp.minimum(kf, 30.0))
            ekv = ek * vf

            def step(carry, x):
                a, b = carry
                ekv_t, ek_t = x
                a = a * decay + ekv_t
                b = b * decay + ek_t
                return ((a, b), (a, b))
            ekv_t = jnp.swapaxes(ekv, 0, 1)
            ek_t = jnp.swapaxes(ek, 0, 1)
            init = (jnp.zeros_like(decay), jnp.zeros_like(decay))
            _, (nf, df) = lax.scan(step, init, (ekv_t, ek_t))
            _, (nb, db) = lax.scan(step, init, (ekv_t, ek_t), reverse=True)
            nf = jnp.swapaxes(nf, 0, 1)
            df = jnp.swapaxes(df, 0, 1)
            nb = jnp.swapaxes(nb, 0, 1)
            db = jnp.swapaxes(db, 0, 1)
            euk = jnp.exp(jnp.minimum(u.astype(jnp.float32)[None, None, :] + kf, 30.0))
            num = nf + nb - ekv + euk * vf
            den = df + db - ek + euk
            base = jax.nn.sigmoid(r.astype(jnp.float32)) * (num / jnp.maximum(den, 1e-08))
            out = base * (0.8 + 0.2 * tf)
            return out.astype(r.dtype)
        key = jax.random.key(seed)
        ks = jax.random.split(key, 6)
        return {'r': jax.random.normal(ks[0], (B, T, C), dtype=jnp.float32), 'k': jax.random.normal(ks[1], (B, T, C), dtype=jnp.float32), 'v': jax.random.normal(ks[2], (B, T, C), dtype=jnp.float32), 'w': jax.random.normal(ks[3], (C,), dtype=jnp.float32), 'u': jax.random.normal(ks[4], (C,), dtype=jnp.float32), 'time_emb': jax.random.normal(ks[5], (B, TD), dtype=jnp.float32)}
    _L1_cond_all = _L1_cond_setup()
    _L1_cond_in = {k: v for k, v in _L1_cond_all.items() if k in ('w', 'u')}
    del _L1_cond_all

    def _L1_ffn_setup():
        import jax, jax.numpy as jnp
        import numpy as np
        EPS = 1e-05

        def rms_norm(x):
            return x * jax.lax.rsqrt(jnp.mean(x * x, axis=-1, keepdims=True) + EPS)

        def act_quant(x):
            scale = 127.0 / jnp.clip(jnp.max(jnp.abs(x), axis=-1, keepdims=True), 1e-05)
            q = jnp.clip(jnp.round(x * scale), -128.0, 127.0) / scale
            return x + jax.lax.stop_gradient(q - x)

        def weight_quant(w):
            scale = 1.0 / jnp.clip(jnp.mean(jnp.abs(w)), 1e-05)
            q = jnp.clip(jnp.round(w * scale), -1.0, 1.0) / scale
            return w + jax.lax.stop_gradient(q - w)

        def bitlinear158(x, w, b):
            xq = act_quant(rms_norm(x))
            wq = weight_quant(w)
            return jnp.einsum('bsd,od->bso', xq, wq) + b

        def layer_norm(x, g, b):
            mu = jnp.mean(x, axis=-1, keepdims=True)
            var = jnp.mean((x - mu) ** 2, axis=-1, keepdims=True)
            return (x - mu) * jax.lax.rsqrt(var + EPS) * g + b
        key = jax.random.key(seed)
        ks = jax.random.split(key, 3)
        d, inner = (512, 2048)
        x = jax.random.normal(ks[0], (4, 512, d), dtype=jnp.float32)
        w1 = jax.random.normal(ks[1], (inner, d), dtype=jnp.float32) * 0.02
        b1 = jnp.zeros((inner,), jnp.float32)
        ln_g = jnp.ones((inner,), jnp.float32)
        ln_b = jnp.zeros((inner,), jnp.float32)
        w2 = jax.random.normal(ks[2], (d, inner), dtype=jnp.float32) * 0.02
        b2 = jnp.zeros((d,), jnp.float32)
        return {'x': x, 'w1': w1, 'b1': b1, 'ln_g': ln_g, 'ln_b': ln_b, 'w2': w2, 'b2': b2}
    _L1_ffn_all = _L1_ffn_setup()
    _L1_ffn_in = {k: v for k, v in _L1_ffn_all.items() if k in ('w1', 'b1', 'ln_g', 'ln_b', 'w2', 'b2')}
    del _L1_ffn_all
    return {'x': x, 'fside_BxSxS_0': fside_BxSxS_0, 'cond_512': cond_512, 'L0_cond_w': _L0_cond_in['w'], 'L0_cond_u': _L0_cond_in['u'], 'L0_ffn_gate_w': _L0_ffn_in['gate_w'], 'L0_ffn_w1': _L0_ffn_in['w1'], 'L0_ffn_w2': _L0_ffn_in['w2'], 'L0_ffn_w3': _L0_ffn_in['w3'], 'L0_ffn_sw1': _L0_ffn_in['sw1'], 'L0_ffn_sw2': _L0_ffn_in['sw2'], 'L0_ffn_sw3': _L0_ffn_in['sw3'], 'L1_cond_w': _L1_cond_in['w'], 'L1_cond_u': _L1_cond_in['u'], 'L1_ffn_w1': _L1_ffn_in['w1'], 'L1_ffn_b1': _L1_ffn_in['b1'], 'L1_ffn_ln_g': _L1_ffn_in['ln_g'], 'L1_ffn_ln_b': _L1_ffn_in['ln_b'], 'L1_ffn_w2': _L1_ffn_in['w2'], 'L1_ffn_b2': _L1_ffn_in['b2']}

def reference(x, fside_BxSxS_0, cond_512, L0_cond_w, L0_cond_u, L0_ffn_gate_w, L0_ffn_w1, L0_ffn_w2, L0_ffn_w3, L0_ffn_sw1, L0_ffn_sw2, L0_ffn_sw3, L1_cond_w, L1_cond_u, L1_ffn_w1, L1_ffn_b1, L1_ffn_ln_g, L1_ffn_ln_b, L1_ffn_w2, L1_ffn_b2):
    import jax
    import jax.numpy as jnp

    def _L0_cond_ref(r, k, v, w, u, time_emb):
        import jax, jax.numpy as jnp
        from jax import lax
        import numpy as np
        B, T, C, TD = (8, 512, 512, 128)

        def _bi_wkv(r, k, v, w, u, time_emb):
            tf = jax.nn.sigmoid(jnp.sum(time_emb, axis=-1))[:, None, None]
            decay = jnp.exp(-jnp.exp(w.astype(jnp.float32)))[None, :] * (0.5 + 0.5 * tf[:, :, 0])
            kf = k.astype(jnp.float32)
            vf = v.astype(jnp.float32)
            ek = jnp.exp(jnp.minimum(kf, 30.0))
            ekv = ek * vf

            def step(carry, x):
                a, b = carry
                ekv_t, ek_t = x
                a = a * decay + ekv_t
                b = b * decay + ek_t
                return ((a, b), (a, b))
            ekv_t = jnp.swapaxes(ekv, 0, 1)
            ek_t = jnp.swapaxes(ek, 0, 1)
            init = (jnp.zeros_like(decay), jnp.zeros_like(decay))
            _, (nf, df) = lax.scan(step, init, (ekv_t, ek_t))
            _, (nb, db) = lax.scan(step, init, (ekv_t, ek_t), reverse=True)
            nf = jnp.swapaxes(nf, 0, 1)
            df = jnp.swapaxes(df, 0, 1)
            nb = jnp.swapaxes(nb, 0, 1)
            db = jnp.swapaxes(db, 0, 1)
            euk = jnp.exp(jnp.minimum(u.astype(jnp.float32)[None, None, :] + kf, 30.0))
            num = nf + nb - ekv + euk * vf
            den = df + db - ek + euk
            base = jax.nn.sigmoid(r.astype(jnp.float32)) * (num / jnp.maximum(den, 1e-08))
            out = base * (0.8 + 0.2 * tf)
            return out.astype(r.dtype)
        return _bi_wkv(r, k, v, w, u, time_emb)

    def _L0_ffn_ref(x, gate_w, w1, w2, w3, sw1, sw2, sw3):
        import jax, jax.numpy as jnp
        import numpy as np
        DIM = 512
        INTER = 352
        N_EXPERTS = 16
        TOP_K = 2
        N_SHARED = 2
        SHARED_INTER = N_SHARED * INTER

        def _swiglu(t, wa, wb, wo):
            h = jax.nn.silu(t @ wa.T) * (t @ wb.T)
            return h @ wo.T
        shape = x.shape
        t = x.reshape(-1, DIM)
        scores = jax.nn.softmax(t @ gate_w.T, axis=-1)
        weights, indices = jax.lax.top_k(scores, TOP_K)
        y = jnp.zeros_like(t)
        for e in range(N_EXPERTS):
            w_e = jnp.sum(jnp.where(indices == e, weights, 0.0), axis=-1)
            y = y + _swiglu(t, w1[e], w3[e], w2[e]) * w_e[:, None]
        z = _swiglu(t, sw1, sw3, sw2)
        return (y + z).reshape(shape)

    def _L1_cond_ref(r, k, v, w, u, time_emb):
        import jax, jax.numpy as jnp
        from jax import lax
        import numpy as np
        B, T, C, TD = (8, 512, 512, 128)

        def _bi_wkv(r, k, v, w, u, time_emb):
            tf = jax.nn.sigmoid(jnp.sum(time_emb, axis=-1))[:, None, None]
            decay = jnp.exp(-jnp.exp(w.astype(jnp.float32)))[None, :] * (0.5 + 0.5 * tf[:, :, 0])
            kf = k.astype(jnp.float32)
            vf = v.astype(jnp.float32)
            ek = jnp.exp(jnp.minimum(kf, 30.0))
            ekv = ek * vf

            def step(carry, x):
                a, b = carry
                ekv_t, ek_t = x
                a = a * decay + ekv_t
                b = b * decay + ek_t
                return ((a, b), (a, b))
            ekv_t = jnp.swapaxes(ekv, 0, 1)
            ek_t = jnp.swapaxes(ek, 0, 1)
            init = (jnp.zeros_like(decay), jnp.zeros_like(decay))
            _, (nf, df) = lax.scan(step, init, (ekv_t, ek_t))
            _, (nb, db) = lax.scan(step, init, (ekv_t, ek_t), reverse=True)
            nf = jnp.swapaxes(nf, 0, 1)
            df = jnp.swapaxes(df, 0, 1)
            nb = jnp.swapaxes(nb, 0, 1)
            db = jnp.swapaxes(db, 0, 1)
            euk = jnp.exp(jnp.minimum(u.astype(jnp.float32)[None, None, :] + kf, 30.0))
            num = nf + nb - ekv + euk * vf
            den = df + db - ek + euk
            base = jax.nn.sigmoid(r.astype(jnp.float32)) * (num / jnp.maximum(den, 1e-08))
            out = base * (0.8 + 0.2 * tf)
            return out.astype(r.dtype)
        return _bi_wkv(r, k, v, w, u, time_emb)

    def _L1_ffn_ref(x, w1, b1, ln_g, ln_b, w2, b2):
        import jax, jax.numpy as jnp
        import numpy as np
        EPS = 1e-05

        def rms_norm(x):
            return x * jax.lax.rsqrt(jnp.mean(x * x, axis=-1, keepdims=True) + EPS)

        def act_quant(x):
            scale = 127.0 / jnp.clip(jnp.max(jnp.abs(x), axis=-1, keepdims=True), 1e-05)
            q = jnp.clip(jnp.round(x * scale), -128.0, 127.0) / scale
            return x + jax.lax.stop_gradient(q - x)

        def weight_quant(w):
            scale = 1.0 / jnp.clip(jnp.mean(jnp.abs(w)), 1e-05)
            q = jnp.clip(jnp.round(w * scale), -1.0, 1.0) / scale
            return w + jax.lax.stop_gradient(q - w)

        def bitlinear158(x, w, b):
            xq = act_quant(rms_norm(x))
            wq = weight_quant(w)
            return jnp.einsum('bsd,od->bso', xq, wq) + b

        def layer_norm(x, g, b):
            mu = jnp.mean(x, axis=-1, keepdims=True)
            var = jnp.mean((x - mu) ** 2, axis=-1, keepdims=True)
            return (x - mu) * jax.lax.rsqrt(var + EPS) * g + b
        h = jax.nn.silu(bitlinear158(x, w1, b1))
        h = jax.nn.gelu(h, approximate=False)
        h = layer_norm(h, ln_g, ln_b)
        return bitlinear158(h, w2, b2)
    x = x + _L0_ffn_ref(_L0_cond_ref(x, fside_BxSxS_0, fside_BxSxS_0, L0_cond_w, L0_cond_u, cond_512), L0_ffn_gate_w, L0_ffn_w1, L0_ffn_w2, L0_ffn_w3, L0_ffn_sw1, L0_ffn_sw2, L0_ffn_sw3)
    x = x + _L1_ffn_ref(_L1_cond_ref(x, fside_BxSxS_0, fside_BxSxS_0, L1_cond_w, L1_cond_u, cond_512), L1_ffn_w1, L1_ffn_b1, L1_ffn_ln_g, L1_ffn_ln_b, L1_ffn_w2, L1_ffn_b2)
    return x

_drawn_inputs = setup_inputs


def setup_inputs(seed=0):
    import zlib

    import numpy as np

    out = dict(_drawn_inputs(seed))
    spreads = {'L1_ffn_b1': (0.0, 0.1),
     'L1_ffn_ln_g': (1.0, 0.537),
     'L1_ffn_ln_b': (0.0, 0.514),
     'L1_ffn_b2': (0.0, 0.303)}
    factors = {'L0_cond_w': 5.674,
     'L0_cond_u': 8.0,
     'L0_ffn_gate_w': 8.0,
     'L0_ffn_w1': 8.0,
     'L0_ffn_w2': 8.0,
     'L0_ffn_w3': 8.0,
     'L0_ffn_sw1': 4.184,
     'L0_ffn_sw2': 4.14,
     'L0_ffn_sw3': 4.16,
     'L1_cond_u': 3.094}
    for name, (base, spread) in spreads.items():
        noise = np.random.default_rng([zlib.crc32(name.encode()), seed]).standard_normal(out[name].shape)
        drawn = base * np.exp(spread * noise) if base else spread * noise
        out[name] = jnp.asarray(drawn.astype(out[name].dtype))
    for name, factor in factors.items():
        out[name] = (out[name] * factor).astype(out[name].dtype)
    return out
```

```python
from contextlib import ExitStack

import concourse.bass as bass
from concourse import mybir

P = 128
F32 = mybir.dt.float32
F32R = mybir.dt.float32r
BF16 = mybir.dt.bfloat16
I32 = mybir.dt.int32
ALU = mybir.AluOpType
ACT = mybir.ActivationFunctionType
AX_X = mybir.AxisListType.X

B, T, C = 4, 512, 512
CK = C // P
TT = T // P
NT = B * TT
E, TOPK = 16, 2
F = 352
FT = 3
SF = 704
SFT = 6
INNER = 2048
IK = INNER // P
NBLK = (B * T * TOPK + E * (P - 1)) // P
SLOTS = NBLK * P
PIECE = 1024
NPIECE = C * INNER // P // PIECE
ROUND = 12582912.0
EPS = 1e-5


def ds(i, n=1):
    return bass.ds(i, n)


def f32(ap):
    return ap.bitcast(F32)


def build(nc, xT, kT, x, cond, wu, gate, sw13, sw2, w13, w2, w1p, w2p, b1, lng, lnb, b2, out,
          xslots, yslots, yshared, upto=5):
    with ExitStack() as ctx:
        base = nc.sbuf_base
        base += -base % 64
        top = [base]

        def region(nbytes):
            at = top[0]
            top[0] += nbytes + (-nbytes % 64)
            return at

        def at(name, shape, dt, offset):
            return nc.alloc_sbuf_tensor_at(name, shape, dt, offset=offset)

        def size(shape, dt):
            n = 2 if dt == BF16 else 4
            for s in shape[1:]:
                n *= s
            return n

        def place(offset, tensors):
            got = []
            for name, shape, dt in tensors:
                got.append(at(name, shape, dt, offset))
                offset += size(shape, dt) + (-size(shape, dt) % 64)
            return got, offset

        def keep(name, shape, dt):
            return at(name, shape, dt, region(size(shape, dt)))

        ident = keep("ident", [P, P], F32)
        ident_b = keep("ident_b", [P, P], BF16)
        ones = keep("ones", [P, P], F32)
        decay = keep("decay", [P, 2, B, CK], F32)
        wu_sb = keep("wu_sb", [P, 4, CK], F32)
        ofac = keep("ofac", [P, B], F32)
        probs = keep("probs", [P, NT, E], F32)
        weight = keep("weight", [P, TOPK, NT], F32)
        slot = keep("slot", [P, TOPK, NT], I32)
        block_expert = keep("block_expert", [1, NBLK + 1], I32)
        wscale = keep("wscale", [P, 2], F32)

        A = region(2 * 4 * (2 * CK * SF + SFT * C))
        Bx = region(2 * 2 * CK * T * 4)
        Ch = region(2 * SFT * T * 4)
        D = region(NT * C * 4)
        W = region(40960)
        Y = region(2 * C * 4)
        assert top[0] <= nc.sbuf_usable_end, (top[0], nc.sbuf_usable_end)

        ratio = at("ratio", [P, NT, C], F32, Bx)
        (w1q, w2q), _ = place(W, [("w1q", [P, NPIECE, PIECE], BF16), ("w2q", [P, NPIECE, PIECE], BF16)])
        y_sb = at("y_sb", [P, 2, C], F32, Y)

        def wkv_buffers(tag, at_):
            bufs, _ = place(at_, [
                (f"k_in{tag}", [P, 2, T], F32),
                (f"x_in{tag}", [P, 2, T], F32),
                (f"ev{tag}", [P, 2, 2, T], F32),
                (f"uv{tag}", [P, 2, 2, T], F32),
                (f"fw{tag}", [P, 2, T], F32),
                (f"bw{tag}", [P, 2, T], F32),
                (f"mixed{tag}", [P, 2, T], F32)])
            return bufs

        class Sems:

            def __init__(self, ctx_, tag):
                self.ctx, self.tag, self.made = ctx_, tag, {}

            def __getitem__(self, name):
                if name not in self.made:
                    self.made[name] = self.ctx.enter_context(nc.semaphore(f"{self.tag}_{name}"))
                return self.made[name]

        with ExitStack() as st:
            s = Sems(st, "c")
            (cond_sb, ea, tf, dfac), _ = place(A, [
                ("cond_sb", [P, B], F32), ("ea", [P, 2, CK], F32), ("tf", [P, B], F32), ("dfac", [P, B], F32)])
            ps_c = st.enter_context(nc.psum_tensor("ps_c", [P, 512], F32))
            block = st.enter_context(nc.Block())

            @block.sync
            def _(sp):
                sp.dma_start(cond_sb[:], cond).then_inc(s["small_in"], 16)
                sp.dma_start(wu_sb[:], wu).then_inc(s["small_in"], 16)

            @block.gpsimd
            def _(pool):
                pool.memset(ones[:], 1.0).then_inc(s["tables"], 1)
                pool.memset(ident[:], 0.0).then_inc(s["tables"], 1)
                pool.wait_ge(s["tables"], 2)
                pool.affine_select(out=ident[:], in_=ident[:], compare_op=ALU.not_equal, fill=1.0, base=0,
                                   pattern=[[-1, P]], channel_multiplier=1).then_inc(s["tables"], 1)
                pool.wait_ge(s["tables"], 3)
                pool.tensor_copy(ident_b[:], ident[:]).then_inc(s["tables"], 1)

            @block.tensor
            def _(pe):
                pe.wait_ge(s["small_in"], 32)
                pe.wait_ge(s["tables"], 1)
                pe.matmul(ps_c[:, 0:B], ones[:], cond_sb[:], start=True, stop=True).then_inc(s["cond_sum"], 1)

            @block.scalar
            def _(act):
                act.wait_ge(s["small_in"], 32)
                wv = wu_sb[:].rearrange("p (l k) c -> p l k c", k=2)[:, :, 0, :]
                act.activation(ea[:], wv, ACT.Exp).then_inc(s["exp_w"], 1)
                act.wait_ge(s["exp_w"], 1)
                act.activation(ea[:], ea[:], ACT.Exp, scale=-1.0).then_inc(s["exp_w"], 1)
                act.wait_ge(s["cond_sum"], 1)
                act.activation(tf[:], ps_c[:, 0:B], ACT.Exp, scale=-1.0).then_inc(s["exp_s"], 1)

            @block.vector
            def _(dve):
                dve.wait_ge(s["exp_s"], 1)
                dve.tensor_scalar(tf[:], tf[:], 1.0, None, ALU.add).then_inc(s["tf"], 1)
                dve.wait_ge(s["tf"], 1)
                dve.reciprocal(tf[:], tf[:]).then_inc(s["tf"], 1)
                dve.wait_ge(s["tf"], 2)
                dve.tensor_scalar(dfac[:], tf[:], 0.5, 0.5, ALU.mult, ALU.add).then_inc(s["tf"], 1)
                dve.tensor_scalar(ofac[:], tf[:], 0.2, 0.8, ALU.mult, ALU.add).then_inc(s["tf"], 1)
                dve.wait_ge(s["tf"], 3)
                dve.wait_ge(s["exp_w"], 2)
                for b in range(B):
                    dve.tensor_scalar(decay[:, :, b, :], ea[:], dfac[:, b:b + 1], None, ALU.mult).then_inc(s["decay"], 1)

        def wkv(layer, s, bufs):
            k_in, x_in, ev, uv, fw, bw, mixed = bufs
            with_x = layer == 0

            def load(sp, b, c, first):
                p = c % 2
                u = CK * b + c
                if not first:
                    sp.wait_ge(s["uv_ready"], u - 1)
                sp.dma_start(k_in[:, p], kT[ds(b), c].rearrange("a p t -> p (a t)")).then_inc(s[f"k_in{p}"], 16)
                if with_x:
                    if not first:
                        sp.wait_ge(s["mixed_ready"], u - 1)
                    sp.dma_start(x_in[:, p], xT[ds(b), c].rearrange("a p t -> p (a t)")).then_inc(s[f"x_in{p}"], 16)

            def landed(b, c):
                return 16 * (2 * b + c // 2 + 1)

            def prep_dve(dve, b, c):
                p = c % 2
                dve.wait_ge(s[f"k_in{p}"], landed(b, c))
                dve.tensor_scalar(ev[:, p, 1], k_in[:, p], 30.0, None, ALU.min).then_inc(s["k_clipped"], 1)
                dve.tensor_scalar(uv[:, p, 1], k_in[:, p], wu_sb[:, 2 * layer + 1, c:c + 1], 30.0,
                                  ALU.add, ALU.min).then_inc(s["uk_clipped"], 1)

            def prep_act(act, b, c):
                p, u = c % 2, CK * b + c
                act.wait_ge(s["k_clipped"], u + 1)
                act.activation(ev[:, p, 1], ev[:, p, 1], ACT.Exp).then_inc(s["ek_ready"], 1)
                act.wait_ge(s["uk_clipped"], u + 1)
                act.activation(uv[:, p, 1], uv[:, p, 1], ACT.Exp).then_inc(s["eu_ready"], 1)
                if with_x:
                    act.wait_ge(s[f"x_in{p}"], landed(b, c))
                    act.activation(x_in[:, p], x_in[:, p], ACT.Exp, scale=-1.0).then_inc(s["ex"], 1)
                    act.wait_ge(s["ex"], 2 * u + 1)
                    act.activation(x_in[:, p], x_in[:, p], ACT.Copy, bias=1.0).then_inc(s["ex"], 1)

            def prep_pool(pool, b, c):
                p, u = c % 2, CK * b + c
                pool.wait_ge(s["ek_ready"], u + 1)
                pool.tensor_tensor(ev[:, p, 0], ev[:, p, 1], k_in[:, p], ALU.mult).then_inc(s["ev_ready"], 1)
                pool.wait_ge(s["eu_ready"], u + 1)
                pool.tensor_tensor(uv[:, p, 0], uv[:, p, 1], k_in[:, p], ALU.mult).then_inc(s["uv_ready"], 1)

            def mix_dve(dve, b, c, first):
                p, u = c % 2, CK * b + c
                d = decay[:, layer, ds(b), c]
                steps = 8
                dve.wait_ge(s["ev_ready"], u + 1)
                if not (first and c == 0):
                    dve.wait_ge(s["mixed_ready"], u)
                for j in range(2):
                    dve.tensor_tensor_scan(fw[:, j], d.to_broadcast([P, T]), ev[:, p, j], 0.0,
                                           ALU.mult, ALU.add).then_inc(s["step"], 1)
                for j in range(2):
                    dve.tensor_tensor_scan(bw[:, j, ::-1], d.to_broadcast([P, T]), ev[:, p, j, ::-1], 0.0,
                                           ALU.mult, ALU.add).then_inc(s["step"], 1)
                dve.wait_ge(s["step"], steps * u + 4)
                dve.scalar_tensor_tensor(out=fw[:, :, 0:T - 1], in0=bw[:, :, 1:T], scalar=d, in1=fw[:, :, 0:T - 1],
                                         op0=ALU.mult, op1=ALU.add).then_inc(s["step"], 1)
                dve.wait_ge(s["uv_ready"], u + 1)
                dve.wait_ge(s["step"], steps * u + 5)
                dve.tensor_tensor(fw[:], fw[:], uv[:, p], ALU.add).then_inc(s["step"], 1)
                dve.wait_ge(s["step"], steps * u + 6)
                if with_x:
                    dve.wait_ge(s["ex"], 2 * u + 2)
                    dve.scalar_tensor_tensor(out=fw[:, 1], in0=fw[:, 1], scalar=1e-8, in1=x_in[:, p],
                                             op0=ALU.max, op1=ALU.mult).then_inc(s["step"], 1)
                else:
                    dve.tensor_scalar(fw[:, 1], fw[:, 1], 1e-8, None, ALU.max).then_inc(s["step"], 1)
                dve.wait_ge(s["step"], steps * u + 7)
                dve.reciprocal(fw[:, 1], fw[:, 1]).then_inc(s["step"], 1)
                dve.wait_ge(s["step"], steps * u + 8)
                if not first:
                    dve.wait_ge(s["mixed_read" if with_x else "turned"], u - 1)
                    if with_x:
                        dve.wait_ge(s["x_lo"], u - 1)
                dve.scalar_tensor_tensor(out=mixed[:, p], in0=fw[:, 0], scalar=ofac[:, ds(b)], in1=fw[:, 1],
                                         op0=ALU.mult, op1=ALU.mult).then_inc(s["mixed_ready"], 1)

            return load, prep_dve, prep_act, prep_pool, mix_dve

        if upto < 1:
            return
        tok = at("tok", [P, NT, C], F32, D)
        with ExitStack() as st:
            s = Sems(st, "m")
            bufs = wkv_buffers("0", W)
            load, prep_dve, prep_act, prep_pool, mix_dve = wkv(0, s, bufs)
            mixed = bufs[-1]
            (s13h, s13l, s2h, s2l), _ = place(A, [
                ("s13h", [P, 2, CK, SF], F32R), ("s13l", [P, 2, CK, SF], F32R),
                ("s2h", [P, SFT, C], F32R), ("s2l", [P, SFT, C], F32R)])
            (xh, xl), _ = place(Bx, [("xh", [P, 2, CK, T], F32R), ("xl", [P, 2, CK, T], F32R)])
            (hh, hl), _ = place(Ch, [("hh", [P, SFT, T], F32R), ("hl", [P, SFT, T], F32R)])
            stage = at("stage", [P, 4, SF], F32, D + 8 * C * 4)
            zero = at("zero", [P, C], F32, Ch)
            gate_sb = at("gate_sb", [P, CK, E], F32, top[0])
            hbase = top[0] + CK * E * 4
            (th, hf), hend = place(hbase, [("th", [P, T], F32), ("hf", [P, T], F32)])
            assert hend <= nc.sbuf_usable_end, (hend, nc.sbuf_usable_end)
            ps_t = st.enter_context(nc.psum_tensor("ps_t", [P, TT, P], F32))
            ps_l = st.enter_context(nc.psum_tensor("ps_l", [P, 512], F32))
            ps_u = st.enter_context(nc.psum_tensor("ps_u", [P, 2, 2, T], F32))
            ps_y = st.enter_context(nc.psum_tensor("ps_y", [P, 2, C], F32))
            ps_lg = ps_l[:, 0:TT * E].rearrange("p (t e) -> p t e", e=E)
            block = st.enter_context(nc.Block())

            pieces = [(sw13[w, c], s13h[:, w, c], s13l[:, w, c], P, SF) for w in range(2) for c in range(CK)]
            for f in range(SFT):
                rows = min(P, SF - f * P)
                pieces.append((sw2[f * P:f * P + rows], s2h[0:rows, f], s2l[0:rows, f], rows, C))
            cut = [0, 4, 8, 12, len(pieces)]

            def rows_of(f):
                return min(P, SF - f * P)

            @block.sync
            def _(sp):
                sp.dma_start(gate_sb[:], gate).then_inc(s["gate_in"], 16)
                load(sp, 0, 0, True)
                load(sp, 0, 1, True)
                for n, (src, _, _, rows, cols) in enumerate(pieces):
                    if n >= 4:
                        sp.wait_ge(s["piece_lo"], n - 3)
                    sp.dma_start(stage[0:rows, n % 4, 0:cols], src).then_inc(s[f"piece_in{n % 4}"], 16)
                    if n == 5:
                        load(sp, 0, 2, False)
                    if n == 9:
                        load(sp, 0, 3, False)

                def store(b, t):
                    y = TT * b + t
                    sp.wait_ge(s["y_evicted"], y + 1)
                    sp.dma_start(yshared[ds(y)].rearrange("a p n -> p (a n)"), y_sb[:, t % 2]).then_inc(s[f"y_out{t % 2}"], 16)

                sp.wait_ge(s["zero"], 1)
                sp.dma_start(xslots.rearrange("(n p) c -> p n c", p=P),
                             zero[:].unsqueeze(1).to_broadcast([P, NBLK, C])).then_inc(s["cleared"], 16)
                with sp.Fori(1, B) as b:
                    for c in range(CK):
                        load(sp, b, c, False)
                    for t in range(TT):
                        store(b - 1, t)
                for t in range(TT):
                    store(B - 1, t)
                for p in range(2):
                    sp.wait_ge(s[f"y_out{p}"], 16 * NT // 2)

            @block.gpsimd
            def _(pool):
                def x_lo(b, c):
                    u = CK * b + c
                    pool.wait_ge(s["x_hi"], u + 1)
                    pool.tensor_tensor(xl[:, ds(b % 2), c].rearrange("p a t -> p (a t)"), mixed[:, c % 2],
                                       f32(xh[:, ds(b % 2), c].rearrange("p a t -> p (a t)")), ALU.subtract).then_inc(s["x_lo"], 1)

                def h_lo(b, f):
                    n = SFT * b + f
                    r = rows_of(f)
                    pool.wait_ge(s["h_hi"], n + 1)
                    pool.tensor_tensor(hl[0:r, f], hf[0:r], f32(hh[0:r, f]), ALU.subtract).then_inc(s["h_lo"], 1)

                pool.memset(zero[:], 0.0).then_inc(s["zero"], 1)
                prep_pool(pool, 0, 0)
                for c in range(CK):
                    if c + 1 < CK:
                        prep_pool(pool, 0, c + 1)
                    for n in range(cut[c], cut[c + 1]):
                        _, hi, lo, rows, cols = pieces[n]
                        pool.wait_ge(s["piece_hi"], n + 1)
                        pool.tensor_tensor(lo, stage[0:rows, n % 4, 0:cols], f32(hi), ALU.subtract).then_inc(s["piece_lo"], 1)
                    x_lo(0, c)
                with pool.Fori(1, B) as b:
                    prep_pool(pool, b, 0)
                    for c in range(CK):
                        if c + 1 < CK:
                            prep_pool(pool, b, c + 1)
                        if c > 0:
                            h_lo(b - 1, 2 * c - 2)
                            h_lo(b - 1, 2 * c - 1)
                        x_lo(b, c)
                for f in range(SFT):
                    h_lo(B - 1, f)

            @block.scalar
            def _(act):
                def x_hi(b, c, first):
                    u = CK * b + c
                    act.wait_ge(s["mixed_ready"], u + 1)
                    if not first:
                        act.wait_ge(s["up_done"], SFT * (b - 1))
                    act.activation(xh[:, ds(b % 2), c].rearrange("p a t -> p (a t)"), mixed[:, c % 2], ACT.Copy).then_inc(s["x_hi"], 1)
                    act.wait_ge(s["turned"], u + 1)
                    act.activation(tok[:, ds(TT * b, TT), c * P:(c + 1) * P], ps_t[:], ACT.Copy).then_inc(s["tok_ready"], 1)

                def hidden(b, f, first):
                    n = SFT * b + f
                    r = rows_of(f)
                    act.wait_ge(s["up_done"], n + 1)
                    act.activation(th[0:r], ps_u[0:r, f % 2, 0], ACT.Tanh, scale=0.5).then_inc(s["tanh"], 1)
                    act.wait_ge(s["hidden"], n + 1)
                    if not first:
                        act.wait_ge(s["down_done"], TT * b)
                    act.activation(hh[0:r, f], hf[0:r], ACT.Copy).then_inc(s["h_hi"], 1)

                def evict(b, t, first):
                    y = TT * b + t
                    act.wait_ge(s["down_done"], y + 1)
                    if not first:
                        act.wait_ge(s[f"y_out{t % 2}"], 16 * (2 * b + t // 2))
                    act.activation(y_sb[:, t % 2], ps_y[:, t % 2], ACT.Copy).then_inc(s["y_evicted"], 1)

                prep_act(act, 0, 0)
                for c in range(CK):
                    if c + 1 < CK:
                        prep_act(act, 0, c + 1)
                    for n in range(cut[c], cut[c + 1]):
                        _, hi, _, rows, cols = pieces[n]
                        act.wait_ge(s[f"piece_in{n % 4}"], 16 * (n // 4 + 1))
                        act.activation(hi, stage[0:rows, n % 4, 0:cols], ACT.Copy).then_inc(s["piece_hi"], 1)
                    x_hi(0, c, True)

                def batch(b, first):
                    prep_act(act, b, 0)
                    for c in range(CK):
                        if c + 1 < CK:
                            prep_act(act, b, c + 1)
                        if c > 0:
                            hidden(b - 1, 2 * c - 2, first)
                            hidden(b - 1, 2 * c - 1, first)
                        x_hi(b, c, first)
                    for t in range(TT):
                        evict(b - 1, t, first and t < 2)

                act.wait_ge(s["cleared"], 16)
                batch(1, True)
                with act.Fori(2, B) as b:
                    batch(b, False)
                for f in range(SFT):
                    hidden(B - 1, f, False)
                for t in range(TT):
                    evict(B - 1, t, False)

            @block.vector
            def _(dve):
                def hidden(b, f, first):
                    n = SFT * b + f
                    r = rows_of(f)
                    dve.wait_ge(s["tanh"], n + 1)
                    dve.scalar_tensor_tensor(out=th[0:r], in0=th[0:r], scalar=1.0, in1=ps_u[0:r, f % 2, 0],
                                             op0=ALU.add, op1=ALU.mult).then_inc(s["silu"], 1)
                    dve.wait_ge(s["silu"], n + 1)
                    if not first:
                        dve.wait_ge(s["h_lo"], n)
                    dve.scalar_tensor_tensor(out=hf[0:r], in0=th[0:r], scalar=0.5, in1=ps_u[0:r, f % 2, 1],
                                             op0=ALU.mult, op1=ALU.mult).then_inc(s["hidden"], 1)

                def logits(b):
                    dve.wait_ge(s["mixed_read"], CK * (b + 1))
                    dve.tensor_copy(probs[:, ds(TT * b, TT), :], ps_lg).then_inc(s["logits_read"], 1)

                prep_dve(dve, 0, 0)
                for c in range(CK):
                    if c + 1 < CK:
                        prep_dve(dve, 0, c + 1)
                    mix_dve(dve, 0, c, c < 2)
                logits(0)

                def batch(b, first):
                    prep_dve(dve, b, 0)
                    for c in range(CK):
                        if c + 1 < CK:
                            prep_dve(dve, b, c + 1)
                        if c > 0:
                            hidden(b - 1, 2 * c - 2, first and c == 1)
                            hidden(b - 1, 2 * c - 1, False)
                        mix_dve(dve, b, c, False)
                    logits(b)

                batch(1, True)
                with dve.Fori(2, B) as b:
                    batch(b, False)
                for f in range(SFT):
                    hidden(B - 1, f, False)

            @block.tensor
            def _(pe):
                def turn(b, c, first_unit, first_batch):
                    u = CK * b + c
                    m = mixed[:, c % 2]
                    pe.wait_ge(s["mixed_ready"], u + 1)
                    if not first_unit:
                        pe.wait_ge(s["tok_ready"], u)
                    for t in range(TT):
                        last = pe.transpose(ps_t[:, t], m[:, t * P:(t + 1) * P], ident[:])
                    last.then_inc(s["turned"], 1)
                    if c == 0 and not first_batch:
                        pe.wait_ge(s["logits_read"], b)
                    for t in range(TT):
                        last = pe.matmul(ps_lg[:, t], m[:, t * P:(t + 1) * P], gate_sb[:, c], start=(c == 0 and t == 0),
                                         stop=(c == CK - 1 and t == TT - 1), skip_group_check=True)
                        if t == TT - 1:
                            last.then_inc(s["mixed_read"], 1)
                    
                def up(b, f, first):
                    n = SFT * b + f
                    r = rows_of(f)
                    if f % 2 == 0 and not first:
                        pe.wait_ge(s["hidden"], n)
                    if f == 0:
                        pe.wait_ge(s["x_lo"], CK * (b + 1))
                    for w in range(2):
                        for c in range(CK):
                            hi, lo = s13h[:, w, c, f * P:f * P + r], s13l[:, w, c, f * P:f * P + r]
                            rh = xh[:, ds(b % 2), c].rearrange("p a t -> p (a t)")
                            rl = xl[:, ds(b % 2), c].rearrange("p a t -> p (a t)")
                            for i, (l_, r_) in enumerate(((hi, rh), (hi, rl), (lo, rh))):
                                last = pe.matmul(ps_u[0:r, f % 2, w], l_, r_, start=(c == 0 and i == 0),
                                                 stop=(c == CK - 1 and i == 2))
                    last.then_inc(s["up_done"], 1)

                def down(b, t, first):
                    y = TT * b + t
                    if not first:
                        pe.wait_ge(s["y_evicted"], y - 1)
                    if t == 0:
                        pe.wait_ge(s["h_lo"], SFT * (b + 1))
                    for f in range(SFT):
                        r = rows_of(f)
                        hi, lo = hh[0:r, f, t * P:(t + 1) * P], hl[0:r, f, t * P:(t + 1) * P]
                        for i, (l_, r_) in enumerate(((hi, s2h[0:r, f]), (hi, s2l[0:r, f]), (lo, s2h[0:r, f]))):
                            last = pe.matmul(ps_y[:, t % 2], l_, r_, start=(f == 0 and i == 0),
                                             stop=(f == SFT - 1 and i == 2))
                    last.then_inc(s["down_done"], 1)

                pe.wait_ge(s["gate_in"], 16)
                for c in range(CK):
                    turn(0, c, c == 0, True)
                pe.wait_ge(s["piece_lo"], len(pieces))

                def batch(b, first):
                    for c in range(CK):
                        turn(b, c, False, False)
                        if c < CK - 1:
                            up(b - 1, 2 * c, first and c == 0)
                            up(b - 1, 2 * c + 1, first and c == 0)
                        else:
                            for t in range(TT):
                                down(b - 1, t, first and t < 2)

                batch(1, True)
                with pe.Fori(2, B) as b:
                    batch(b, False)
                for f in range(SFT):
                    up(B - 1, f, False)
                for t in range(TT):
                    down(B - 1, t, False)

        if upto < 2:
            return
        with ExitStack() as st:
            s = Sems(st, "r")
            bufs = wkv_buffers("1", A)
            load, prep_dve, prep_act, prep_pool, mix_dve = wkv(1, s, bufs)
            mixed = bufs[-1]
            (raw, shifted), _ = place(A + 40960, [
                ("raw", [P, 2, PIECE], F32), ("shifted", [P, 2, PIECE], F32)])
            tables, _ = place(Ch, [
                ("below", [P, P], BF16), ("ones_b", [P, P], BF16), ("mask", [P, NT, E], BF16),
                ("index16", [P, E], F32), ("full", [P, NT], F32), ("block_no", [1, NBLK + 1], F32),
                ("top", [P, NT], F32), ("cand", [P, NT, E], F32), ("chosen", [P, TOPK, NT, E], F32),
                ("rank", [P, NT, E], F32), ("many", [P, E, NT], F32), ("blocks", [P, E], F32),
                ("ends", [P, E], F32), ("first", [P, E], F32), ("slotf", [P, TOPK, NT], F32),
                ("count", [P, E], F32), ("past", [1, NBLK + 1, E], F32), ("owner", [1, NBLK + 1], F32),
                ("abs_sum", [P, 2 * NPIECE], F32), ("wtotal", [P, 2], F32), ("winv", [P, 2], F32)])
            (below, ones_b, mask, index16, full, block_no, top_, cand, chosen, rank, many, blocks,
             ends, first_, slotf, count, past, owner, abs_sum, wtotal, winv) = tables
            ps_t = st.enter_context(nc.psum_tensor("ps_t1", [P, TT, P], F32))
            ps_r = st.enter_context(nc.psum_tensor("ps_r", [P, NT, E], F32))
            ps_n = st.enter_context(nc.psum_tensor("ps_n", [P, 512], F32))
            ps_w = st.enter_context(nc.psum_tensor("ps_w", [P, 512], F32))
            block = st.enter_context(nc.Block())
            NW = 2 * NPIECE
            assert NW == CK * B

            def source(m):
                return (w1p if m < NPIECE else w2p)[m % NPIECE]

            @block.sync
            def _(sp):
                load(sp, 0, 0, True)
                load(sp, 0, 1, True)
                for m in range(NW):
                    if m >= 2:
                        sp.wait_ge(s["abs_summed"], m - 1)
                    sp.dma_start(raw[:, m % 2], source(m)).then_inc(s[f"raw_in{m % 2}"], 16)
                for m in range(NW):
                    if m < 2:
                        sp.wait_ge(s["abs_summed"], NW - 1 + m)
                    else:
                        sp.wait_ge(s["scaled"], m - 1)
                    sp.dma_start(raw[:, m % 2], source(m)).then_inc(s[f"raw_in{m % 2}"], 16)
                    if m + 2 < NW:
                        load(sp, (m + 2) // CK, (m + 2) % CK, False)

            @block.gpsimd
            def _(pool):
                pool.memset(ones_b[:], 1.0).then_inc(s["tables"], 1)
                pool.wait_ge(s["tables"], 1)
                pool.affine_select(out=below[:], in_=ones_b[:], compare_op=ALU.is_gt, fill=0.0, base=0,
                                   pattern=[[1, P]], channel_multiplier=-1).then_inc(s["tables"], 1)
                pool.iota(index16[:], pattern=[[1, E]], base=-E, channel_multiplier=0,
                          allow_small_or_imprecise_dtypes=True).then_inc(s["tables"], 1)
                pool.iota(full[:], pattern=[[P, NT]], base=0, channel_multiplier=0,
                          allow_small_or_imprecise_dtypes=True).then_inc(s["tables"], 1)
                pool.iota(block_no[:], pattern=[[1, NBLK + 1]], base=0, channel_multiplier=0,
                          allow_small_or_imprecise_dtypes=True).then_inc(s["tables"], 1)
                pool.wait_ge(s["slots"], 1)
                for t in range(NT):
                    for k in range(TOPK):
                        pool.indirect_dma_start(
                            xslots, bass.IndirectOffsetOnAxis(ap=slot[:, k, t:t + 1], axis=0),
                            tok[:, t], None).then_inc(s["scattered"], 16)
                prep_pool(pool, 0, 0)
                pool.wait_ge(s["wscale"], 1)
                for m in range(NW):
                    if m + 1 < NW:
                        prep_pool(pool, (m + 1) // CK, (m + 1) % CK)
                    pool.wait_ge(s[f"raw_in{m % 2}"], 16 * (NW // 2 + m // 2 + 1))
                    if m >= 2:
                        pool.wait_ge(s["ternary"], m - 1)
                    layer_w = m // NPIECE
                    pool.tensor_scalar(shifted[:, m % 2], raw[:, m % 2], winv[:, layer_w:layer_w + 1], -1.0,
                                       ALU.mult, ALU.max).then_inc(s["scaled"], 1)
                    pool.wait_ge(s["scaled"], m + 1)
                    pool.tensor_scalar(shifted[:, m % 2], shifted[:, m % 2], 1.0, ROUND,
                                       ALU.min, ALU.add).then_inc(s["rounded"], 1)
                pool.wait_ge(s["scattered"], 16 * NT * TOPK)

            @block.scalar
            def _(act):
                for m in range(NW):
                    act.wait_ge(s[f"raw_in{m % 2}"], 16 * (m // 2 + 1))
                    act.activation(shifted[:, m % 2], raw[:, m % 2], ACT.Abs,
                                   accum_out=abs_sum[:, m:m + 1]).then_inc(s["abs_summed"], 1)
                    if m == 1:
                        act.wait_ge(s["centred"], 1)
                        act.activation(probs[:], probs[:], ACT.Exp).then_inc(s["exped"], 1)
                prep_act(act, 0, 0)
                for u in range(CK * B):
                    b, c = u // CK, u % CK
                    if u + 1 < CK * B:
                        prep_act(act, (u + 1) // CK, (u + 1) % CK)
                    m = u
                    act.wait_ge(s["rounded"], m + 1)
                    wq = (w1q if m < NPIECE else w2q)[:, m % NPIECE]
                    act.activation(wq, shifted[:, m % 2], ACT.Copy, bias=-ROUND).then_inc(s["ternary"], 1)
                    act.wait_ge(s["turned"], u + 1)
                    act.activation(ratio[:, TT * b:TT * b + TT, c * P:(c + 1) * P], ps_t[:], ACT.Copy).then_inc(s["tok_ready"], 1)

            @block.tensor
            def _(pe):
                pe.wait_ge(s["tables"], 2)
                pe.wait_ge(s["mask"], 1)
                pe.matmul(ps_r[:], below[:], mask[:], start=True, stop=False, skip_group_check=True)
                for t in range(NT - 1):
                    last = pe.matmul(ps_r[:, t + 1:NT], ones_b[:], mask[:, t].unsqueeze(1).to_broadcast([P, NT - 1 - t, E]),
                                     start=False, stop=t == NT - 2, skip_group_check=True)
                for t in range(NT):
                    last = pe.matmul(ps_n[:, 0:E], ones_b[:], mask[:, t], start=t == 0, stop=t == NT - 1)
                last.then_inc(s["ranked"], 1)
                pe.wait_ge(s["abs_summed"], NW)
                pe.matmul(ps_w[:, 0:NW], ones[:], abs_sum[:], start=True, stop=True).then_inc(s["abs_total"], 1)
                for u in range(CK * B):
                    pe.wait_ge(s["mixed_ready"], u + 1)
                    if u > 0:
                        pe.wait_ge(s["tok_ready"], u)
                    for t in range(TT):
                        last = pe.transpose(ps_t[:, t], mixed[:, u % 2, t * P:(t + 1) * P], ident[:])
                    last.then_inc(s["turned"], 1)

            @block.vector
            def _(dve):
                done = [0]

                def step(ins):
                    ins.then_inc(s["route"], 1)
                    done[0] += 1
                    dve.wait_ge(s["route"], done[0])

                def over_experts(v):
                    return v.unsqueeze(2).to_broadcast([P, NT, E])

                def over_tiles(v):
                    return v.unsqueeze(1).to_broadcast([P, NT, E])

                step(dve.tensor_reduce(top_[:], probs[:], AX_X, ALU.max))
                dve.tensor_tensor(probs[:], probs[:], over_experts(top_[:]), ALU.subtract).then_inc(s["centred"], 1)
                prep_dve(dve, 0, 0)
                dve.wait_ge(s["exped"], 1)
                step(dve.tensor_reduce(top_[:], probs[:], AX_X, ALU.add))
                step(dve.reciprocal(top_[:], top_[:]))
                step(dve.tensor_tensor(probs[:], probs[:], over_experts(top_[:]), ALU.mult))
                dve.wait_ge(s["tables"], 5)
                for k in range(TOPK):
                    step(dve.tensor_reduce(weight[:, k], probs[:], AX_X, ALU.max))
                    step(dve.tensor_tensor(cand[:], probs[:], over_experts(weight[:, k]), ALU.is_equal))
                    step(dve.tensor_tensor(cand[:], cand[:], over_tiles(index16[:]), ALU.mult))
                    step(dve.tensor_reduce(top_[:], cand[:], AX_X, ALU.min))
                    step(dve.tensor_tensor(chosen[:, k], over_tiles(index16[:]), over_experts(top_[:]), ALU.is_equal))
                    if k == 0:
                        step(dve.scalar_tensor_tensor(out=probs[:], in0=chosen[:, k], scalar=-2.0, in1=probs[:],
                                                      op0=ALU.mult, op1=ALU.add))
                dve.tensor_tensor(mask[:], chosen[:, 0], chosen[:, 1], ALU.add).then_inc(s["mask"], 1)
                dve.wait_ge(s["ranked"], 1)
                step(dve.tensor_copy(count[:], ps_n[:, 0:E]))
                step(dve.tensor_tensor(many[:], count[:].unsqueeze(2).to_broadcast([P, E, NT]),
                                       full[:].unsqueeze(1).to_broadcast([P, E, NT]), ALU.is_gt))
                step(dve.tensor_reduce(blocks[:], many[:], AX_X, ALU.add))
                step(dve.tensor_tensor_scan(ends[:], ones[:, 0:E], blocks[:], 0.0, ALU.mult, ALU.add))
                step(dve.tensor_tensor(first_[:], ends[:], blocks[:], ALU.subtract))
                step(dve.tensor_scalar(first_[:], first_[:], float(P), None, ALU.mult))
                step(dve.tensor_tensor(rank[:], ps_r[:], over_tiles(first_[:]), ALU.add))
                for k in range(TOPK):
                    step(dve.tensor_tensor(cand[:], chosen[:, k], rank[:], ALU.mult))
                    step(dve.tensor_reduce(slotf[:, k], cand[:], AX_X, ALU.add))
                dve.tensor_copy(slot[:], slotf[:]).then_inc(s["slots"], 1)
                step(dve.tensor_tensor(past[:], ends[0:1].unsqueeze(1).to_broadcast([1, NBLK + 1, E]),
                                       block_no[:].unsqueeze(2).to_broadcast([1, NBLK + 1, E]), ALU.is_le))
                step(dve.tensor_reduce(owner[:], past[:], AX_X, ALU.add))
                step(dve.tensor_scalar(block_expert[:], owner[:], float(E - 1), None, ALU.min))
                dve.wait_ge(s["abs_total"], 1)
                step(dve.tensor_reduce(wtotal[:], ps_w[:, 0:NW].rearrange("p (l n) -> p l n", l=2), AX_X, ALU.add))
                step(dve.tensor_scalar(wscale[:], wtotal[:], 1.0 / (C * INNER), 1e-5, ALU.mult, ALU.max))
                dve.reciprocal(winv[:], wscale[:]).then_inc(s["wscale"], 1)
                for u in range(CK * B):
                    if u + 1 < CK * B:
                        prep_dve(dve, (u + 1) // CK, (u + 1) % CK)
                    mix_dve(dve, u // CK, u % CK, u < 2)

        if upto < 3:
            return
        with ExitStack() as st:
            s = Sems(st, "e")
            NU, ND = CK, FT
            (wuh, wul, wdh, wdl), end = place(A, [
                ("wuh", [P, 2, CK, 2 * F], F32R), ("wul", [P, 2, CK, 2 * F], F32R),
                ("wdh", [P, 2, FT, C], F32R), ("wdl", [P, 2, FT, C], F32R)])
            (rawu, rawd, rows_in, hid, gatev), end = place(Ch, [
                ("rawu", [P, CK, 2 * F], F32), ("rawd", [P, FT, C], F32), ("rows_in", [P, 2, C], F32),
                ("hid", [P, FT * P], F32), ("gatev", [P, F], F32)])
            assert end <= D
            (ah, al, bh, bl), _ = place(D, [
                ("ah", [P, 2, CK, P], F32R), ("al", [P, 2, CK, P], F32R),
                ("bh", [P, FT, P], F32R), ("bl", [P, FT, P], F32R)])
            ps_x = st.enter_context(nc.psum_tensor("ps_x", [P, CK, P], F32))
            ps_h = st.enter_context(nc.psum_tensor("ps_h", [P, 4, P], F32))
            ps_1 = st.enter_context(nc.psum_tensor("ps_1", [P, 512], F32))
            ps_3 = st.enter_context(nc.psum_tensor("ps_3", [P, 512], F32))
            ps_o = st.enter_context(nc.psum_tensor("ps_o", [P, 2, C], F32))
            block = st.enter_context(nc.Block())

            def rows(j):
                return min(P, F - j * P)

            def every_block(eng, body):
                for i in range(4):
                    body(i, i % 2, i >= 1, i >= 2)
                with eng.Fori(2, NBLK // 2) as j:
                    body(2 * j, 0, True, True)
                    body(2 * j + 1, 1, True, True)
                if NBLK % 2:
                    body(NBLK - 1, 0, True, True)

            @block.sync
            def _(sp):
                def body(i, p, one_before, two_before):
                    if two_before:
                        sp.wait_ge(s["x_turned"], i - 1)
                    sp.dma_start(rows_in[:, p], xslots[ds(i * P, P)]).then_inc(s[f"rows_in{p}"], 16)
                    e = sp.value_load(block_expert[0:1, ds(i)], min_val=0, max_val=E - 1)
                    for j in range(NU):
                        if one_before:
                            sp.wait_ge(s["wu_lo"], NU * (i - 1) + j + 1)
                        sp.dma_start(rawu[:, j], w13[ds(e), j].rearrange("a p n -> p (a n)")).then_inc(s[f"wu_in{j}"], 16)
                    for j in range(ND):
                        if one_before:
                            sp.wait_ge(s["wd_lo"], ND * (i - 1) + j + 1)
                        sp.dma_start(rawd[0:rows(j), j], w2[ds(e), j * P:j * P + rows(j)].rearrange("a p n -> p (a n)")).then_inc(s[f"wd_in{j}"], 16)

                every_block(sp, body)

            @block.gpsimd
            def _(pool):
                def body(i, p, one_before, two_before):
                    for j in range(ND):
                        r = rows(j)
                        pool.wait_ge(s["wd_hi"], ND * i + j + 1)
                        pool.tensor_tensor(wdl[0:r, p, j], rawd[0:r, j], f32(wdh[0:r, p, j]), ALU.subtract).then_inc(s["wd_lo"], 1)

                every_block(pool, body)

            def split_up_act(act, i, p, two_before):
                for j in range(NU):
                    act.wait_ge(s[f"wu_in{j}"], 16 * (i + 1))
                    if j == 0 and two_before:
                        act.wait_ge(s["up_done"], i - 1)
                    act.activation(wuh[:, p, j], rawu[:, j], ACT.Copy).then_inc(s["wu_hi"], 1)

            def split_down_act(act, i, p, two_before):
                for j in range(ND):
                    r = rows(j)
                    act.wait_ge(s[f"wd_in{j}"], 16 * (i + 1))
                    if j == 0 and two_before:
                        act.wait_ge(s["down_done"], i - 1)
                    act.activation(wdh[0:r, p, j], rawd[0:r, j], ACT.Copy).then_inc(s["wd_hi"], 1)

            @block.scalar
            def _(act):
                def a_hi(i, p, two_before):
                    act.wait_ge(s["x_turned"], i + 1)
                    if two_before:
                        act.wait_ge(s["up_done"], i - 1)
                    act.activation(ah[:, p], ps_x[:], ACT.Copy).then_inc(s["a_hi"], 1)

                def b_hi(i, first):
                    act.wait_ge(s["h_turned"], i + 1)
                    if not first:
                        act.wait_ge(s["down_done"], i)
                    act.activation(bh[:], ps_h[:, 0:FT], ACT.Copy).then_inc(s["b_hi"], 1)

                def evict(i, p, two_before):
                    act.wait_ge(s["down_done"], i + 1)
                    if two_before:
                        act.wait_ge(s[f"y_out{p}"], 8 * (i - p))
                    act.activation(y_sb[:, p], ps_o[:, p], ACT.Copy).then_inc(s["y_evicted"], 1)
                    act.wait_ge(s["y_evicted"], i + 1)
                    act.dma_start(yslots[ds(i * P, P)], y_sb[:, p]).then_inc(s[f"y_out{p}"], 16)

                def body(i, p, one_before, two_before):
                    last = type(i) is int and i == NBLK - 1
                    if one_before:
                        b_hi(i - 1, type(i) is int and i == 1)
                    if not last:
                        a_hi(i + 1, 1 - p, one_before)
                        split_up_act(act, i + 1, 1 - p, one_before)
                    act.wait_ge(s["up_done"], i + 1)
                    act.activation(gatev[:], ps_1[:, 0:F], ACT.Silu).then_inc(s["silu"], 1)
                    if one_before:
                        evict(i - 1, 1 - p, type(i) is not int or i >= 3)
                    if not last:
                        split_down_act(act, i + 1, 1 - p, one_before)

                a_hi(0, 0, False)
                split_up_act(act, 0, 0, False)
                split_down_act(act, 0, 0, False)
                every_block(act, body)
                b_hi(NBLK - 1, False)
                evict(NBLK - 1, (NBLK - 1) % 2, True)
                act.wait_ge(s["y_out0"], 16 * ((NBLK + 1) // 2))
                act.wait_ge(s["y_out1"], 16 * (NBLK // 2))

            @block.vector
            def _(dve):
                def a_lo(i, p):
                    dve.wait_ge(s["a_hi"], i + 1)
                    dve.tensor_tensor(al[:, p], ps_x[:], f32(ah[:, p]), ALU.subtract).then_inc(s["a_lo"], 1)

                def b_lo(i):
                    dve.wait_ge(s["b_hi"], i + 1)
                    dve.tensor_tensor(bl[:], ps_h[:, 0:FT], f32(bh[:]), ALU.subtract).then_inc(s["b_lo"], 1)

                def w_lo(i, p):
                    for j in range(NU):
                        dve.wait_ge(s["wu_hi"], NU * i + j + 1)
                        dve.tensor_tensor(wul[:, p, j], rawu[:, j], f32(wuh[:, p, j]), ALU.subtract).then_inc(s["wu_lo"], 1)

                def body(i, p, one_before, two_before):
                    last = type(i) is int and i == NBLK - 1
                    if one_before:
                        b_lo(i - 1)
                    if not last:
                        a_lo(i + 1, 1 - p)
                        w_lo(i + 1, 1 - p)
                    dve.wait_ge(s["silu"], i + 1)
                    if one_before:
                        dve.wait_ge(s["h_turned"], i)
                    dve.tensor_tensor(hid[:, 0:F], gatev[:], ps_3[:, 0:F], ALU.mult).then_inc(s["hidden"], 1)

                dve.memset(hid[:, F:FT * P], 0.0).then_inc(s["padded"], 1)
                a_lo(0, 0)
                w_lo(0, 0)
                every_block(dve, body)
                b_lo(NBLK - 1)

            @block.tensor
            def _(pe):
                def turn_x(i, p, first):
                    pe.wait_ge(s[f"rows_in{p}"], 8 * (i - p) + 16)
                    if not first:
                        pe.wait_ge(s["a_lo"], i)
                    for c in range(CK):
                        last = pe.transpose(ps_x[:, c], rows_in[:, p, c * P:(c + 1) * P], ident[:])
                    last.then_inc(s["x_turned"], 1)

                def turn_h(i, first):
                    pe.wait_ge(s["hidden"], i + 1)
                    if not first:
                        pe.wait_ge(s["b_lo"], i)
                    for f in range(FT):
                        last = pe.transpose(ps_h[:, f], hid[:, f * P:(f + 1) * P], ident[:])
                    last.then_inc(s["h_turned"], 1)

                def up(i, p):
                    pe.wait_ge(s["a_lo"], i + 1)
                    for c in range(CK):
                        pe.wait_ge(s["wu_lo"], NU * i + c + 1)
                        for w, ps in enumerate((ps_1, ps_3)):
                            hi, lo = wuh[:, p, c, w * F:(w + 1) * F], wul[:, p, c, w * F:(w + 1) * F]
                            for n, (l_, r_) in enumerate(((ah, hi), (ah, lo), (al, hi))):
                                last = pe.matmul(ps[:, 0:F], l_[:, p, c], r_, start=(c == 0 and n == 0),
                                                 stop=(c == CK - 1 and n == 2))
                    last.then_inc(s["up_done"], 1)

                def down(i, p, two_before):
                    pe.wait_ge(s["b_lo"], i + 1)
                    pe.wait_ge(s["wd_lo"], ND * (i + 1))
                    if two_before:
                        pe.wait_ge(s["y_evicted"], i - 1)
                    for f in range(FT):
                        r = rows(f)
                        for n, (l_, r_) in enumerate(((bh, wdh), (bh, wdl), (bl, wdh))):
                            last = pe.matmul(ps_o[:, p], l_[0:r, f], r_[0:r, p, f], start=(f == 0 and n == 0),
                                             stop=(f == FT - 1 and n == 2))
                    last.then_inc(s["down_done"], 1)

                def body(i, p, one_before, two_before):
                    if not (type(i) is int and i == NBLK - 1):
                        turn_x(i + 1, 1 - p, False)
                    if one_before:
                        turn_h(i - 1, type(i) is int and i == 1)
                    up(i, p)
                    if one_before:
                        down(i - 1, 1 - p, type(i) is not int or i >= 3)

                pe.wait_ge(s["padded"], 1)
                turn_x(0, 0, True)
                every_block(pe, body)
                turn_h(NBLK - 1, False)
                down(NBLK - 1, (NBLK - 1) % 2, True)

        if upto < 4:
            return

        def wait(eng, sem, value):
            if type(value) is not int or value > 0:
                eng.wait_ge(sem, value)

        (x1, z1), end = place(A, [("x1", [P, NT, C], F32), ("z1", [P, NT, C], F32)])
        assert end <= Bx
        (alpha, quant1, ssq, amax1, half, minus1, consts), _ = place(Y, [
            ("alpha", [P, NT], F32), ("quant1", [P, NT], F32), ("ssq", [P, NT], F32),
            ("amax1", [P, NT], F32), ("half", [P, NT], F32), ("minus1", [P, NT], F32),
            ("consts", [P, 6], F32)])
        with ExitStack() as st:
            s = Sems(st, "g")
            (ya, yb, ysh, xin, sig), end = place(Ch, [
                ("ya", [P, 2, C], F32), ("yb", [P, 2, C], F32), ("ysh", [P, 2, C], F32),
                ("xin", [P, 2, C], F32), ("sig", [P, 2, C], F32)])
            assert end <= D
            (square, inv, rstd1), _ = place(D, [("square", [P, C], F32), ("inv", [P, NT], F32), ("rstd1", [P, NT], F32)])
            block = st.enter_context(nc.Block())

            @block.sync
            def _(sp):
                for t in range(NT):
                    p = t % 2
                    wait(sp, s["summed"], 3 * (t - 1))
                    sp.dma_start(ysh[:, p], yshared[t]).then_inc(s[f"rows_in{p}"], 16)
                    sp.dma_start(xin[:, p], x[t]).then_inc(s[f"rows_in{p}"], 16)

            @block.gpsimd
            def _(pool):
                pool.memset(half[:], -0.5).then_inc(s["half"], 1)
                for t in range(NT):
                    p = t % 2
                    wait(pool, s["summed"], 3 * (t - 1))
                    for k, dst in enumerate((ya, yb)):
                        pool.indirect_dma_start(dst[:, p], None, yslots, bass.IndirectOffsetOnAxis(
                            ap=slot[:, k, t:t + 1], axis=0)).then_inc(s[f"gathered{p}"], 16)
                pool.wait_ge(s["mean_square"], 1)
                pool.wait_ge(s["half"], 1)
                pool.tensor_tensor(rstd1[:], ssq[:], half[:], ALU.pow).then_inc(s["rstd"], 1)

            @block.scalar
            def _(act):
                for t in range(NT):
                    p = t % 2
                    act.wait_ge(s["summed"], 3 * t + 3)
                    wait(act, s["mixed"], t - 1)
                    act.activation(sig[:, p], x1[:, t], ACT.Sigmoid).then_inc(s["sigmoid"], 1)
                    if t:
                        act.wait_ge(s["mixed"], t)
                        wait(act, s["squared"], t - 1)
                        act.activation(square[:], z1[:, t - 1], ACT.Square, accum_out=ssq[:, t - 1:t]).then_inc(s["squared"], 1)
                act.wait_ge(s["mixed"], NT)
                act.wait_ge(s["squared"], NT - 1)
                act.activation(square[:], z1[:, NT - 1], ACT.Square, accum_out=ssq[:, NT - 1:NT]).then_inc(s["squared"], 1)

            @block.vector
            def _(dve):
                def mix(t):
                    dve.wait_ge(s["sigmoid"], t + 1)
                    dve.tensor_tensor(z1[:, t], sig[:, t % 2], ratio[:, t], ALU.mult).then_inc(s["mixed"], 1)
                    dve.wait_ge(s["mixed"], t + 1)
                    dve.tensor_reduce(amax1[:, t:t + 1], z1[:, t], AX_X, ALU.max, apply_absolute_value=True).then_inc(s["amax"], 1)

                for t in range(NT):
                    p = t % 2
                    dve.wait_ge(s[f"rows_in{p}"], 32 * (t // 2 + 1))
                    dve.tensor_tensor(x1[:, t], xin[:, p], ysh[:, p], ALU.add).then_inc(s["summed"], 1)
                    dve.wait_ge(s[f"gathered{p}"], 32 * (t // 2 + 1))
                    for k, rows_ in enumerate((ya, yb)):
                        dve.wait_ge(s["summed"], 3 * t + 1 + k)
                        dve.scalar_tensor_tensor(out=x1[:, t], in0=rows_[:, p], scalar=weight[:, k, t:t + 1], in1=x1[:, t],
                                                 op0=ALU.mult, op1=ALU.add).then_inc(s["summed"], 1)
                    if t:
                        mix(t - 1)
                mix(NT - 1)
                dve.wait_ge(s["squared"], NT)
                dve.tensor_scalar(ssq[:], ssq[:], 1.0 / C, EPS, ALU.mult, ALU.add).then_inc(s["mean_square"], 1)
                dve.wait_ge(s["rstd"], 1)
                dve.wait_ge(s["amax"], NT)
                dve.tensor_tensor(amax1[:], amax1[:], rstd1[:], ALU.mult).then_inc(s["stat"], 1)
                dve.wait_ge(s["stat"], 1)
                dve.tensor_scalar(amax1[:], amax1[:], 1e-5, None, ALU.max).then_inc(s["stat"], 1)
                dve.wait_ge(s["stat"], 2)
                dve.tensor_scalar(alpha[:], amax1[:], wscale[:, 0:1], 1.0 / 127.0, ALU.mult, ALU.mult).then_inc(s["stat"], 1)
                dve.reciprocal(inv[:], amax1[:]).then_inc(s["stat"], 1)
                dve.wait_ge(s["stat"], 4)
                dve.scalar_tensor_tensor(out=quant1[:], in0=inv[:], scalar=127.0, in1=rstd1[:],
                                         op0=ALU.mult, op1=ALU.mult).then_inc(s["stat"], 1)

        if upto < 5:
            return
        with ExitStack() as st:
            s = Sems(st, "f")
            big, end = place(Bx, [
                ("b1_sb", [P, INNER], F32), ("lng_sb", [P, INNER], F32), ("lnb_sb", [P, INNER], F32),
                ("b2_sb", [P, C], F32), ("pre", [P, 2, INNER], F32), ("hid5", [P, 2, INNER], F32),
                ("moved", [P, INNER], F32), ("junk", [P, INNER], BF16), ("hq", [P, INNER], BF16),
                ("hqT", [P, IK, P], BF16), ("moved1", [P, C], F32), ("xq", [P, C], BF16),
                ("xqT", [P, 2, CK, P], BF16), ("out_sb", [P, 2, C], F32)])
            b1_sb, lng_sb, lnb_sb, b2_sb, pre, hid5, moved, junk, hq, hqT, moved1, xq, xqT, out_sb = big
            assert end <= W, (end, W)
            (gsum, negmu, vsum, rstd, hsum, r2, amax2, m2, inv2, quant2, beta), end = place(W + 32768, [
                (n, [P, 2], F32) for n in ("gsum", "negmu", "vsum", "rstd", "hsum", "r2", "amax2", "m2", "inv2",
                                            "quant2", "beta")])
            ps_q = st.enter_context(nc.psum_tensor("ps_q", [P, CK, P], BF16))
            ps_i = st.enter_context(nc.psum_tensor("ps_i", [P, INNER], F32))
            ps_k = st.enter_context(nc.psum_tensor("ps_k", [P, 2, IK // 2, P], BF16))
            ps_z = st.enter_context(nc.psum_tensor("ps_z", [P, C], F32))
            block = st.enter_context(nc.Block())

            def there(t):
                return type(t) is not int or 0 <= t < NT

            def every_step(eng, step):
                for t in range(-1, 4):
                    step(t, t % 2)
                with eng.Fori(2, NT // 2 - 1) as j:
                    step(2 * j, 0)
                    step(2 * j + 1, 1)
                for t in (NT - 2, NT - 1, NT, NT + 1):
                    step(t, t % 2)

            @block.sync
            def _(sp):
                for dst, src, n in ((b1_sb, b1, INNER), (lng_sb, lng, INNER), (lnb_sb, lnb, INNER), (b2_sb, b2, C)):
                    sp.dma_start(dst[:], src.to_broadcast([P, n])).then_inc(s["rows_in"], 16)

                def step(t, p):
                    if there(t - 1):
                        sp.wait_ge(s["out_ready"], 2 * (t - 1) + 2)
                        sp.dma_start(out[ds(t - 1)].rearrange("a p n -> p (a n)"), out_sb[:, 1 - p]).then_inc(s[f"out{1 - p}"], 16)

                for t in range(1, 3):
                    step(t, t % 2)
                with sp.Fori(1, NT // 2) as j:
                    step(2 * j + 1, 1)
                    step(2 * j + 2, 0)
                for p in range(2):
                    sp.wait_ge(s[f"out{p}"], 16 * NT // 2)

            @block.gpsimd
            def _(pool):
                def tiny(out_, a, b, op, name):
                    pool.tensor_tensor(out_, a, b, op).then_inc(s[name], 1)

                def const(n):
                    return consts[:, n:n + 1]

                def step(t, p):
                    def col(v):
                        return v[:, p:p + 1]

                    steps = 5
                    pool.wait_ge(s["gelu"], t + 1)
                    tiny(col(negmu), col(gsum), const(0), ALU.mult, "negmu")
                    pool.wait_ge(s["var"], t + 1)
                    tiny(col(vsum), col(vsum), const(1), ALU.mult, "tiny")
                    pool.wait_ge(s["tiny"], steps * t + 1)
                    tiny(col(vsum), col(vsum), const(2), ALU.add, "tiny")
                    pool.wait_ge(s["tiny"], steps * t + 2)
                    tiny(col(rstd), col(vsum), half[:, 0:1], ALU.pow, "rstd")
                    pool.wait_ge(s["hsq"], t + 1)
                    tiny(col(hsum), col(hsum), const(1), ALU.mult, "tiny")
                    pool.wait_ge(s["tiny"], steps * t + 3)
                    tiny(col(hsum), col(hsum), const(2), ALU.add, "tiny")
                    pool.wait_ge(s["tiny"], steps * t + 4)
                    tiny(col(r2), col(hsum), half[:, 0:1], ALU.pow, "r2")
                    pool.wait_ge(s["peak"], t + 1)
                    tiny(col(inv2), col(m2), minus1[:, 0:1], ALU.pow, "tiny")
                    tiny(col(beta), col(m2), const(3), ALU.mult, "beta")
                    pool.wait_ge(s["tiny"], steps * t + 5)
                    tiny(col(inv2), col(inv2), const(4), ALU.mult, "inv2")
                    pool.wait_ge(s["inv2"], t + 1)
                    tiny(col(quant2), col(r2), col(inv2), ALU.mult, "quant2")

                pool.memset(minus1[:], -1.0).then_inc(s["consts"], 1)
                for n, value in ((0, -1.0 / INNER), (1, 1.0 / INNER), (2, EPS), (4, 127.0)):
                    pool.memset(const(n), value).then_inc(s["consts"], 1)
                pool.tensor_scalar(const(3), wscale[:, 1:2], 1.0 / 127.0, None, ALU.mult).then_inc(s["consts"], 1)
                pool.wait_ge(s["consts"], 6)
                for t in (0, 1):
                    step(t, t % 2)
                with pool.Fori(1, NT // 2) as j:
                    step(2 * j, 0)
                    step(2 * j + 1, 1)

            @block.scalar
            def _(act):
                def step(t, p):
                    if there(t + 1):
                        wait(act, s["xq"], t + 1)
                        act.activation(moved1[:], z1[:, ds(t + 1)].rearrange("p a n -> p (a n)"), ACT.Copy, bias=ROUND,
                                       scale=quant1[:, ds(t + 1)]).then_inc(s["moved1"], 1)
                    if there(t):
                        act.wait_ge(s["pre"], t + 1)
                        act.activation(hid5[:, p], pre[:, p], ACT.Tanh, scale=0.5).then_inc(s["tanh"], 1)
                        act.wait_ge(s["silu2"], t + 1)
                        act.activation(hid5[:, p], pre[:, p], ACT.Gelu, scale=0.5, accum_out=gsum[:, p:p + 1]).then_inc(s["gelu"], 1)
                    if there(t - 1):
                        act.wait_ge(s["normed"], t)
                        act.wait_ge(s["var"], t)
                        act.activation(junk[:], hid5[:, 1 - p], ACT.Square, accum_out=hsum[:, 1 - p:2 - p]).then_inc(s["hsq"], 1)
                        act.wait_ge(s["quant2"], t)
                        wait(act, s["hq"], t - 1)
                        act.activation(moved[:], hid5[:, 1 - p], ACT.Copy, bias=ROUND, scale=quant2[:, 1 - p:2 - p]).then_inc(s["moved"], 1)
                    if there(t):
                        act.wait_ge(s["negmu"], t + 1)
                        wait(act, s["hsq"], t)
                        act.activation(junk[:], hid5[:, p], ACT.Square, bias=negmu[:, p:p + 1], accum_out=vsum[:, p:p + 1]).then_inc(s["var"], 1)
                    if there(t - 1):
                        act.wait_ge(s["h_turned"], t)
                        wait(act, s["down_done"], t - 1)
                        act.activation(hqT[:], ps_k[:].rearrange("p a k n -> p (a k) n"), ACT.Copy).then_inc(s["hqT"], 1)

                every_step(act, step)

            @block.vector
            def _(dve):
                def step(t, p):
                    if there(t):
                        dve.wait_ge(s["up_done"], t + 1)
                        wait(dve, s["gelu"], t - 1)
                        dve.scalar_tensor_tensor(out=pre[:, p], in0=ps_i[:], scalar=alpha[:, ds(t)], in1=b1_sb[:],
                                                 op0=ALU.mult, op1=ALU.add).then_inc(s["pre"], 1)
                    if there(t - 1):
                        dve.wait_ge(s["var"], t)
                        dve.scalar_tensor_tensor(out=hid5[:, 1 - p], in0=hid5[:, 1 - p], scalar=negmu[:, 1 - p:2 - p], in1=lng_sb[:],
                                                 op0=ALU.add, op1=ALU.mult).then_inc(s["centred"], 1)
                    if there(t):
                        dve.wait_ge(s["tanh"], t + 1)
                        dve.scalar_tensor_tensor(out=pre[:, p], in0=hid5[:, p], scalar=1.0, in1=pre[:, p],
                                                 op0=ALU.add, op1=ALU.mult).then_inc(s["silu2"], 1)
                    if there(t - 1):
                        dve.wait_ge(s["rstd"], t)
                        dve.wait_ge(s["centred"], t)
                        dve.scalar_tensor_tensor(out=hid5[:, 1 - p], in0=hid5[:, 1 - p], scalar=rstd[:, 1 - p:2 - p], in1=lnb_sb[:],
                                                 op0=ALU.mult, op1=ALU.add).then_inc(s["normed"], 1)
                        dve.wait_ge(s["normed"], t)
                        dve.tensor_reduce(amax2[:, 1 - p:2 - p], hid5[:, 1 - p], AX_X, ALU.max, apply_absolute_value=True).then_inc(s["amax"], 1)
                    if there(t + 1):
                        dve.wait_ge(s["moved1"], t + 2)
                        wait(dve, s["x_turned"], t + 1)
                        dve.tensor_scalar(xq[:], moved1[:], ROUND, None, ALU.subtract).then_inc(s["xq"], 1)
                    if there(t - 1):
                        dve.wait_ge(s["r2"], t)
                        dve.wait_ge(s["amax"], t)
                        dve.tensor_scalar(m2[:, 1 - p:2 - p], amax2[:, 1 - p:2 - p], r2[:, 1 - p:2 - p], 1e-5,
                                          ALU.mult, ALU.max).then_inc(s["peak"], 1)
                    if there(t + 1):
                        dve.wait_ge(s["x_turned"], t + 2)
                        wait(dve, s["up_done"], t)
                        dve.tensor_copy(xqT[:, 1 - p], ps_q[:]).then_inc(s["xqT"], 1)
                    if there(t - 1):
                        dve.wait_ge(s["moved"], t)
                        wait(dve, s["h_turned"], t - 1)
                        dve.tensor_scalar(hq[:], moved[:], ROUND, None, ALU.subtract).then_inc(s["hq"], 1)
                    if there(t - 2):
                        dve.wait_ge(s["down_done"], t - 1)
                        wait(dve, s[f"out{p}"], 8 * (t - 2 - p))
                        dve.wait_ge(s["beta"], t - 1)
                        dve.scalar_tensor_tensor(out=out_sb[:, p], in0=ps_z[:], scalar=beta[:, p:p + 1],
                                                 in1=x1[:, ds(t - 2)].rearrange("p a n -> p (a n)"),
                                                 op0=ALU.mult, op1=ALU.add).then_inc(s["out_ready"], 1)
                        dve.wait_ge(s["out_ready"], 2 * (t - 2) + 1)
                        dve.tensor_tensor(out_sb[:, p], out_sb[:, p], b2_sb[:], ALU.add).then_inc(s["out_ready"], 1)

                dve.wait_ge(s["rows_in"], 64)
                every_step(dve, step)

            @block.tensor
            def _(pe):
                def step(t, p):
                    if there(t + 1):
                        pe.wait_ge(s["xq"], t + 2)
                        wait(pe, s["xqT"], t + 1)
                        for c in range(CK):
                            last = pe.transpose(ps_q[:, c], xq[:, c * P:(c + 1) * P], ident_b[:])
                        last.then_inc(s["x_turned"], 1)
                        pe.wait_ge(s["xqT"], t + 2)
                        wait(pe, s["pre"], t + 1)
                        for n in range(INNER // C):
                            for c in range(CK):
                                last = pe.matmul(ps_i[:, n * C:(n + 1) * C], xqT[:, 1 - p, c],
                                                 w1q[:, 2 * c + n // 2, (n % 2) * C:(n % 2 + 1) * C], start=c == 0, stop=c == CK - 1)
                        last.then_inc(s["up_done"], 1)
                    if there(t - 1):
                        pe.wait_ge(s["hq"], t)
                        wait(pe, s["hqT"], t - 1)
                        for k in range(IK):
                            last = pe.transpose(ps_k[:, k // 8, k % 8], hq[:, k * P:(k + 1) * P], ident_b[:])
                        last.then_inc(s["h_turned"], 1)
                        pe.wait_ge(s["hqT"], t)
                        wait(pe, s["out_ready"], 2 * (t - 2) + 1)
                        for k in range(IK):
                            last = pe.matmul(ps_z[:], hqT[:, k], w2q[:, k // 2, (k % 2) * C:(k % 2 + 1) * C],
                                             start=k == 0, stop=k == IK - 1)
                        last.then_inc(s["down_done"], 1)

                every_step(pe, step)


def laid_out(inputs):
    import numpy as np

    def a(name):
        return np.asarray(inputs[name])

    def by_channel(v):
        return v.reshape(B, T, CK, P).transpose(0, 2, 3, 1)

    def column(v):
        return v.reshape(CK, P).T

    def up_weights(w1, w3):
        return np.concatenate([w1, w3], axis=-2).swapaxes(-1, -2).reshape(*w1.shape[:-2], CK, P, -1)

    arrays = {
        "xT": by_channel(a("x")),
        "kT": by_channel(a("fside_BxSxS_0")),
        "x": a("x").reshape(NT, P, C),
        "cond": a("cond_512").T,
        "wu": np.stack([column(a(n)) for n in ("L0_cond_w", "L0_cond_u", "L1_cond_w", "L1_cond_u")], axis=1),
        "gate": a("L0_ffn_gate_w").T.reshape(CK, P, E).transpose(1, 0, 2),
        "sw13": np.stack([a("L0_ffn_sw1").T.reshape(CK, P, SF), a("L0_ffn_sw3").T.reshape(CK, P, SF)]),
        "sw2": a("L0_ffn_sw2").T,
        "w13": up_weights(a("L0_ffn_w1"), a("L0_ffn_w3")),
        "w2": a("L0_ffn_w2").swapaxes(1, 2),
        "w1p": a("L1_ffn_w1").T.reshape(CK, P, 2, PIECE).transpose(0, 2, 1, 3).reshape(NPIECE, P, PIECE),
        "w2p": a("L1_ffn_w2").T.reshape(NPIECE, 2, P, C).transpose(0, 2, 1, 3).reshape(NPIECE, P, PIECE),
        "b1": a("L1_ffn_b1").reshape(1, INNER),
        "lng": a("L1_ffn_ln_g").reshape(1, INNER),
        "lnb": a("L1_ffn_ln_b").reshape(1, INNER),
        "b2": a("L1_ffn_b2").reshape(1, C),
    }
    return {n: np.ascontiguousarray(v) for n, v in arrays.items()}


def kernel(**inputs):
    import concourse.bacc as bacc
    from concourse.bass_utils import run_bass_kernel_spmd

    nc = bacc.Bacc("TRN2", target_bir_lowering=False, num_devices=1)
    arrays = laid_out(inputs)
    args = [nc.dram_tensor(n, v.shape, F32, kind="ExternalInput").ap() for n, v in arrays.items()]
    args.append(nc.dram_tensor("out", (NT, P, C), F32, kind="ExternalOutput").ap())
    args.append(nc.dram_tensor("xslots", (SLOTS, C), F32, kind="Internal").ap())
    args.append(nc.dram_tensor("yslots", (SLOTS, C), F32, kind="Internal").ap())
    args.append(nc.dram_tensor("yshared", (NT, P, C), F32, kind="Internal").ap())
    build(nc, *args)
    got = run_bass_kernel_spmd(nc, [arrays], core_ids=[0])
    return got.results[0]["out"].reshape(B, T, C)
```

```python
from contextlib import ExitStack

import concourse.bass as bass
from concourse import mybir

P = 128
F32 = mybir.dt.float32
F32R = mybir.dt.float32r
BF16 = mybir.dt.bfloat16
I32 = mybir.dt.int32
ALU = mybir.AluOpType
ACT = mybir.ActivationFunctionType
AX_X = mybir.AxisListType.X

B, T, C = 4, 512, 512
CK = C // P
TT = T // P
NT = B * TT
E, TOPK = 16, 2
F = 352
FT = 3
SF = 704
SFT = 6
INNER = 2048
IK = INNER // P
NBLK = (B * T * TOPK + E * (P - 1)) // P
SLOTS = NBLK * P
PIECE = 1024
NPIECE = C * INNER // P // PIECE
ROUND = 12582912.0
EPS = 1e-5
BR = P


def ds(i, n=1):
    return bass.ds(i, n)


def f32(ap):
    return ap.bitcast(F32)


def build(nc, xT, kT, x, cond, wu, gate, sw13, sw2, w13, w2, w1p, w2p, b1, lng, lnb, b2, out,
          xslots, yslots, yshared, upto=5):
    with ExitStack() as ctx:
        base = nc.sbuf_base
        base += -base % 64
        top = [base]

        def region(nbytes):
            at = top[0]
            top[0] += nbytes + (-nbytes % 32)
            return at

        def at(name, shape, dt, offset):
            return nc.alloc_sbuf_tensor_at(name, shape, dt, offset=offset)

        def size(shape, dt):
            n = 2 if dt == BF16 else 4
            for s in shape[1:]:
                n *= s
            return n

        def place(offset, tensors):
            got = []
            for name, shape, dt in tensors:
                got.append(at(name, shape, dt, offset))
                offset += size(shape, dt) + (-size(shape, dt) % 64)
            return got, offset

        def keep(name, shape, dt):
            return at(name, shape, dt, region(size(shape, dt)))

        ident = keep("ident", [P, P], F32)
        ident_b = keep("ident_b", [P, P], BF16)
        ones = keep("ones", [P, P], F32)
        decay = keep("decay", [P, 2, B, CK], F32)
        wu_sb = keep("wu_sb", [P, 4, CK], F32)
        probs = keep("probs", [P, NT, E], F32)
        weight = keep("weight", [P, TOPK, NT], F32)
        slot = keep("slot", [P, TOPK, NT], I32)
        block_expert = keep("block_expert", [1, NBLK + 1], I32)
        fresh = keep("fresh", [1, NBLK + 1], I32)
        turn_before = keep("turn_before", [1, NBLK + 1], I32)
        turn = keep("turn", [1, NBLK + 1], I32)
        unit_out = keep("unit_out", [P, B, CK], F32)
        unit_u = keep("unit_u", [P, B, CK], F32)
        wscale = keep("wscale", [P, 2], F32)

        A = region(2 * 4 * (2 * CK * SF + SFT * C))
        Bx = region(2 * 2 * CK * T * 4)
        Ch = region(2 * SFT * T * 4)
        D = region(NT * C * 4)
        W = region(40960)
        Y = region(2 * C * 4)
        assert top[0] <= nc.sbuf_usable_end, (top[0], nc.sbuf_usable_end)

        ratio = at("ratio", [P, B * CK, T], F32, Bx)
        (w1q, w2q), _ = place(W, [("w1q", [P, NPIECE, PIECE], BF16), ("w2q", [P, NPIECE, PIECE], BF16)])
        y_sb = at("y_sb", [P, 2, C], F32, Y)

        def wait(eng, sem, value):
            if type(value) is not int or value > 0:
                eng.wait_ge(sem, value)

        class Sems:

            def __init__(self, tag):
                self.tag, self.made = tag, {}

            def __getitem__(self, name):
                if name not in self.made:
                    self.made[name] = nc.alloc_semaphore(name=f"{self.tag}_{name}")
                return self.made[name]

        with ExitStack() as st:
            s = Sems("c")
            (cond_sb, ea, tf, dfac, ofac), _ = place(A, [
                ("cond_sb", [P, B], F32), ("ea", [P, 2, CK], F32), ("tf", [P, B], F32), ("dfac", [P, B], F32),
                ("ofac", [P, B], F32)])
            ps_c = st.enter_context(nc.psum_tensor("ps_c", [P, 512], F32))
            block = st.enter_context(nc.Block())

            @block.sync
            def _(sp):
                sp.dma_start(cond_sb[:], cond).then_inc(s["small_in"], 16)
                sp.dma_start(wu_sb[:], wu).then_inc(s["small_in"], 16)

            @block.gpsimd
            def _(pool):
                pool.memset(ones[:], 1.0).then_inc(s["tables"], 1)
                pool.memset(ident[:], 0.0).then_inc(s["tables"], 1)
                pool.wait_ge(s["tables"], 2)
                pool.affine_select(out=ident[:], in_=ident[:], compare_op=ALU.not_equal, fill=1.0, base=0,
                                   pattern=[[-1, P]], channel_multiplier=1).then_inc(s["tables"], 1)
                pool.wait_ge(s["tables"], 3)
                pool.tensor_copy(ident_b[:], ident[:]).then_inc(s["tables"], 1)

            @block.tensor
            def _(pe):
                pe.wait_ge(s["small_in"], 32)
                pe.wait_ge(s["tables"], 1)
                pe.matmul(ps_c[:, 0:B], ones[:], cond_sb[:], start=True, stop=True).then_inc(s["cond_sum"], 1)

            @block.scalar
            def _(act):
                act.wait_ge(s["small_in"], 32)
                wv = wu_sb[:].rearrange("p (l k) c -> p l k c", k=2)[:, :, 0, :]
                act.activation(ea[:], wv, ACT.Exp).then_inc(s["exp_w"], 1)
                act.wait_ge(s["exp_w"], 1)
                act.activation(ea[:], ea[:], ACT.Exp, scale=-1.0).then_inc(s["exp_w"], 1)
                act.wait_ge(s["cond_sum"], 1)
                act.activation(tf[:], ps_c[:, 0:B], ACT.Exp, scale=-1.0).then_inc(s["exp_s"], 1)

            @block.vector
            def _(dve):
                dve.wait_ge(s["exp_s"], 1)
                dve.tensor_scalar(tf[:], tf[:], 1.0, None, ALU.add).then_inc(s["tf"], 1)
                dve.wait_ge(s["tf"], 1)
                dve.reciprocal(tf[:], tf[:]).then_inc(s["tf"], 1)
                dve.wait_ge(s["tf"], 2)
                dve.tensor_scalar(dfac[:], tf[:], 0.5, 0.5, ALU.mult, ALU.add).then_inc(s["tf"], 1)
                dve.tensor_scalar(ofac[:], tf[:], 0.2, 0.8, ALU.mult, ALU.add).then_inc(s["tf"], 1)
                dve.wait_ge(s["tf"], 3)
                dve.wait_ge(s["exp_w"], 2)
                for b in range(B):
                    dve.tensor_scalar(decay[:, :, b, :], ea[:], dfac[:, b:b + 1], None, ALU.mult).then_inc(s["decay"], 1)
                dve.wait_ge(s["tf"], 4)
                dve.tensor_copy(unit_out[:], ofac[:].unsqueeze(2).to_broadcast([P, B, CK])).then_inc(s["decay"], 1)
                dve.tensor_copy(unit_u[:], wu_sb[:, 3].unsqueeze(1).to_broadcast([P, B, CK])).then_inc(s["decay"], 1)

        NUNIT = CK * B

        def wkv(s, bufs):
            k_in, x_in, ev, uv, fw, bw, mixed = bufs

            def load(sp, u):
                b, c, p = u // CK, u % CK, u % 2
                wait(sp, s["uv_ready"], u - 1)
                sp.dma_start(k_in[:, p], kT[b, c]).then_inc(s[f"k_in{p}"], 16)
                wait(sp, s["mixed_ready"], u - 1)
                sp.dma_start(x_in[:, p], xT[b, c]).then_inc(s[f"x_in{p}"], 16)

            def landed(u):
                return 16 * (u // 2 + 1)

            def prep_dve(dve, u):
                p = u % 2
                dve.wait_ge(s[f"k_in{p}"], landed(u))
                dve.tensor_scalar(ev[:, p, 1], k_in[:, p], 30.0, None, ALU.min).then_inc(s["k_clipped"], 1)
                dve.tensor_scalar(uv[:, p, 1], k_in[:, p], wu_sb[:, 1, u % CK:u % CK + 1], 30.0,
                                  ALU.add, ALU.min).then_inc(s["uk_clipped"], 1)

            def prep_act(act, u):
                p = u % 2
                act.wait_ge(s["k_clipped"], u + 1)
                act.activation(ev[:, p, 1], ev[:, p, 1], ACT.Exp).then_inc(s["ek_ready"], 1)
                act.wait_ge(s["uk_clipped"], u + 1)
                act.activation(uv[:, p, 1], uv[:, p, 1], ACT.Exp).then_inc(s["eu_ready"], 1)
                act.wait_ge(s[f"x_in{p}"], landed(u))
                act.activation(x_in[:, p], x_in[:, p], ACT.Exp, scale=-1.0).then_inc(s["ex"], 1)
                act.wait_ge(s["ex"], 2 * u + 1)
                act.activation(x_in[:, p], x_in[:, p], ACT.Copy, bias=1.0).then_inc(s["ex"], 1)

            def prep_pool(pool, u):
                p = u % 2
                pool.wait_ge(s["ek_ready"], u + 1)
                pool.tensor_tensor(ev[:, p, 0], ev[:, p, 1], k_in[:, p], ALU.mult).then_inc(s["ev_ready"], 1)
                pool.wait_ge(s["eu_ready"], u + 1)
                pool.tensor_tensor(uv[:, p, 0], uv[:, p, 1], k_in[:, p], ALU.mult).then_inc(s["uv_ready"], 1)

            def mix_dve(dve, u):
                b, c, p = u // CK, u % CK, u % 2
                d = decay[:, 0, b, c:c + 1]
                steps = 8
                dve.wait_ge(s["ev_ready"], u + 1)
                wait(dve, s["mixed_ready"], u)
                for j in range(2):
                    dve.tensor_tensor_scan(fw[:, j], d.to_broadcast([P, T]), ev[:, p, j], 0.0,
                                           ALU.mult, ALU.add).then_inc(s["step"], 1)
                for j in range(2):
                    dve.tensor_tensor_scan(bw[:, j, ::-1], d.to_broadcast([P, T]), ev[:, p, j, ::-1], 0.0,
                                           ALU.mult, ALU.add).then_inc(s["step"], 1)
                dve.wait_ge(s["step"], steps * u + 4)
                dve.scalar_tensor_tensor(out=fw[:, :, 0:T - 1], in0=bw[:, :, 1:T], scalar=d, in1=fw[:, :, 0:T - 1],
                                         op0=ALU.mult, op1=ALU.add).then_inc(s["step"], 1)
                dve.wait_ge(s["uv_ready"], u + 1)
                dve.wait_ge(s["step"], steps * u + 5)
                dve.tensor_tensor(fw[:], fw[:], uv[:, p], ALU.add).then_inc(s["step"], 1)
                dve.wait_ge(s["step"], steps * u + 6)
                dve.wait_ge(s["ex"], 2 * u + 2)
                dve.scalar_tensor_tensor(out=fw[:, 1], in0=fw[:, 1], scalar=1e-8, in1=x_in[:, p],
                                         op0=ALU.max, op1=ALU.mult).then_inc(s["step"], 1)
                dve.wait_ge(s["step"], steps * u + 7)
                dve.reciprocal(fw[:, 1], fw[:, 1]).then_inc(s["step"], 1)
                dve.wait_ge(s["step"], steps * u + 8)
                wait(dve, s["mixed_read"], u - 1)
                wait(dve, s["x_lo"], u - 1)
                dve.scalar_tensor_tensor(out=mixed[:, p], in0=fw[:, 0], scalar=unit_out[:, b, c:c + 1], in1=fw[:, 1],
                                         op0=ALU.mult, op1=ALU.mult).then_inc(s["mixed_ready"], 1)

            return load, prep_dve, prep_act, prep_pool, mix_dve

        if upto < 1:
            return
        tok = at("tok", [P, NT, C], F32, D)
        with ExitStack() as st:
            s = Sems("m")
            bufs, _ = place(W, [
                ("k_in", [P, 2, T], F32), ("x_in", [P, 2, T], F32),
                ("ev", [P, 2, 2, T], F32),
                ("uv", [P, 2, 2, T], F32),
                ("fw", [P, 2, T], F32),
                ("bw", [P, 2, T], F32),
                ("mixed", [P, 2, T], F32)])
            load, prep_dve, prep_act, prep_pool, mix_dve = wkv(s, bufs)
            mixed = bufs[-1]
            (s13h, s13l, s2h, s2l), _ = place(A, [
                ("s13h", [P, 2, CK, SF], F32R), ("s13l", [P, 2, CK, SF], F32R),
                ("s2h", [P, SFT, C], F32R), ("s2l", [P, SFT, C], F32R)])
            (xh, xl), _ = place(Bx, [("xh", [P, 2, CK, T], F32R), ("xl", [P, 2, CK, T], F32R)])
            (hh, hl), _ = place(Ch, [("hh", [P, SFT, T], F32R), ("hl", [P, SFT, T], F32R)])
            stage = at("stage", [P, 4, SF], F32, D + 8 * C * 4)
            zero = at("zero", [P, C], F32, D + (NT - 1) * C * 4)
            CLEAR = 5
            gate_sb = at("gate_sb", [P, CK, E], F32, top[0])
            hbase = top[0] + CK * E * 4
            hf = at("hf", [P, 2, T], F32, hbase)
            th = at("th", [P, 2, T], F32, Y)
            ps_t = st.enter_context(nc.psum_tensor("ps_t", [P, TT, P], F32))
            ps_l = st.enter_context(nc.psum_tensor("ps_l", [P, 512], F32))
            ps_u = st.enter_context(nc.psum_tensor("ps_u", [P, 2, 2, T], F32))
            ps_y = st.enter_context(nc.psum_tensor("ps_y", [P, 2, C], F32))
            ps_lg = ps_l[:, 0:TT * E].rearrange("p (t e) -> p t e", e=E)
            block = st.enter_context(nc.Block())

            pieces = [(sw13[w, c], s13h[:, w, c], s13l[:, w, c], P, SF) for w in range(2) for c in range(CK)]
            for f in range(SFT):
                rows = min(P, SF - f * P)
                pieces.append((sw2[f * P:f * P + rows], s2h[0:rows, f], s2l[0:rows, f], rows, C))
            cut = [0, 4, 8, 12, len(pieces)]

            def rows_of(f):
                return min(P, SF - f * P)

            def tiles_of(b, c):
                return (2 * c, 2 * c + 1) if b and 2 * c < SFT else ()

            @block.sync
            def _(sp):
                sp.dma_start(gate_sb[:], gate).then_inc(s["gate_in"], 16)
                load(sp, 0)
                load(sp, 1)
                for n, (src, _, _, rows, cols) in enumerate(pieces):
                    if n >= 4:
                        sp.wait_ge(s["piece_lo"], n - 3)
                    sp.dma_start(stage[0:rows, n % 4, 0:cols], src).then_inc(s[f"piece_in{n % 4}"], 16)
                    if n in (3, 7, 11):
                        load(sp, n // 4 + 2)
                sp.wait_ge(s["zero"], 1)
                for b in range(1, B + 1):
                    for u in range(5 if b == 1 else CK * b + 3, min(CK * (b + 1) + 3, NUNIT)):
                        load(sp, u)
                        n = min(CLEAR, NBLK - CLEAR * (u - 5))
                        if n > 0:
                            sp.dma_start(xslots.rearrange("(n p) c -> p n c", p=P)[:, CLEAR * (u - 5):CLEAR * (u - 5) + n],
                                         zero[:].unsqueeze(1).to_broadcast([P, n, C])).then_inc(s["cleared"], 16)
                    for t in range(TT):
                        y = TT * (b - 1) + t
                        sp.wait_ge(s["y_evicted"], y + 1)
                        sp.dma_start(yshared[y], y_sb[:, t % 2]).then_inc(s[f"y_out{t % 2}"], 16)
                for p in range(2):
                    sp.wait_ge(s[f"y_out{p}"], 16 * NT // 2)

            @block.gpsimd
            def _(pool):
                def x_lo(b, c):
                    u = CK * b + c
                    pool.wait_ge(s["x_hi"], u + 1)
                    pool.tensor_tensor(xl[:, b % 2, c], mixed[:, c % 2], f32(xh[:, b % 2, c]), ALU.subtract).then_inc(s["x_lo"], 1)

                def h_lo(b, f):
                    n = SFT * b + f
                    r = rows_of(f)
                    pool.wait_ge(s["h_hi"], n + 1)
                    pool.tensor_tensor(hl[0:r, f], hf[0:r, f % 2], f32(hh[0:r, f]), ALU.subtract).then_inc(s["h_lo"], 1)

                pool.memset(zero[:], 0.0).then_inc(s["zero"], 1)
                prep_pool(pool, 0)
                prep_pool(pool, 1)
                for b in range(B + 1):
                    for c in range(CK):
                        if b < B:
                            x_lo(b, c)
                        if CK * b + c + 2 < NUNIT:
                            prep_pool(pool, CK * b + c + 2)
                        for n in range(cut[c], cut[c + 1]) if b == 0 else ():
                            _, hi, lo, rows, cols = pieces[n]
                            pool.wait_ge(s["piece_hi"], n + 1)
                            pool.tensor_tensor(lo, stage[0:rows, n % 4, 0:cols], f32(hi), ALU.subtract).then_inc(s["piece_lo"], 1)
                        for f in tiles_of(b, c):
                            h_lo(b - 1, f)

            @block.scalar
            def _(act):
                def x_hi(b, c):
                    u = CK * b + c
                    act.wait_ge(s["mixed_ready"], u + 1)
                    wait(act, s["up_done"], SFT * (b - 1))
                    act.activation(xh[:, b % 2, c], mixed[:, c % 2], ACT.Copy).then_inc(s["x_hi"], 1)
                    act.wait_ge(s["turned"], u + 1)
                    if b == B - 1 and c == 0:
                        act.wait_ge(s["cleared"], 16 * -(-NBLK // CLEAR))
                    act.activation(tok[:, TT * b:TT * (b + 1), c * P:(c + 1) * P], ps_t[:], ACT.Copy).then_inc(s["tok_ready"], 1)

                def tanh(b, f):
                    n = SFT * b + f
                    r = rows_of(f)
                    act.wait_ge(s["up_done"], n + 1)
                    if f < 2:
                        wait(act, s[f"y_out{f}"], 16 * 2 * b)
                    act.activation(th[0:r, f % 2], ps_u[0:r, f % 2, 0], ACT.Tanh, scale=0.5).then_inc(s["tanh"], 1)

                def h_hi(b, f):
                    n = SFT * b + f
                    r = rows_of(f)
                    act.wait_ge(s["hidden"], n + 1)
                    wait(act, s["down_done"], TT * b)
                    act.activation(hh[0:r, f], hf[0:r, f % 2], ACT.Copy).then_inc(s["h_hi"], 1)

                def evict(b, t):
                    y = TT * b + t
                    act.wait_ge(s["down_done"], y + 1)
                    wait(act, s[f"y_out{t % 2}"], 16 * (2 * b + t // 2))
                    act.activation(y_sb[:, t % 2], ps_y[:, t % 2], ACT.Copy).then_inc(s["y_evicted"], 1)

                prep_act(act, 0)
                prep_act(act, 1)
                for b in range(B + 1):
                    for c in range(CK):
                        if b < B:
                            x_hi(b, c)
                        if CK * b + c + 2 < NUNIT:
                            prep_act(act, CK * b + c + 2)
                        for n in range(cut[c], cut[c + 1]) if b == 0 else ():
                            _, hi, _, rows, cols = pieces[n]
                            act.wait_ge(s[f"piece_in{n % 4}"], 16 * (n // 4 + 1))
                            act.activation(hi, stage[0:rows, n % 4, 0:cols], ACT.Copy).then_inc(s["piece_hi"], 1)
                        for f in tiles_of(b, c):
                            tanh(b - 1, f)
                        for f in tiles_of(b, c):
                            h_hi(b - 1, f)
                        if b and c == CK - 1:
                            for t in range(TT):
                                evict(b - 1, t)

            @block.vector
            def _(dve):
                def hidden(b, f):
                    n = SFT * b + f
                    r = rows_of(f)
                    dve.wait_ge(s["tanh"], n + 1)
                    dve.scalar_tensor_tensor(out=th[0:r, f % 2], in0=th[0:r, f % 2], scalar=1.0, in1=ps_u[0:r, f % 2, 0],
                                             op0=ALU.add, op1=ALU.mult).then_inc(s["silu"], 1)
                    dve.wait_ge(s["silu"], n + 1)
                    wait(dve, s["h_lo"], n - 1)
                    dve.scalar_tensor_tensor(out=hf[0:r, f % 2], in0=th[0:r, f % 2], scalar=0.5, in1=ps_u[0:r, f % 2, 1],
                                             op0=ALU.mult, op1=ALU.mult).then_inc(s["hidden"], 1)

                prep_dve(dve, 0)
                prep_dve(dve, 1)
                mix_dve(dve, 0)
                for b in range(B + 1):
                    for c in range(CK):
                        u = CK * b + c
                        if u + 2 < NUNIT:
                            prep_dve(dve, u + 2)
                        if u + 1 < NUNIT:
                            mix_dve(dve, u + 1)
                        for f in tiles_of(b, c):
                            hidden(b - 1, f)
                        if c == CK - 1 and b < B:
                            dve.wait_ge(s["mixed_read"], u + 1)
                            dve.tensor_copy(probs[:, TT * b:TT * (b + 1), :], ps_lg).then_inc(s["logits_read"], 1)

            @block.tensor
            def _(pe):
                def turn(b, c):
                    u = CK * b + c
                    m = mixed[:, c % 2]
                    pe.wait_ge(s["mixed_ready"], u + 1)
                    wait(pe, s["tok_ready"], u)
                    for t in range(TT):
                        last = pe.transpose(ps_t[:, t], m[:, t * P:(t + 1) * P], ident[:])
                    last.then_inc(s["turned"], 1)
                    if c == 0:
                        wait(pe, s["logits_read"], b)
                    for t in range(TT):
                        last = pe.matmul(ps_lg[:, t], m[:, t * P:(t + 1) * P], gate_sb[:, c], start=(c == 0 and t == 0),
                                         stop=(c == CK - 1 and t == TT - 1), skip_group_check=True)
                    last.then_inc(s["mixed_read"], 1)

                def up(b, f):
                    n = SFT * b + f
                    r = rows_of(f)
                    wait(pe, s["hidden"], n - 1)
                    if f == 0:
                        pe.wait_ge(s["x_lo"], CK * (b + 1))
                    for w in range(2):
                        for c in range(CK):
                            hi, lo = s13h[:, w, c, f * P:f * P + r], s13l[:, w, c, f * P:f * P + r]
                            for i, (l_, r_) in enumerate(((hi, xh), (hi, xl), (lo, xh))):
                                last = pe.matmul(ps_u[0:r, f % 2, w], l_, r_[:, b % 2, c], start=(c == 0 and i == 0),
                                                 stop=(c == CK - 1 and i == 2))
                    last.then_inc(s["up_done"], 1)

                def down(b, t):
                    y = TT * b + t
                    wait(pe, s["y_evicted"], y - 1)
                    if t == 0:
                        pe.wait_ge(s["h_lo"], SFT * (b + 1))
                    for f in range(SFT):
                        r = rows_of(f)
                        hi, lo = hh[0:r, f, t * P:(t + 1) * P], hl[0:r, f, t * P:(t + 1) * P]
                        for i, (l_, r_) in enumerate(((hi, s2h[0:r, f]), (hi, s2l[0:r, f]), (lo, s2h[0:r, f]))):
                            last = pe.matmul(ps_y[:, t % 2], l_, r_, start=(f == 0 and i == 0),
                                             stop=(f == SFT - 1 and i == 2))
                    last.then_inc(s["down_done"], 1)

                pe.wait_ge(s["gate_in"], 16)
                for b in range(B + 1):
                    for c in range(CK):
                        if b < B:
                            turn(b, c)
                        if b == 1 and c == 0:
                            pe.wait_ge(s["piece_lo"], len(pieces))
                        for f in tiles_of(b, c):
                            up(b - 1, f)
                        if b and c == CK - 1:
                            for t in range(TT):
                                down(b - 1, t)

        if upto < 2:
            return
        with ExitStack() as st:
            s = Sems("r")
            NW = 2 * NPIECE
            (raw,), _ = place(A, [("raw", [P, NW, PIECE], F32)])
            tables, end = place(Ch, [
                ("below", [P, P], BF16), ("ones_b", [P, P], BF16), ("mask", [P, NT, E], BF16),
                ("index16", [P, E], F32), ("full", [P, NT], F32), ("block_no", [1, NBLK + 1], F32),
                ("top", [P, NT], F32), ("cand", [P, NT, E], F32), ("chosen", [P, TOPK, NT, E], F32),
                ("rank", [P, NT, E], F32), ("many", [P, E, NT], F32), ("blocks", [P, E], F32),
                ("ends", [P, E], F32), ("first", [P, E], F32), ("slotf", [P, TOPK, NT], F32),
                ("count", [P, E], F32), ("past", [1, NBLK + 1, E], F32), ("owner", [1, NBLK + 1], F32),
                ("change", [1, NBLK + 1], F32), ("changes", [1, NBLK + 1], F32),
                ("abs_sum", [P, NW], F32), ("wtotal", [P, 2], F32), ("winv", [P, 2], F32),
                ("junk2", [P, PIECE], BF16)])
            assert end <= D
            (below, ones_b, mask, index16, full, block_no, top_, cand, chosen, rank, many, blocks,
             ends, first_, slotf, count, past, owner, change, changes, abs_sum, wtotal, winv, junk2) = tables
            ps_r = st.enter_context(nc.psum_tensor("ps_r", [P, NT, E], F32))
            ps_n = st.enter_context(nc.psum_tensor("ps_n", [P, 512], F32))
            ps_w = st.enter_context(nc.psum_tensor("ps_w", [P, 512], F32))
            block = st.enter_context(nc.Block())

            @block.sync
            def _(sp):
                for m in range(0, NW, 4):
                    w = (w1p if m < NPIECE else w2p)[m % NPIECE:m % NPIECE + 4]
                    sp.dma_start(raw[:, m:m + 4], w.rearrange("n p c -> p n c")).then_inc(s[f"raw_in{m // 4}"], 16)

            @block.gpsimd
            def _(pool):
                pool.memset(ones_b[:], 1.0).then_inc(s["tables"], 1)
                pool.wait_ge(s["tables"], 1)
                pool.affine_select(out=below[:], in_=ones_b[:], compare_op=ALU.is_gt, fill=0.0, base=0,
                                   pattern=[[1, P]], channel_multiplier=-1).then_inc(s["tables"], 1)
                pool.iota(index16[:], pattern=[[1, E]], base=-E, channel_multiplier=0,
                          allow_small_or_imprecise_dtypes=True).then_inc(s["tables"], 1)
                pool.iota(full[:], pattern=[[P, NT]], base=0, channel_multiplier=0,
                          allow_small_or_imprecise_dtypes=True).then_inc(s["tables"], 1)
                pool.iota(block_no[:], pattern=[[1, NBLK + 1]], base=0, channel_multiplier=0,
                          allow_small_or_imprecise_dtypes=True).then_inc(s["tables"], 1)
                pool.wait_ge(s["slots"], 1)
                for t in range(NT):
                    for k in range(TOPK):
                        pool.indirect_dma_start(
                            xslots, bass.IndirectOffsetOnAxis(ap=slot[:, k, t:t + 1], axis=0),
                            tok[:, t], None).then_inc(s["scattered"], 16)
                pool.wait_ge(s["scattered"], 16 * NT * TOPK)

            @block.scalar
            def _(act):
                act.wait_ge(s["centred"], 1)
                act.activation(probs[:], probs[:], ACT.Exp).then_inc(s["exped"], 1)
                for m in range(NW):
                    act.wait_ge(s[f"raw_in{m // 4}"], 16)
                    if m:
                        act.wait_ge(s["abs_summed"], m)
                    act.activation(junk2[:], raw[:, m], ACT.Abs,
                                   accum_out=abs_sum[:, m:m + 1]).then_inc(s["abs_summed"], 1)
                for m in range(NW):
                    act.wait_ge(s["rounded"], m + 1)
                    wq = (w1q if m < NPIECE else w2q)[:, m % NPIECE]
                    act.activation(wq, raw[:, m], ACT.Copy, bias=-ROUND).then_inc(s["ternary"], 1)

            @block.tensor
            def _(pe):
                pe.wait_ge(s["tables"], 2)
                pe.wait_ge(s["mask"], 1)
                pe.matmul(ps_r[:], below[:], mask[:], start=True, stop=False, skip_group_check=True)
                for t in range(NT - 1):
                    last = pe.matmul(ps_r[:, t + 1:NT], ones_b[:], mask[:, t].unsqueeze(1).to_broadcast([P, NT - 1 - t, E]),
                                     start=False, stop=t == NT - 2, skip_group_check=True)
                for t in range(NT):
                    last = pe.matmul(ps_n[:, 0:E], ones_b[:], mask[:, t], start=t == 0, stop=t == NT - 1)
                last.then_inc(s["ranked"], 1)
                pe.wait_ge(s["abs_summed"], NW)
                pe.matmul(ps_w[:, 0:NW], ones[:], abs_sum[:], start=True, stop=True).then_inc(s["abs_total"], 1)

            @block.vector
            def _(dve):
                done = [0]

                def step(ins):
                    ins.then_inc(s["route"], 1)
                    done[0] += 1
                    dve.wait_ge(s["route"], done[0])

                def over_experts(v):
                    return v.unsqueeze(2).to_broadcast([P, NT, E])

                def over_tiles(v):
                    return v.unsqueeze(1).to_broadcast([P, NT, E])

                step(dve.tensor_reduce(top_[:], probs[:], AX_X, ALU.max))
                dve.tensor_tensor(probs[:], probs[:], over_experts(top_[:]), ALU.subtract).then_inc(s["centred"], 1)
                dve.wait_ge(s["exped"], 1)
                step(dve.tensor_reduce(top_[:], probs[:], AX_X, ALU.add))
                step(dve.reciprocal(top_[:], top_[:]))
                step(dve.tensor_tensor(probs[:], probs[:], over_experts(top_[:]), ALU.mult))
                dve.wait_ge(s["tables"], 5)
                for k in range(TOPK):
                    step(dve.tensor_reduce(weight[:, k], probs[:], AX_X, ALU.max))
                    step(dve.tensor_tensor(cand[:], probs[:], over_experts(weight[:, k]), ALU.is_equal))
                    step(dve.tensor_tensor(cand[:], cand[:], over_tiles(index16[:]), ALU.mult))
                    step(dve.tensor_reduce(top_[:], cand[:], AX_X, ALU.min))
                    step(dve.tensor_tensor(chosen[:, k], over_tiles(index16[:]), over_experts(top_[:]), ALU.is_equal))
                    if k == 0:
                        step(dve.scalar_tensor_tensor(out=probs[:], in0=chosen[:, k], scalar=-2.0, in1=probs[:],
                                                      op0=ALU.mult, op1=ALU.add))
                dve.tensor_tensor(mask[:], chosen[:, 0], chosen[:, 1], ALU.add).then_inc(s["mask"], 1)
                dve.wait_ge(s["ranked"], 1)
                step(dve.tensor_copy(count[:], ps_n[:, 0:E]))
                step(dve.tensor_tensor(many[:], count[:].unsqueeze(2).to_broadcast([P, E, NT]),
                                       full[:].unsqueeze(1).to_broadcast([P, E, NT]), ALU.is_gt))
                step(dve.tensor_reduce(blocks[:], many[:], AX_X, ALU.add))
                step(dve.tensor_tensor_scan(ends[:], ones[:, 0:E], blocks[:], 0.0, ALU.mult, ALU.add))
                step(dve.tensor_tensor(first_[:], ends[:], blocks[:], ALU.subtract))
                step(dve.tensor_scalar(first_[:], first_[:], float(P), None, ALU.mult))
                step(dve.tensor_tensor(rank[:], ps_r[:], over_tiles(first_[:]), ALU.add))
                for k in range(TOPK):
                    step(dve.tensor_tensor(cand[:], chosen[:, k], rank[:], ALU.mult))
                    step(dve.tensor_reduce(slotf[:, k], cand[:], AX_X, ALU.add))
                dve.tensor_copy(slot[:], slotf[:]).then_inc(s["slots"], 1)
                step(dve.tensor_tensor(past[:], ends[0:1].unsqueeze(1).to_broadcast([1, NBLK + 1, E]),
                                       block_no[:].unsqueeze(2).to_broadcast([1, NBLK + 1, E]), ALU.is_le))
                step(dve.tensor_reduce(owner[:], past[:], AX_X, ALU.add))
                step(dve.tensor_scalar(owner[:], owner[:], float(E - 1), None, ALU.min))
                step(dve.tensor_copy(block_expert[:], owner[:]))
                dve.memset(change[:, 0:1], 0.0).then_inc(s["change0"], 1)
                step(dve.tensor_tensor(change[:, 1:], owner[:, 1:], owner[:, 0:NBLK], ALU.is_gt))
                dve.wait_ge(s["change0"], 1)
                step(dve.tensor_tensor_scan(changes[:], ones[0:1, 0:NBLK + 1], change[:], 0.0, ALU.mult, ALU.add))
                step(dve.tensor_copy(fresh[:], change[:]))
                step(dve.tensor_copy(turn[:], changes[:]))
                step(dve.tensor_scalar(turn_before[:], changes[:], -1.0, 0.0, ALU.add, ALU.max))
                dve.wait_ge(s["abs_total"], 1)
                step(dve.tensor_reduce(wtotal[:], ps_w[:, 0:NW].rearrange("p (l n) -> p l n", l=2), AX_X, ALU.add))
                step(dve.tensor_scalar(wscale[:], wtotal[:], 1.0 / (C * INNER), 1e-5, ALU.mult, ALU.max))
                step(dve.reciprocal(winv[:], wscale[:]))
                for m in range(NW):
                    l = m // NPIECE
                    dve.tensor_scalar(raw[:, m], raw[:, m], winv[:, l:l + 1], -1.0, ALU.mult, ALU.max).then_inc(s["scaled"], 1)
                    if m:
                        dve.wait_ge(s["scaled"], m)
                        dve.tensor_scalar(raw[:, m - 1], raw[:, m - 1], 1.0, ROUND, ALU.min, ALU.add).then_inc(s["rounded"], 1)
                dve.wait_ge(s["scaled"], NW)
                dve.tensor_scalar(raw[:, NW - 1], raw[:, NW - 1], 1.0, ROUND, ALU.min, ALU.add).then_inc(s["rounded"], 1)

        if upto < 3:
            return
        with ExitStack() as st:
            s = Sems("e")
            NU, ND = CK, FT
            NV = 3
            NG = NU - NV + ND
            PER = 3
            (wuh, wul, wdh, wdl), end = place(A, [
                ("wuh", [P, 2, CK, 2 * F], F32R), ("wul", [P, 2, CK, 2 * F], F32R),
                ("wdh", [P, 2, FT, C], F32R), ("wdl", [P, 2, FT, C], F32R)])
            assert end <= Bx
            (rawu, rawd, rows_in, hid, gatev, ah, al, bh, bl, ev, uv, fw, bw), end = place(Ch, [
                ("rawu", [P, CK, 2 * F], F32), ("rawd", [P, FT, C], F32), ("rows_in", [P, 2, C], F32),
                ("hid", [P, FT * P], F32), ("gatev", [P, F], F32),
                ("ah", [P, 2, CK, P], F32R), ("al", [P, 2, CK, P], F32R),
                ("bh", [P, FT, P], F32R), ("bl", [P, FT, P], F32R),
                ("ev1", [P, 2, T], F32),
                ("uv1", [P, 2, T], F32),
                ("fw1", [P, 2, T], F32), ("bw1", [P, 2, T], F32)])
            assert end <= W, (end, W)
            (k_in,), end = place(W + 32768, [("k_in1", [P, 2, T], F32)])
            assert end <= Y
            ps_x = st.enter_context(nc.psum_tensor("ps_x", [P, CK, P], F32))
            ps_h = st.enter_context(nc.psum_tensor("ps_h", [P, 4, P], F32))
            ps_1 = st.enter_context(nc.psum_tensor("ps_1", [P, 512], F32))
            ps_3 = st.enter_context(nc.psum_tensor("ps_3", [P, 512], F32))
            ps_o = st.enter_context(nc.psum_tensor("ps_o", [P, 2, C], F32))
            block = st.enter_context(nc.Block())
            decay1 = decay[:, 1].rearrange("p b c -> p (b c)")
            out1 = unit_out[:].rearrange("p b c -> p (b c)")
            u1 = unit_u[:].rearrange("p b c -> p (b c)")
            k_units = kT.rearrange("b c p t -> (b c) p t")
            assert PER * NUNIT >= NBLK > PER * (NUNIT - 1)

            def rows(j):
                return min(P, F - j * P)

            def every_block(eng, body):
                R = 2 * PER
                for i in range(R):
                    body(i, i % 2, i // PER, i % PER)
                with eng.Fori(1, NBLK // R) as j:
                    for i in range(R):
                        body(R * j + i, i % 2, 2 * j + i // PER, i % PER)
                for i in range(R * (NBLK // R), NBLK):
                    body(i, i % 2, i // PER, i % PER)

            def is_first(i):
                return type(i) is int and i == 0

            def is_last(i):
                return type(i) is int and i == NBLK - 1

            def lo_count(n, j):
                return (s["vec_lo"], NV * n + j + 1) if j < NV else (s["pool_lo"], NG * n + j - NV + 1)

            def buffer(t, n, j):
                return t[:, ds(n % 2), j].rearrange("p a n -> p (a n)")

            def when_fresh(eng, i, turns, load_):
                changed = eng.value_load(fresh[0:1, ds(i)], min_val=0, max_val=1)
                with eng.If(changed > 0):
                    load_(i, eng.value_load(turns[0:1, ds(i)], min_val=0, max_val=E - 1))

            @block.sync
            def _(sp):
                def weights(i, before):
                    e = sp.value_load(block_expert[0:1, ds(i)], min_val=0, max_val=E - 1)
                    for j in range(NU):
                        if not is_first(i):
                            sp.wait_ge(*lo_count(before, j))
                        sp.dma_start(rawu[:, j], w13[ds(e), j].rearrange("a p n -> p (a n)")).then_inc(s[f"wu_in{j}"], 16)
                    for j in range(ND):
                        if not is_first(i):
                            sp.wait_ge(s["pool_lo"], NG * before + NU - NV + j + 1)
                        sp.dma_start(rawd[0:rows(j), j], w2[ds(e), j * P:j * P + rows(j)].rearrange("a p n -> p (a n)")).then_inc(s[f"wd_in{j}"], 16)

                weights(0, 0)
                with sp.Fori(1, NBLK) as i:
                    when_fresh(sp, i, turn_before, weights)

            @block.gpsimd
            def _(pool):
                def split(i, n):
                    for j in range(NV, NU):
                        pool.wait_ge(s["wu_hi"], NU * n + j + 1)
                        pool.tensor_tensor(buffer(wul, n, j), rawu[:, j], f32(buffer(wuh, n, j)), ALU.subtract).then_inc(s["pool_lo"], 1)
                    for j in range(ND):
                        r = rows(j)
                        pool.wait_ge(s["wd_hi"], ND * n + j + 1)
                        pool.tensor_tensor(buffer(wdl, n, j)[0:r], rawd[0:r, j], f32(buffer(wdh, n, j)[0:r]), ALU.subtract).then_inc(s["pool_lo"], 1)

                split(0, 0)
                with pool.Fori(1, NBLK) as i:
                    when_fresh(pool, i, turn, split)

            @block.scalar
            def _(act):
                def rows_load(i, p, first):
                    if not first:
                        act.wait_ge(s["x_turned"], i - 1)
                    act.dma_start(rows_in[:, p], xslots[ds(i * P, P)]).then_inc(s[f"rows_in{p}"], 16)

                def k_load(u, p, first):
                    if not first:
                        act.wait_ge(s["uv_ready"], u - 1)
                    act.dma_start(k_in[:, p], k_units[ds(u)].rearrange("a p t -> p (a t)")).then_inc(s[f"k_in{p}"], 16)

                def exps(u):
                    act.wait_ge(s["clipped"], 2 * u + 1)
                    act.activation(ev[:, 1], ev[:, 1], ACT.Exp).then_inc(s["exped"], 1)
                    act.wait_ge(s["clipped"], 2 * u + 2)
                    act.activation(uv[:, 1], uv[:, 1], ACT.Exp).then_inc(s["exped"], 1)

                def a_hi(i, p, two_before):
                    act.wait_ge(s["x_turned"], i + 1)
                    if two_before:
                        act.wait_ge(s["up_done"], i)
                    act.activation(ah[:, p], ps_x[:], ACT.Copy).then_inc(s["a_hi"], 1)

                def b_hi(i):
                    act.wait_ge(s["h_turned"], i + 1)
                    if not is_first(i):
                        act.wait_ge(s["down_done"], i + 1)
                    act.activation(bh[:], ps_h[:, 0:FT], ACT.Copy).then_inc(s["b_hi"], 1)

                def evict(i, p):
                    act.wait_ge(s["down_done"], i + 2)
                    if type(i) is not int or i >= 2:
                        act.wait_ge(s[f"y_out{p}"], 8 * (i - p))
                    act.activation(y_sb[:, p], ps_o[:, p], ACT.Copy).then_inc(s["y_evicted"], 1)
                    act.wait_ge(s["y_evicted"], i + 1)
                    act.dma_start(yslots[ds(i * P, P)], y_sb[:, p]).then_inc(s[f"y_out{p}"], 16)

                def split_up(i, n):
                    for j in range(NU):
                        act.wait_ge(s[f"wu_in{j}"], 16 * (n + 1))
                        if j == 0 and not is_first(i):
                            act.wait_ge(s["up_done"], i)
                        act.activation(buffer(wuh, n, j), rawu[:, j], ACT.Copy).then_inc(s["wu_hi"], 1)

                def split_down(i, n):
                    for j in range(ND):
                        r = rows(j)
                        act.wait_ge(s[f"wd_in{j}"], 16 * (n + 1))
                        if j == 0 and not is_first(i):
                            act.wait_ge(s["down_done"], i)
                        act.activation(buffer(wdh, n, j)[0:r], rawd[0:r, j], ACT.Copy).then_inc(s["wd_hi"], 1)

                def body(i, p, u, part):
                    if not (type(i) is int and i >= NBLK - 2):
                        rows_load(i + 2, p, False)
                    if not is_last(i):
                        changed = act.value_load(fresh[0:1, ds(i + 1)], min_val=0, max_val=1)
                        n = act.value_load(turn[0:1, ds(i + 1)], min_val=0, max_val=E - 1)
                    if not is_first(i):
                        b_hi(i - 1)
                    if not is_last(i):
                        a_hi(i + 1, 1 - p, not is_first(i))
                        with act.If(changed > 0):
                            split_up(i + 1, n)
                    if part == 0 and type(u) is not int or type(u) is int and part == 0 and 1 <= u < NUNIT - 1:
                        k_load(u + 1, (part_parity(p, part) + 1) % 2, False)
                    act.wait_ge(s["up_done"], i + 2)
                    act.activation(gatev[:], ps_1[:, 0:F], ACT.Silu).then_inc(s["silu"], 1)
                    if not is_first(i):
                        evict(i - 1, 1 - p)
                    if not is_last(i):
                        with act.If(changed > 0):
                            split_down(i + 1, n)
                    if part == PER - 1:
                        exps(u + 1)

                def part_parity(p, part):
                    return (p - part) % 2

                for p in range(2):
                    rows_load(p, p, True)
                    k_load(p, p, True)
                split_up(0, 0)
                split_down(0, 0)
                a_hi(0, 0, False)
                exps(0)
                every_block(act, body)
                b_hi(NBLK - 1)
                evict(NBLK - 1, (NBLK - 1) % 2)
                act.wait_ge(s["y_out0"], 16 * ((NBLK + 1) // 2))
                act.wait_ge(s["y_out1"], 16 * (NBLK // 2))

            @block.vector
            def _(dve):
                def a_lo(i, p):
                    dve.wait_ge(s["a_hi"], i + 1)
                    dve.tensor_tensor(al[:, p], ps_x[:], f32(ah[:, p]), ALU.subtract).then_inc(s["a_lo"], 1)

                def b_lo(i):
                    dve.wait_ge(s["b_hi"], i + 1)
                    dve.tensor_tensor(bl[:], ps_h[:, 0:FT], f32(bh[:]), ALU.subtract).then_inc(s["b_lo"], 1)

                def hidden(i):
                    dve.wait_ge(s["silu"], i + 1)
                    if not is_first(i):
                        dve.wait_ge(s["h_turned"], i)
                    dve.tensor_tensor(hid[:, 0:F], gatev[:], ps_3[:, 0:F], ALU.mult).then_inc(s["hidden"], 1)

                def w_lo(i, n):
                    for j in range(NV):
                        dve.wait_ge(s["wu_hi"], NU * n + j + 1)
                        dve.tensor_tensor(buffer(wul, n, j), rawu[:, j], f32(buffer(wuh, n, j)), ALU.subtract).then_inc(s["vec_lo"], 1)

                STEPS = 8

                def clip(u, p):
                    if not is_first(u):
                        dve.wait_ge(s["step"], STEPS * (u - 1) + 6)
                    dve.wait_ge(s[f"k_in{p}"], 8 * (u - p) + 16)
                    dve.tensor_scalar(ev[:, 1], k_in[:, p], 30.0, None, ALU.min).then_inc(s["clipped"], 1)
                    dve.tensor_scalar(uv[:, 1], k_in[:, p], u1[:, ds(u)], 30.0, ALU.add, ALU.min).then_inc(s["clipped"], 1)

                def scan(u, to, j, back):
                    d = decay1[:, ds(u)].to_broadcast([P, T])
                    o, i_ = (to[:, j, ::-1], ev[:, j, ::-1]) if back else (to[:, j], ev[:, j])
                    dve.tensor_tensor_scan(o, d, i_, 0.0, ALU.mult, ALU.add).then_inc(s["step"], 1)

                def early(u, p, part):
                    if part == 0:
                        dve.wait_ge(s["exped"], 2 * u + 1)
                        dve.tensor_tensor(ev[:, 0], ev[:, 1], k_in[:, p], ALU.mult).then_inc(s["ev_ready"], 1)
                        scan(u, fw, 1, False)
                        dve.wait_ge(s["ev_ready"], u + 1)
                        scan(u, fw, 0, False)
                    if part == 1:
                        scan(u, bw, 0, True)
                        dve.wait_ge(s["step"], STEPS * u + 4)
                        dve.scalar_tensor_tensor(out=fw[:, :, 0:T - 1], in0=bw[:, :, 1:T], scalar=decay1[:, ds(u)],
                                                 in1=fw[:, :, 0:T - 1], op0=ALU.mult, op1=ALU.add).then_inc(s["step"], 1)
                    if part == 2 and (type(u) is not int or u < NUNIT - 1):
                        clip(u + 1, 1 - p)

                def late(u, p, part):
                    if part == 0:
                        scan(u, bw, 1, True)
                    if part == 1:
                        dve.wait_ge(s["exped"], 2 * u + 2)
                        dve.tensor_tensor(uv[:, 0], uv[:, 1], k_in[:, p], ALU.mult).then_inc(s["uv_ready"], 1)
                        dve.wait_ge(s["uv_ready"], u + 1)
                        dve.wait_ge(s["step"], STEPS * u + 5)
                        dve.tensor_tensor(fw[:], fw[:], uv[:], ALU.add).then_inc(s["step"], 1)
                        dve.wait_ge(s["step"], STEPS * u + 6)
                        dve.tensor_scalar(fw[:, 1], fw[:, 1], 1e-8, None, ALU.max).then_inc(s["step"], 1)
                    if part == 2:
                        dve.wait_ge(s["step"], STEPS * u + 7)
                        dve.reciprocal(fw[:, 1], fw[:, 1]).then_inc(s["step"], 1)
                        dve.wait_ge(s["step"], STEPS * u + 8)
                        dve.scalar_tensor_tensor(out=ratio[:, ds(u)].rearrange("p a t -> p (a t)"), in0=fw[:, 0],
                                                 scalar=out1[:, ds(u)], in1=fw[:, 1],
                                                 op0=ALU.mult, op1=ALU.mult).then_inc(s["ratio"], 1)

                def body(i, p, u, part):
                    pu = (p - part) % 2
                    if not is_last(i):
                        changed = dve.value_load(fresh[0:1, ds(i + 1)], min_val=0, max_val=1)
                        n = dve.value_load(turn[0:1, ds(i + 1)], min_val=0, max_val=E - 1)
                    if not is_first(i):
                        b_lo(i - 1)
                    if not is_last(i):
                        a_lo(i + 1, 1 - p)
                        with dve.If(changed > 0):
                            w_lo(i + 1, n)
                    if part == 0 and not is_first(u):
                        dve.wait_ge(s["ratio"], u)
                    early(u, pu, part)
                    hidden(i)
                    late(u, pu, part)

                dve.memset(hid[:, F:FT * P], 0.0).then_inc(s["up_done"], 1)
                dve.memset(hid[:, 0:F], 0.0).then_inc(s["down_done"], 1)
                w_lo(0, 0)
                a_lo(0, 0)
                clip(0, 0)
                every_block(dve, body)
                b_lo(NBLK - 1)
                early(NUNIT - 1, (NUNIT - 1) % 2, PER - 1)
                late(NUNIT - 1, (NUNIT - 1) % 2, PER - 1)

            @block.tensor
            def _(pe):
                def turn_x(i, p):
                    pe.wait_ge(s[f"rows_in{p}"], 8 * (i - p) + 16)
                    if not is_first(i):
                        pe.wait_ge(s["a_lo"], i)
                    for c in range(CK):
                        last = pe.transpose(ps_x[:, c], rows_in[:, p, c * P:(c + 1) * P], ident[:])
                    last.then_inc(s["x_turned"], 1)

                def turn_h(i):
                    pe.wait_ge(s["hidden"], i + 1)
                    if not is_first(i):
                        pe.wait_ge(s["b_lo"], i)
                    for f in range(FT):
                        last = pe.transpose(ps_h[:, f], hid[:, f * P:(f + 1) * P], ident[:])
                    last.then_inc(s["h_turned"], 1)

                def up(i, p, n):
                    pe.wait_ge(s["a_lo"], i + 1)
                    for c in range(CK):
                        pe.wait_ge(*lo_count(n, c))
                        for w, ps in enumerate((ps_1, ps_3)):
                            hi, lo = (buffer(v, n, c)[:, w * F:(w + 1) * F] for v in (wuh, wul))
                            for k, (l_, r_) in enumerate(((ah, hi), (ah, lo), (al, hi))):
                                last = pe.matmul(ps[:, 0:F], l_[:, p, c], r_, start=(c == 0 and k == 0),
                                                 stop=(c == CK - 1 and k == 2))
                    last.then_inc(s["up_done"], 1)

                def down(i, p, n):
                    pe.wait_ge(s["b_lo"], i + 1)
                    pe.wait_ge(s["pool_lo"], NG * n + NG)
                    if type(i) is not int or i >= 2:
                        pe.wait_ge(s["y_evicted"], i - 1)
                    for f in range(FT):
                        r = rows(f)
                        hi, lo = (buffer(v, n, f)[0:r] for v in (wdh, wdl))
                        for k, (l_, r_) in enumerate(((bh, hi), (bh, lo), (bl, hi))):
                            last = pe.matmul(ps_o[:, p], l_[0:r, f], r_, start=(f == 0 and k == 0),
                                             stop=(f == FT - 1 and k == 2))
                    last.then_inc(s["down_done"], 1)

                def turn_of(i):
                    return pe.value_load(turn[0:1, ds(i)], min_val=0, max_val=E - 1)

                def body(i, p, u, part):
                    n = turn_of(i)
                    if not is_first(i):
                        n_before = turn_of(i - 1)
                    if not is_last(i):
                        turn_x(i + 1, 1 - p)
                    if not is_first(i):
                        turn_h(i - 1)
                    up(i, p, n)
                    if not is_first(i):
                        down(i - 1, 1 - p, n_before)

                pe.wait_ge(s["up_done"], 1)
                turn_x(0, 0)
                every_block(pe, body)
                turn_h(NBLK - 1)
                down(NBLK - 1, (NBLK - 1) % 2, turn_of(NBLK - 1))

        if upto < 4:
            return

        (x1, z1), end = place(A, [("x1", [P, NT, C], F32), ("z1", [P, NT, C], F32)])
        assert end <= Bx
        (alpha, quant1, ssq, amax1, half, minus1, consts, halfalpha), _ = place(Y, [
            ("alpha", [P, NT], F32), ("quant1", [P, NT], F32), ("ssq", [P, NT], F32),
            ("amax1", [P, NT], F32), ("half", [P, NT], F32), ("minus1", [P, NT], F32),
            ("consts", [P, 6], F32), ("halfalpha", [P, NT], F32)])
        big, end = place(Bx, [
            ("lng_sb", [P, INNER], F32), ("lnb_sb", [P, INNER], F32), ("b2_sb", [P, C], F32),
            ("pre", [P, INNER], F32), ("hid5", [P, 2, INNER], F32),
            ("moved", [P, INNER], F32), ("junk", [P, INNER], BF16), ("hq", [P, INNER], BF16),
            ("hqT", [P, IK, P], BF16), ("moved1", [P, C], F32), ("xq", [P, C], BF16),
            ("xqT", [P, 2, CK, P], BF16), ("out_sb", [P, 2, C], F32), ("arow", [BR, 2, P], F32R),
            ("arows", [BR, NT, P], F32R), ("brow", [BR, INNER], F32R)])
        lng_sb, lnb_sb, b2_sb, pre, hid5, moved, junk, hq, hqT, moved1, xq, xqT, out_sb, arow, arows, brow = big
        assert end <= W, (end, W)
        with ExitStack() as st:
            s = Sems("g")
            (ya, yb, ysh, xin, sig), end = place(Ch, [
                ("ya", [P, 2, C], F32), ("yb", [P, 2, C], F32), ("ysh", [P, 2, C], F32),
                ("xin", [P, 2, C], F32), ("sig", [P, 2, C], F32)])
            assert end <= D
            (square, inv, rstd1, ia, ia_hi, winv1, acols), end = place(D, [
                ("square", [P, C], F32), ("inv", [P, NT], F32), ("rstd1", [P, NT], F32), ("ia", [P, NT], F32),
                ("ia_hi", [P, NT], F32R), ("winv1", [P, 1], F32), ("acols", [P, NT, BR], F32)])
            assert end <= Bx + (W - Bx) - 4 * (NT * P + INNER), "free of arows and brow"
            braw = at("braw", [BR, INNER], F32, W + 32768)
            ps_r = st.enter_context(nc.psum_tensor("ps_r4", [P, 2, CK, P], F32))
            ps_a = st.enter_context(nc.psum_tensor("ps_a", [BR, NT, P], F32))
            block = st.enter_context(nc.Block())

            @block.sync
            def _(sp):
                sp.wait_ge(s["braw0"], 1)
                for r in (0, 32, 64):
                    sp.dma_start(braw[r:r + 1], b1).then_inc(s["b_in"], 16)
                for t in range(NT):
                    p = t % 2
                    wait(sp, s["summed"], 3 * (t - 1))
                    sp.dma_start(ysh[:, p], yshared[t]).then_inc(s[f"rows_in{p}"], 16)
                    sp.dma_start(xin[:, p], x[t]).then_inc(s[f"rows_in{p}"], 16)

            @block.gpsimd
            def _(pool):
                pool.memset(half[:], -0.5).then_inc(s["half"], 1)
                pool.memset(braw[:], 0.0).then_inc(s["braw0"], 1)
                pool.memset(acols[:], 0.0).then_inc(s["acols0"], 1)
                for t in range(NT):
                    p = t % 2
                    wait(pool, s["summed"], 3 * (t - 1))
                    for k, dst in enumerate((ya, yb)):
                        pool.indirect_dma_start(dst[:, p], None, yslots, bass.IndirectOffsetOnAxis(
                            ap=slot[:, k, t:t + 1], axis=0)).then_inc(s[f"gathered{p}"], 16)
                pool.wait_ge(s["mean_square"], 1)
                pool.wait_ge(s["half"], 1)
                pool.tensor_tensor(rstd1[:], ssq[:], half[:], ALU.pow).then_inc(s["rstd"], 1)

            @block.tensor
            def _(pe):
                for t in range(NT):
                    wait(pe, s["mixed"], t - 1)
                    for c in range(CK):
                        last = pe.transpose(ps_r[:, t % 2, c], ratio[:, CK * (t // TT) + c, (t % TT) * P:(t % TT + 1) * P], ident[:])
                    last.then_inc(s["ratio_turned"], 1)
                pe.wait_ge(s["acols"], 3)
                for t in range(NT):
                    last = pe.transpose(ps_a[:, t], acols[:, t], ident[:])
                last.then_inc(s["a_turned"], 1)

            @block.scalar
            def _(act):
                for t in range(NT):
                    p = t % 2
                    act.wait_ge(s["summed"], 3 * t + 3)
                    wait(act, s["mixed"], t - 1)
                    act.activation(sig[:, p], x1[:, t], ACT.Sigmoid).then_inc(s["sigmoid"], 1)
                    if t:
                        act.wait_ge(s["mixed"], t)
                        wait(act, s["squared"], t - 1)
                        act.activation(square[:], z1[:, t - 1], ACT.Square, accum_out=ssq[:, t - 1:t]).then_inc(s["squared"], 1)
                act.wait_ge(s["b_in"], 48)
                act.activation(brow[:], braw[:], ACT.Copy).then_inc(s["brow"], 1)
                act.wait_ge(s["mixed"], NT)
                act.wait_ge(s["squared"], NT - 1)
                act.activation(square[:], z1[:, NT - 1], ACT.Square, accum_out=ssq[:, NT - 1:NT]).then_inc(s["squared"], 1)
                act.wait_ge(s["a_turned"], 1)
                act.activation(arows[:], ps_a[:], ACT.Copy).then_inc(s["arows"], 1)

            @block.vector
            def _(dve):
                def mix(t):
                    dve.wait_ge(s["sigmoid"], t + 1)
                    dve.wait_ge(s["ratio_turned"], t + 1)
                    dve.tensor_tensor(z1[:, t], sig[:, t % 2], ps_r[:, t % 2].rearrange("p c n -> p (c n)"), ALU.mult).then_inc(s["mixed"], 1)
                    dve.wait_ge(s["mixed"], t + 1)
                    dve.tensor_reduce(amax1[:, t:t + 1], z1[:, t], AX_X, ALU.max, apply_absolute_value=True).then_inc(s["amax"], 1)

                for t in range(NT):
                    p = t % 2
                    dve.wait_ge(s[f"rows_in{p}"], 32 * (t // 2 + 1))
                    dve.tensor_tensor(x1[:, t], xin[:, p], ysh[:, p], ALU.add).then_inc(s["summed"], 1)
                    dve.wait_ge(s[f"gathered{p}"], 32 * (t // 2 + 1))
                    for k, rows_ in enumerate((ya, yb)):
                        dve.wait_ge(s["summed"], 3 * t + 1 + k)
                        dve.scalar_tensor_tensor(out=x1[:, t], in0=rows_[:, p], scalar=weight[:, k, t:t + 1], in1=x1[:, t],
                                                 op0=ALU.mult, op1=ALU.add).then_inc(s["summed"], 1)
                    if t:
                        mix(t - 1)
                mix(NT - 1)
                dve.wait_ge(s["squared"], NT)
                dve.tensor_scalar(ssq[:], ssq[:], 1.0 / C, EPS, ALU.mult, ALU.add).then_inc(s["mean_square"], 1)
                dve.wait_ge(s["rstd"], 1)
                dve.wait_ge(s["amax"], NT)
                dve.tensor_tensor(amax1[:], amax1[:], rstd1[:], ALU.mult).then_inc(s["stat"], 1)
                dve.wait_ge(s["stat"], 1)
                dve.tensor_scalar(amax1[:], amax1[:], 1e-5, None, ALU.max).then_inc(s["stat"], 1)
                dve.wait_ge(s["stat"], 2)
                dve.tensor_scalar(alpha[:], amax1[:], wscale[:, 0:1], 1.0 / 127.0, ALU.mult, ALU.mult).then_inc(s["stat"], 1)
                dve.reciprocal(inv[:], amax1[:]).then_inc(s["stat"], 1)
                dve.reciprocal(winv1[:], wscale[:, 0:1]).then_inc(s["stat"], 1)
                dve.wait_ge(s["stat"], 5)
                dve.tensor_scalar(halfalpha[:], alpha[:], 0.5, None, ALU.mult).then_inc(s["stat"], 1)
                dve.tensor_scalar(ia[:], inv[:], winv1[:], 127.0, ALU.mult, ALU.mult).then_inc(s["ia"], 1)
                dve.wait_ge(s["ia"], 1)
                dve.tensor_copy(ia_hi[:], ia[:]).then_inc(s["ia"], 1)
                dve.wait_ge(s["ia"], 2)
                dve.wait_ge(s["acols0"], 1)
                dve.tensor_copy(acols[:, :, 0], f32(ia_hi[:])).then_inc(s["acols"], 1)
                dve.tensor_tensor(acols[:, :, 32], ia[:], f32(ia_hi[:]), ALU.subtract).then_inc(s["acols"], 1)
                dve.tensor_copy(acols[:, :, 64], f32(ia_hi[:])).then_inc(s["acols"], 1)
                dve.wait_ge(s["brow"], 1)
                dve.tensor_tensor(brow[64:65], braw[64:65], f32(brow[64:65]), ALU.subtract).then_inc(s["brow_lo"], 1)
                dve.scalar_tensor_tensor(out=quant1[:], in0=inv[:], scalar=127.0, in1=rstd1[:],
                                         op0=ALU.mult, op1=ALU.mult).then_inc(s["stat"], 1)

        if upto < 5:
            return
        with ExitStack() as st:
            s = Sems("f")
            (gsum, negmu, vsum, rstd, hsum, r2, amax2, m2, inv2, quant2, beta, factor), end = place(W + 32768, [
                (n, [P, 2], F32) for n in ("gsum", "negmu", "vsum", "rstd", "hsum", "r2", "amax2", "m2", "inv2",
                                            "quant2", "beta", "factor")])
            ps_q = st.enter_context(nc.psum_tensor("ps_q", [P, CK, P], BF16))
            ps_i = st.enter_context(nc.psum_tensor("ps_i", [P, INNER], F32))
            ps_k = st.enter_context(nc.psum_tensor("ps_k", [P, 2, IK // 2, P], BF16))
            ps_z = st.enter_context(nc.psum_tensor("ps_z", [P, C], F32))
            block = st.enter_context(nc.Block())
            FIRST, LAST = -2, NT + 2

            def there(t):
                return type(t) is not int or 0 <= t < NT

            def every_step(eng, step):
                for t in range(FIRST, 4):
                    step(t, t % 2)
                with eng.Fori(2, NT // 2 - 1) as j:
                    step(2 * j, 0)
                    step(2 * j + 1, 1)
                for t in range(NT - 2, LAST + 1):
                    step(t, t % 2)

            @block.sync
            def _(sp):
                for dst, src, n in ((lng_sb, lng, INNER), (lnb_sb, lnb, INNER), (b2_sb, b2, C)):
                    sp.dma_start(dst[:], src.to_broadcast([P, n])).then_inc(s["rows_in"], 16)

                def store(t, p):
                    sp.wait_ge(s["out_ready"], t + 1)
                    sp.dma_start(out[ds(t)].rearrange("a p n -> p (a n)"), out_sb[:, p]).then_inc(s[f"out{p}"], 16)

                with sp.Fori(0, NT // 2) as j:
                    store(2 * j, 0)
                    store(2 * j + 1, 1)
                for p in range(2):
                    sp.wait_ge(s[f"out{p}"], 16 * NT // 2)

            @block.gpsimd
            def _(pool):
                def tiny(out_, a, b, op, name):
                    pool.tensor_tensor(out_, a, b, op).then_inc(s[name], 1)

                def const(n):
                    return consts[:, n:n + 1]

                def after_square(t, p):
                    def col(v):
                        return v[:, p:p + 1]

                    pool.wait_ge(s["hsq"], t + 1)
                    tiny(col(hsum), col(hsum), const(1), ALU.mult, "tiny_h")
                    pool.wait_ge(s["tiny_h"], 3 * t + 1)
                    tiny(col(hsum), col(hsum), const(2), ALU.add, "tiny_h")
                    pool.wait_ge(s["tiny_h"], 3 * t + 2)
                    tiny(col(r2), col(hsum), half[:, 0:1], ALU.pow, "r2")
                    pool.wait_ge(s["peak"], t + 1)
                    tiny(col(inv2), col(m2), minus1[:, 0:1], ALU.pow, "tiny_h")
                    wait(pool, s["out_ready"], t - 1)
                    tiny(col(beta), col(m2), const(3), ALU.mult, "beta")
                    pool.wait_ge(s["tiny_h"], 3 * t + 3)
                    tiny(col(inv2), col(inv2), const(4), ALU.mult, "inv2")
                    pool.wait_ge(s["inv2"], t + 1)
                    tiny(col(quant2), col(r2), col(inv2), ALU.mult, "quant2")

                def after_variance(t, p):
                    def col(v):
                        return v[:, p:p + 1]

                    pool.wait_ge(s["var"], t + 1)
                    tiny(col(vsum), col(vsum), const(1), ALU.mult, "tiny_v")
                    pool.wait_ge(s["tiny_v"], 2 * t + 1)
                    tiny(col(vsum), col(vsum), const(2), ALU.add, "tiny_v")
                    pool.wait_ge(s["tiny_v"], 2 * t + 2)
                    tiny(col(rstd), col(vsum), half[:, 0:1], ALU.pow, "rstd")

                def step(t, p):
                    if there(t - 1):
                        after_square(t - 1, 1 - p)
                    if there(t):
                        x_ = x1[:, ds(t)].rearrange("p a n -> p (a n)")
                        pool.tensor_tensor(x_, x_, b2_sb[:], ALU.add).then_inc(s["x_bias"], 1)
                        after_variance(t, p)

                pool.memset(minus1[:], -1.0).then_inc(s["consts"], 1)
                for n, value in ((1, 1.0 / INNER), (2, EPS), (4, 127.0)):
                    pool.memset(const(n), value).then_inc(s["consts"], 1)
                pool.tensor_scalar(const(3), wscale[:, 1:2], 1.0 / 127.0, None, ALU.mult).then_inc(s["consts"], 1)
                pool.wait_ge(s["consts"], 5)
                pool.wait_ge(s["rows_in"], 48)
                every_step(pool, step)

            @block.scalar
            def _(act):
                def step(t, p):
                    if there(t):
                        act.wait_ge(s["up_done"], t + 1)
                        wait(act, s["moved"], t - 1)
                        act.wait_ge(s["factor"], t + 1)
                        act.activation(hid5[:, p], ps_i[:], ACT.Tanh, scale=factor[:, p:p + 1]).then_inc(s["tanh"], 1)
                    if there(t - 2):
                        act.wait_ge(s["h_turned"], t - 1)
                        wait(act, s["down_done"], t - 2)
                        act.activation(hqT[:], ps_k[:].rearrange("p a k n -> p (a k) n"), ACT.Copy).then_inc(s["hqT"], 1)
                    if there(t - 1):
                        act.wait_ge(s["normed"], t)
                        act.wait_ge(s["var"], t)
                        act.activation(junk[:], hid5[:, 1 - p], ACT.Square, accum_out=hsum[:, 1 - p:2 - p]).then_inc(s["hsq"], 1)
                    if there(t + 2):
                        wait(act, s["xq"], t + 2)
                    if there(t):
                        act.wait_ge(s["silu2"], t + 1)
                        act.activation(hid5[:, p], pre[:], ACT.Gelu, scale=factor[:, p:p + 1], accum_out=gsum[:, p:p + 1]).then_inc(s["gelu"], 1)
                    if there(t + 2):
                        act.activation(moved1[:], z1[:, ds(t + 2)].rearrange("p a n -> p (a n)"), ACT.Copy, bias=ROUND,
                                       scale=quant1[:, ds(t + 2)]).then_inc(s["moved1"], 1)
                        act.activation(arow[:, p], f32(arows[:, ds(t + 2)].rearrange("r a n -> r (a n)")), ACT.Copy).then_inc(s["arow"], 1)
                    if there(t):
                        act.wait_ge(s["gelu"], t + 1)
                        act.activation(negmu[:, p:p + 1], gsum[:, p:p + 1], ACT.Copy, scale=-1.0 / INNER).then_inc(s["negmu"], 1)
                        act.wait_ge(s["negmu"], t + 1)
                        wait(act, s["hsq"], t)
                        act.activation(junk[:], hid5[:, p], ACT.Square, bias=negmu[:, p:p + 1], accum_out=vsum[:, p:p + 1]).then_inc(s["var"], 1)
                    if there(t + 1):
                        act.activation(factor[:, 1 - p:2 - p], halfalpha[:, ds(t + 1)], ACT.Copy).then_inc(s["factor"], 1)
                    if there(t - 1):
                        act.wait_ge(s["quant2"], t)
                        wait(act, s["hq"], t - 1)
                        act.activation(moved[:], hid5[:, 1 - p], ACT.Copy, bias=ROUND, scale=quant2[:, 1 - p:2 - p]).then_inc(s["moved"], 1)

                every_step(act, step)

            @block.vector
            def _(dve):
                def step(t, p):
                    if there(t - 1):
                        dve.wait_ge(s["rstd"], t)
                        dve.wait_ge(s["centred"], t)
                        dve.scalar_tensor_tensor(out=hid5[:, 1 - p], in0=hid5[:, 1 - p], scalar=rstd[:, 1 - p:2 - p], in1=lnb_sb[:],
                                                 op0=ALU.mult, op1=ALU.add).then_inc(s["normed"], 1)
                    if there(t):
                        dve.wait_ge(s["tanh"], t + 1)
                        wait(dve, s["gelu"], t)
                        dve.scalar_tensor_tensor(out=pre[:], in0=hid5[:, p], scalar=1.0, in1=ps_i[:],
                                                 op0=ALU.add, op1=ALU.mult).then_inc(s["silu2"], 1)
                    if there(t - 1):
                        dve.wait_ge(s["normed"], t)
                        dve.tensor_reduce(amax2[:, 1 - p:2 - p], hid5[:, 1 - p], AX_X, ALU.max, apply_absolute_value=True).then_inc(s["amax"], 1)
                    if there(t - 3):
                        q = 1 - p
                        wait(dve, s[f"out{q}"], 8 * (t - 3 - q))
                        dve.wait_ge(s["beta"], t - 2)
                        dve.wait_ge(s["x_bias"], t - 2)
                        dve.wait_ge(s["down_done"], t - 2)
                        dve.scalar_tensor_tensor(out=out_sb[:, q], in0=ps_z[:], scalar=beta[:, q:q + 1],
                                                 in1=x1[:, ds(t - 3)].rearrange("p a n -> p (a n)"),
                                                 op0=ALU.mult, op1=ALU.add).then_inc(s["out_ready"], 1)
                    if there(t - 1):
                        dve.wait_ge(s["r2"], t)
                        dve.wait_ge(s["amax"], t)
                        dve.tensor_scalar(m2[:, 1 - p:2 - p], amax2[:, 1 - p:2 - p], r2[:, 1 - p:2 - p], 1e-5,
                                          ALU.mult, ALU.max).then_inc(s["peak"], 1)
                    if there(t + 2):
                        dve.wait_ge(s["moved1"], t + 3)
                        wait(dve, s["x_turned"], t + 2)
                        dve.tensor_scalar(xq[:], moved1[:], ROUND, None, ALU.subtract).then_inc(s["xq"], 1)
                    if there(t):
                        dve.wait_ge(s["var"], t + 1)
                        dve.scalar_tensor_tensor(out=hid5[:, p], in0=hid5[:, p], scalar=negmu[:, p:p + 1], in1=lng_sb[:],
                                                 op0=ALU.add, op1=ALU.mult).then_inc(s["centred"], 1)
                    if there(t + 2):
                        dve.wait_ge(s["x_turned"], t + 3)
                        wait(dve, s["up_done"], t + 1)
                        dve.tensor_copy(xqT[:, p], ps_q[:]).then_inc(s["xqT"], 1)
                    if there(t - 1):
                        dve.wait_ge(s["moved"], t)
                        wait(dve, s["h_turned"], t - 1)
                        dve.tensor_scalar(hq[:], moved[:], ROUND, None, ALU.subtract).then_inc(s["hq"], 1)

                dve.wait_ge(s["rows_in"], 48)
                every_step(dve, step)

            @block.tensor
            def _(pe):
                def step(t, p):
                    if there(t + 1):
                        pe.wait_ge(s["xqT"], t + 2)
                        wait(pe, s["silu2"], t + 1)
                        pe.wait_ge(s["arow"], t + 2)
                        for n in range(INNER // C):
                            for c in range(CK):
                                last = pe.matmul(ps_i[:, n * C:(n + 1) * C], xqT[:, 1 - p, c],
                                                 w1q[:, 2 * c + n // 2, (n % 2) * C:(n % 2 + 1) * C], start=c == 0, stop=False)
                            last = pe.matmul(ps_i[:, n * C:(n + 1) * C], arow[:, 1 - p], brow[:, n * C:(n + 1) * C],
                                             start=False, stop=True)
                        last.then_inc(s["up_done"], 1)
                    if there(t + 2):
                        pe.wait_ge(s["xq"], t + 3)
                        wait(pe, s["xqT"], t + 2)
                        for c in range(CK):
                            last = pe.transpose(ps_q[:, c], xq[:, c * P:(c + 1) * P], ident_b[:])
                        last.then_inc(s["x_turned"], 1)
                    if there(t - 2):
                        pe.wait_ge(s["hqT"], t - 1)
                        wait(pe, s["out_ready"], t - 2)
                        for k in range(IK):
                            last = pe.matmul(ps_z[:], hqT[:, k], w2q[:, k // 2, (k % 2) * C:(k % 2 + 1) * C],
                                             start=k == 0, stop=k == IK - 1)
                        last.then_inc(s["down_done"], 1)
                    if there(t - 1):
                        pe.wait_ge(s["hq"], t)
                        wait(pe, s["hqT"], t - 1)
                        for k in range(IK):
                            last = pe.transpose(ps_k[:, k // 8, k % 8], hq[:, k * P:(k + 1) * P], ident_b[:])
                        last.then_inc(s["h_turned"], 1)

                every_step(pe, step)




def laid_out(inputs):
    import numpy as np

    def a(name):
        return np.asarray(inputs[name])

    def by_channel(v):
        return v.reshape(B, T, CK, P).transpose(0, 2, 3, 1)

    def column(v):
        return v.reshape(CK, P).T

    def up_weights(w1, w3):
        return np.concatenate([w1, w3], axis=-2).swapaxes(-1, -2).reshape(*w1.shape[:-2], CK, P, -1)

    arrays = {
        "xT": by_channel(a("x")),
        "kT": by_channel(a("fside_BxSxS_0")),
        "x": a("x").reshape(NT, P, C),
        "cond": a("cond_512").T,
        "wu": np.stack([column(a(n)) for n in ("L0_cond_w", "L0_cond_u", "L1_cond_w", "L1_cond_u")], axis=1),
        "gate": a("L0_ffn_gate_w").T.reshape(CK, P, E).transpose(1, 0, 2),
        "sw13": np.stack([a("L0_ffn_sw1").T.reshape(CK, P, SF), a("L0_ffn_sw3").T.reshape(CK, P, SF)]),
        "sw2": a("L0_ffn_sw2").T,
        "w13": up_weights(a("L0_ffn_w1"), a("L0_ffn_w3")),
        "w2": a("L0_ffn_w2").swapaxes(1, 2),
        "w1p": a("L1_ffn_w1").T.reshape(CK, P, 2, PIECE).transpose(0, 2, 1, 3).reshape(NPIECE, P, PIECE),
        "w2p": a("L1_ffn_w2").T.reshape(NPIECE, 2, P, C).transpose(0, 2, 1, 3).reshape(NPIECE, P, PIECE),
        "b1": a("L1_ffn_b1").reshape(1, INNER),
        "lng": a("L1_ffn_ln_g").reshape(1, INNER),
        "lnb": a("L1_ffn_ln_b").reshape(1, INNER),
        "b2": a("L1_ffn_b2").reshape(1, C),
    }
    return {n: np.ascontiguousarray(v) for n, v in arrays.items()}


def kernel(**inputs):
    import concourse.bacc as bacc
    from concourse.bass_utils import run_bass_kernel_spmd

    nc = bacc.Bacc("TRN2", target_bir_lowering=False, num_devices=1)
    arrays = laid_out(inputs)
    args = [nc.dram_tensor(n, v.shape, F32, kind="ExternalInput").ap() for n, v in arrays.items()]
    args.append(nc.dram_tensor("out", (NT, P, C), F32, kind="ExternalOutput").ap())
    args.append(nc.dram_tensor("xslots", (SLOTS, C), F32, kind="Internal").ap())
    args.append(nc.dram_tensor("yslots", (SLOTS, C), F32, kind="Internal").ap())
    args.append(nc.dram_tensor("yshared", (NT, P, C), F32, kind="Internal").ap())
    build(nc, *args)
    got = run_bass_kernel_spmd(nc, [arrays], core_ids=[0])
    return got.results[0]["out"].reshape(B, T, C)
```

```python
from contextlib import ExitStack

import concourse.bass as bass
from concourse import mybir

P = 128
F32 = mybir.dt.float32
F32R = mybir.dt.float32r
BF16 = mybir.dt.bfloat16
I32 = mybir.dt.int32
ALU = mybir.AluOpType
ACT = mybir.ActivationFunctionType
AX_X = mybir.AxisListType.X

B, T, C = 4, 512, 512
CK = C // P
TT = T // P
NT = B * TT
E, TOPK = 16, 2
F = 352
FT = 3
SF = 704
SFT = 6
INNER = 2048
IK = INNER // P
NBLK = (B * T * TOPK + E * (P - 1)) // P
SLOTS = NBLK * P
PIECE = 1024
NPIECE = C * INNER // P // PIECE
NW = 2 * NPIECE
ROUND = 12582912.0
EPS = 1e-5
BR = P


def ds(i, n=1):
    return bass.ds(i, n)


def f32(ap):
    return ap.bitcast(F32)


def build(nc, xT, kT, x, cond, wu, gate, sw13, sw2, w13, w2, wp, b1, lng, lnb, b2, out,
          xslots, yslots, yshared):
    with ExitStack() as ctx:
        base = nc.sbuf_base
        base += -base % 64
        top = [base]

        def region(nbytes):
            at = top[0]
            top[0] += nbytes + (-nbytes % 32)
            return at

        def at(name, shape, dt, offset):
            return nc.alloc_sbuf_tensor_at(name, shape, dt, offset=offset)

        def size(shape, dt):
            n = 2 if dt == BF16 else 4
            for s in shape[1:]:
                n *= s
            return n

        def place(offset, tensors):
            got = []
            for name, shape, dt in tensors:
                got.append(at(name, shape, dt, offset))
                offset += size(shape, dt) + (-size(shape, dt) % 64)
            return got, offset

        def keep(name, shape, dt):
            return at(name, shape, dt, region(size(shape, dt)))

        ident = keep("ident", [P, P], F32)
        ones = keep("ones", [P, P], F32)
        decay = keep("decay", [P, 2, B, CK], F32)
        wu_sb = keep("wu_sb", [P, 4, CK], F32)
        probs = keep("probs", [P, NT, E], F32)
        weight = keep("weight", [P, TOPK, NT], F32)
        slot = keep("slot", [P, TOPK, NT], I32)
        block_expert = keep("block_expert", [1, NBLK + 1], I32)
        fresh = keep("fresh", [1, NBLK + 1], I32)
        turn_before = keep("turn_before", [1, NBLK + 1], I32)
        turn = keep("turn", [1, NBLK + 1], I32)
        unit_out = keep("unit_out", [P, B, CK], F32)
        unit_u = keep("unit_u", [P, B, CK], F32)
        wscale = keep("wscale", [P, 2], F32)
        winv = keep("winv", [P, 2, NPIECE], F32)

        A = region(2 * 4 * (2 * CK * SF + SFT * C))
        Bx = region(2 * 2 * CK * T * 4)
        Ch = region(2 * SFT * T * 4)
        D = region(NT * C * 4)
        W = region(40960)
        Y = region(2 * C * 4)
        assert top[0] <= nc.sbuf_usable_end, (top[0], nc.sbuf_usable_end)

        ratio = at("ratio", [P, B * CK, T], F32, Bx)
        wq = at("wq", [P, NW, PIECE], BF16, W)
        w1q, w2q = wq[:, 0:NPIECE], wq[:, NPIECE:NW]
        y_sb = at("y_sb", [P, 2, C], F32, Y)

        def wait(eng, sem, value):
            if type(value) is not int or value > 0:
                eng.wait_ge(sem, value)

        class Sems:

            def __init__(self, tag):
                self.tag, self.made = tag, {}

            def __getitem__(self, name):
                if name not in self.made:
                    self.made[name] = nc.alloc_semaphore(name=f"{self.tag}_{name}")
                return self.made[name]

        with ExitStack() as st:
            s = Sems("c")
            (cond_sb, ea, tf, dfac, ofac), _ = place(A, [
                ("cond_sb", [P, B], F32), ("ea", [P, 2, CK], F32), ("tf", [P, B], F32), ("dfac", [P, B], F32),
                ("ofac", [P, B], F32)])
            ps_c = st.enter_context(nc.psum_tensor("ps_c", [P, 512], F32))
            block = st.enter_context(nc.Block())

            @block.sync
            def _(sp):
                sp.dma_start(cond_sb[:], cond).then_inc(s["small_in"], 16)
                sp.dma_start(wu_sb[:], wu).then_inc(s["small_in"], 16)

            @block.gpsimd
            def _(pool):
                pool.memset(ones[:], 1.0).then_inc(s["tables"], 1)
                pool.memset(ident[:], 0.0).then_inc(s["tables"], 1)
                pool.wait_ge(s["tables"], 2)
                pool.affine_select(out=ident[:], in_=ident[:], compare_op=ALU.not_equal, fill=1.0, base=0,
                                   pattern=[[-1, P]], channel_multiplier=1).then_inc(s["tables"], 1)

            @block.tensor
            def _(pe):
                pe.wait_ge(s["small_in"], 32)
                pe.wait_ge(s["tables"], 1)
                pe.matmul(ps_c[:, 0:B], ones[:], cond_sb[:], start=True, stop=True).then_inc(s["cond_sum"], 1)

            @block.scalar
            def _(act):
                act.wait_ge(s["small_in"], 32)
                wv = wu_sb[:].rearrange("p (l k) c -> p l k c", k=2)[:, :, 0, :]
                act.activation(ea[:], wv, ACT.Exp).then_inc(s["exp_w"], 1)
                act.wait_ge(s["exp_w"], 1)
                act.activation(ea[:], ea[:], ACT.Exp, scale=-1.0).then_inc(s["exp_w"], 1)
                act.wait_ge(s["cond_sum"], 1)
                act.activation(tf[:], ps_c[:, 0:B], ACT.Exp, scale=-1.0).then_inc(s["exp_s"], 1)

            @block.vector
            def _(dve):
                dve.wait_ge(s["exp_s"], 1)
                dve.tensor_scalar(tf[:], tf[:], 1.0, None, ALU.add).then_inc(s["tf"], 1)
                dve.wait_ge(s["tf"], 1)
                dve.reciprocal(tf[:], tf[:]).then_inc(s["tf"], 1)
                dve.wait_ge(s["tf"], 2)
                dve.tensor_scalar(dfac[:], tf[:], 0.5, 0.5, ALU.mult, ALU.add).then_inc(s["tf"], 1)
                dve.tensor_scalar(ofac[:], tf[:], 0.2, 0.8, ALU.mult, ALU.add).then_inc(s["tf"], 1)
                dve.wait_ge(s["tf"], 3)
                dve.wait_ge(s["exp_w"], 2)
                for b in range(B):
                    dve.tensor_scalar(decay[:, :, b, :], ea[:], dfac[:, b:b + 1], None, ALU.mult).then_inc(s["decay"], 1)
                dve.wait_ge(s["tf"], 4)
                dve.tensor_copy(unit_out[:], ofac[:].unsqueeze(2).to_broadcast([P, B, CK])).then_inc(s["decay"], 1)
                dve.tensor_copy(unit_u[:], wu_sb[:, 3].unsqueeze(1).to_broadcast([P, B, CK])).then_inc(s["decay"], 1)

        NUNIT = CK * B

        def wkv(s, bufs):
            k_in, x_in, ev, uv, fw, bw, mixed = bufs

            def load(sp, u):
                p = u % 2
                wait(sp, s["mixed_ready"], u - 1)
                sp.dma_start(x_in[:, p], xT[u // CK, u % CK]).then_inc(s[f"x_in{p}"], 16)
                if u + 1 < NUNIT:
                    load_k(sp, u + 1)

            def load_k(sp, u):
                p = u % 2
                wait(sp, s["uv_ready"], u - 1)
                sp.dma_start(k_in[:, p], kT[u // CK, u % CK]).then_inc(s[f"k_in{p}"], 16)

            def landed(u):
                return 16 * (u // 2 + 1)

            def prep_dve(dve, u):
                p = u % 2
                dve.wait_ge(s[f"k_in{p}"], landed(u))
                dve.tensor_scalar(ev[:, p, 1], k_in[:, p], 30.0, None, ALU.min).then_inc(s["k_clipped"], 1)
                dve.tensor_scalar(uv[:, p, 1], k_in[:, p], wu_sb[:, 1, u % CK:u % CK + 1], 30.0,
                                  ALU.add, ALU.min).then_inc(s["uk_clipped"], 1)

            def prep_act(act, u):
                p = u % 2
                act.wait_ge(s["k_clipped"], u + 1)
                act.activation(ev[:, p, 1], ev[:, p, 1], ACT.Exp).then_inc(s["ek_ready"], 1)
                act.wait_ge(s["uk_clipped"], u + 1)
                act.activation(uv[:, p, 1], uv[:, p, 1], ACT.Exp).then_inc(s["eu_ready"], 1)
                act.wait_ge(s[f"x_in{p}"], landed(u))
                act.activation(x_in[:, p], x_in[:, p], ACT.Exp, scale=-1.0).then_inc(s["ex"], 1)
                act.wait_ge(s["ex"], 2 * u + 1)
                act.activation(x_in[:, p], x_in[:, p], ACT.Copy, bias=1.0).then_inc(s["ex"], 1)

            def prep_pool(pool, u):
                p = u % 2
                pool.wait_ge(s["ek_ready"], u + 1)
                pool.tensor_tensor(ev[:, p, 0], ev[:, p, 1], k_in[:, p], ALU.mult).then_inc(s["ev_ready"], 1)
                pool.wait_ge(s["eu_ready"], u + 1)
                pool.tensor_tensor(uv[:, p, 0], uv[:, p, 1], k_in[:, p], ALU.mult).then_inc(s["uv_ready"], 1)

            def mix_dve(dve, u):
                b, c, p = u // CK, u % CK, u % 2
                d = decay[:, 0, b, c:c + 1]
                steps = 8
                dve.wait_ge(s["ev_ready"], u + 1)
                wait(dve, s["mixed_ready"], u)
                for j in range(2):
                    dve.tensor_tensor_scan(fw[:, j], d.to_broadcast([P, T]), ev[:, p, j], 0.0,
                                           ALU.mult, ALU.add).then_inc(s["step"], 1)
                for j in range(2):
                    dve.tensor_tensor_scan(bw[:, j, ::-1], d.to_broadcast([P, T]), ev[:, p, j, ::-1], 0.0,
                                           ALU.mult, ALU.add).then_inc(s["step"], 1)
                dve.wait_ge(s["step"], steps * u + 4)
                dve.scalar_tensor_tensor(out=fw[:, :, 0:T - 1], in0=bw[:, :, 1:T], scalar=d, in1=fw[:, :, 0:T - 1],
                                         op0=ALU.mult, op1=ALU.add).then_inc(s["step"], 1)
                dve.wait_ge(s["uv_ready"], u + 1)
                dve.wait_ge(s["step"], steps * u + 5)
                dve.tensor_tensor(fw[:], fw[:], uv[:, p], ALU.add).then_inc(s["step"], 1)
                dve.wait_ge(s["step"], steps * u + 6)
                dve.wait_ge(s["ex"], 2 * u + 2)
                dve.scalar_tensor_tensor(out=fw[:, 1], in0=fw[:, 1], scalar=1e-8, in1=x_in[:, p],
                                         op0=ALU.max, op1=ALU.mult).then_inc(s["step"], 1)
                dve.wait_ge(s["step"], steps * u + 7)
                dve.reciprocal(fw[:, 1], fw[:, 1]).then_inc(s["step"], 1)
                dve.wait_ge(s["step"], steps * u + 8)
                wait(dve, s["mixed_read"], u - 1)
                wait(dve, s["x_lo"], u - 1)
                dve.scalar_tensor_tensor(out=mixed[:, p], in0=fw[:, 0], scalar=unit_out[:, b, c:c + 1], in1=fw[:, 1],
                                         op0=ALU.mult, op1=ALU.mult).then_inc(s["mixed_ready"], 1)

            return load, load_k, prep_dve, prep_act, prep_pool, mix_dve

        tok = at("tok", [P, NT, C], F32, D)
        with ExitStack() as st:
            s = Sems("m")
            bufs, _ = place(W, [
                ("k_in", [P, 2, T], F32), ("x_in", [P, 2, T], F32),
                ("ev", [P, 2, 2, T], F32),
                ("uv", [P, 2, 2, T], F32),
                ("fw", [P, 2, T], F32),
                ("bw", [P, 2, T], F32),
                ("mixed", [P, 2, T], F32)])
            load, load_k, prep_dve, prep_act, prep_pool, mix_dve = wkv(s, bufs)
            mixed = bufs[-1]
            (s13h, s13l, s2h, s2l), _ = place(A, [
                ("s13h", [P, 2, CK, SF], F32R), ("s13l", [P, 2, CK, SF], F32R),
                ("s2h", [P, SFT, C], F32R), ("s2l", [P, SFT, C], F32R)])
            (xh, xl), _ = place(Bx, [("xh", [P, 2, CK, T], F32R), ("xl", [P, 2, CK, T], F32R)])
            (hh, hl), _ = place(Ch, [("hh", [P, SFT, T], F32R), ("hl", [P, SFT, T], F32R)])
            stage = at("stage", [P, 4, SF], F32, D + 8 * C * 4)
            zero = at("zero", [P, C], F32, D + (NT - 1) * C * 4)
            CLEAR = 5
            raw = at("raw", [P, 2, PIECE], F32, D + 2 * TT * C * 4)
            junk2 = at("junk2", [P, PIECE], BF16, D + 3 * TT * C * 4)
            tables, tend = place(W, [
                ("below", [P, P], BF16), ("ones_b", [P, P], BF16), ("mask", [P, NT, E], BF16),
                ("index16", [P, E], F32), ("full", [P, NT], F32), ("block_no", [1, NBLK + 1], F32),
                ("top", [P, NT], F32), ("cand", [P, NT, E], F32), ("chosen", [P, TOPK, NT, E], F32),
                ("rank", [P, NT, E], F32), ("many", [P, E, NT], F32), ("blocks", [P, E], F32),
                ("ends", [P, E], F32), ("first", [P, E], F32), ("slotf", [P, TOPK, NT], F32),
                ("count", [P, E], F32), ("past", [1, NBLK + 1, E], F32), ("owner", [1, NBLK + 1], F32),
                ("change", [1, NBLK + 1], F32), ("changes", [1, NBLK + 1], F32), ("wtotal", [P, 2], F32),
                ("wmean", [P, 2], F32)])
            assert tend <= W + 36864
            (below, ones_b, mask, index16, full, block_no, top_, cand, chosen, rank, many, blocks,
             ends, first_, slotf, count, past, owner, change, changes, wtotal, wmean) = tables
            abs_sum = winv[:].rearrange("p l n -> p (l n)")
            gate_sb = at("gate_sb", [P, CK, E], F32, top[0])
            hbase = top[0] + CK * E * 4
            hf = at("hf", [P, 2, T], F32, hbase)
            th = at("th", [P, 2, T], F32, Y)
            ps_t = st.enter_context(nc.psum_tensor("ps_t", [P, TT, P], F32))
            ps_l = st.enter_context(nc.psum_tensor("ps_l", [P, 512], F32))
            ps_u = st.enter_context(nc.psum_tensor("ps_u", [P, 2, 2, T], F32))
            ps_y = st.enter_context(nc.psum_tensor("ps_y", [P, 2, C], F32))
            ps_lg = ps_l[:, 0:TT * E].rearrange("p (t e) -> p t e", e=E)
            ps_r = ps_t[:].rearrange("p a n -> p (a n)")[:, 0:NT * E].rearrange("p (t e) -> p t e", e=E)
            block = st.enter_context(nc.Block())

            pieces = [(sw13[w, c], s13h[:, w, c], s13l[:, w, c], P, SF) for w in range(2) for c in range(CK)]
            for f in range(SFT):
                rows = min(P, SF - f * P)
                pieces.append((sw2[f * P:f * P + rows], s2h[0:rows, f], s2l[0:rows, f], rows, C))
            cut = [0, 4, 8, 12, len(pieces)]

            def rows_of(f):
                return min(P, SF - f * P)

            def tiles_of(b, c):
                return (2 * c, 2 * c + 1) if b and 2 * c < SFT else ()

            @block.sync
            def _(sp):
                load_k(sp, 0)
                load(sp, 0)
                load(sp, 1)
                sp.dma_start(gate_sb[:], gate).then_inc(s["gate_in"], 16)
                for n, (src, _, _, rows, cols) in enumerate(pieces):
                    if n >= 4:
                        sp.wait_ge(s["piece_lo"], n - 3)
                    sp.dma_start(stage[0:rows, n % 4, 0:cols], src).then_inc(s[f"piece_in{n % 4}"], 16)
                    if n in (3, 7, 11):
                        load(sp, n // 4 + 2)
                sp.wait_ge(s["zero"], 1)
                def raw_loads(m0):
                    for m in (m0, m0 + 1):
                        wait(sp, s["abs_summed"], m - 1)
                        sp.dma_start(raw[:, m % 2], wp[m]).then_inc(s[f"raw_in{m % 2}"], 16)

                for b in range(1, B + 1):
                    for u in range(5 if b == 1 else CK * b + 3, min(CK * (b + 1) + 3, NUNIT)):
                        if u in (7, 8, 9, 10):
                            raw_loads(4 * (u - 7) + 2)
                        load(sp, u)
                        if u in (7, 8, 9):
                            raw_loads(4 * (u - 6))
                        if u == 5:
                            sp.wait_ge(s["piece_lo"], len(pieces))
                            raw_loads(0)
                        n = min(CLEAR, NBLK - CLEAR * (u - 5))
                        if n > 0:
                            sp.dma_start(xslots.rearrange("(n p) c -> p n c", p=P)[:, CLEAR * (u - 5):CLEAR * (u - 5) + n],
                                         zero[:].unsqueeze(1).to_broadcast([P, n, C])).then_inc(s["cleared"], 16)
                    for t in range(TT):
                        y = TT * (b - 1) + t
                        sp.wait_ge(s["y_evicted"], y + 1)
                        sp.dma_start(yshared[y], y_sb[:, t % 2]).then_inc(s[f"y_out{t % 2}"], 16)

            @block.gpsimd
            def _(pool):
                def x_lo(b, c):
                    u = CK * b + c
                    pool.wait_ge(s["x_hi"], u + 1)
                    pool.tensor_tensor(xl[:, b % 2, c], mixed[:, c % 2], f32(xh[:, b % 2, c]), ALU.subtract).then_inc(s["x_lo"], 1)

                def h_lo(b, f):
                    n = SFT * b + f
                    r = rows_of(f)
                    pool.wait_ge(s["h_hi"], n + 1)
                    pool.tensor_tensor(hl[0:r, f], hf[0:r, f % 2], f32(hh[0:r, f]), ALU.subtract).then_inc(s["h_lo"], 1)

                def make_tables():
                    pool.wait_ge(s["mixed_ready"], NUNIT)
                    pool.memset(ones_b[:], 1.0).then_inc(s["tables"], 1)
                    pool.wait_ge(s["tables"], 1)
                    pool.affine_select(out=below[:], in_=ones_b[:], compare_op=ALU.is_gt, fill=0.0, base=0,
                                       pattern=[[1, P]], channel_multiplier=-1).then_inc(s["tables"], 1)
                    pool.iota(index16[:], pattern=[[1, E]], base=-E, channel_multiplier=0,
                              allow_small_or_imprecise_dtypes=True).then_inc(s["tables"], 1)
                    pool.iota(full[:], pattern=[[P, NT]], base=0, channel_multiplier=0,
                              allow_small_or_imprecise_dtypes=True).then_inc(s["tables"], 1)
                    pool.iota(block_no[:], pattern=[[1, NBLK + 1]], base=0, channel_multiplier=0,
                              allow_small_or_imprecise_dtypes=True).then_inc(s["tables"], 1)

                def scatter(n0, n1):
                    for n in range(n0, n1):
                        t, k = n // TOPK, n % TOPK
                        pool.indirect_dma_start(
                            xslots, bass.IndirectOffsetOnAxis(ap=slot[:, k, t:t + 1], axis=0),
                            tok[:, t], None).then_inc(s["scattered"], 16)

                pool.memset(zero[:], 0.0).then_inc(s["zero"], 1)
                prep_pool(pool, 0)
                prep_pool(pool, 1)
                for b in range(B + 1):
                    for c in range(CK):
                        if b < B:
                            x_lo(b, c)
                        if CK * b + c + 2 < NUNIT:
                            prep_pool(pool, CK * b + c + 2)
                        for n in range(cut[c], cut[c + 1]) if b == 0 else ():
                            _, hi, lo, rows, cols = pieces[n]
                            pool.wait_ge(s["piece_hi"], n + 1)
                            pool.tensor_tensor(lo, stage[0:rows, n % 4, 0:cols], f32(hi), ALU.subtract).then_inc(s["piece_lo"], 1)
                        if b == B - 1 and c == CK - 1:
                            make_tables()
                            pool.wait_ge(s["cleared"], 16 * -(-NBLK // CLEAR))
                            pool.wait_ge(s["tok_ready"], NUNIT)
                            pool.wait_ge(s["slots"], 1)
                            scatter(0, 8)
                        for f in tiles_of(b, c):
                            h_lo(b - 1, f)
                            if b == B and f < SFT - 2:
                                scatter(3 * f + 8, 3 * f + 11)
                scatter(3 * (SFT - 2) + 8, NT * TOPK)
                pool.wait_ge(s["scattered"], 16 * NT * TOPK)

            @block.scalar
            def _(act):
                def x_hi(b, c):
                    u = CK * b + c
                    act.wait_ge(s["mixed_ready"], u + 1)
                    wait(act, s["up_done"], SFT * (b - 1))
                    act.activation(xh[:, b % 2, c], mixed[:, c % 2], ACT.Copy).then_inc(s["x_hi"], 1)
                    act.wait_ge(s["turned"], u + 1)
                    if b == B - 1 and c == 0:
                        act.wait_ge(s["cleared"], 16 * -(-NBLK // CLEAR))
                    act.activation(tok[:, TT * b:TT * (b + 1), c * P:(c + 1) * P], ps_t[:], ACT.Copy).then_inc(s["tok_ready"], 1)

                def tanh(b, f):
                    n = SFT * b + f
                    r = rows_of(f)
                    act.wait_ge(s["up_done"], n + 1)
                    if f < 2:
                        wait(act, s[f"y_out{f}"], 16 * 2 * b)
                    act.activation(th[0:r, f % 2], ps_u[0:r, f % 2, 0], ACT.Tanh, scale=0.5).then_inc(s["tanh"], 1)

                def h_hi(b, f):
                    n = SFT * b + f
                    r = rows_of(f)
                    act.wait_ge(s["hidden"], n + 1)
                    wait(act, s["down_done"], TT * b)
                    act.activation(hh[0:r, f], hf[0:r, f % 2], ACT.Copy).then_inc(s["h_hi"], 1)

                def evict(b, t):
                    y = TT * b + t
                    act.wait_ge(s["down_done"], y + 1)
                    wait(act, s[f"y_out{t % 2}"], 16 * (2 * b + t // 2))
                    act.activation(y_sb[:, t % 2], ps_y[:, t % 2], ACT.Copy).then_inc(s["y_evicted"], 1)

                def sum_abs(m):
                    act.wait_ge(s[f"raw_in{m % 2}"], 16 * (m // 2 + 1))
                    wait(act, s["abs_summed"], m)
                    act.activation(junk2[:], raw[:, m % 2], ACT.Abs, accum_out=abs_sum[:, m:m + 1]).then_inc(s["abs_summed"], 1)

                prep_act(act, 0)
                prep_act(act, 1)
                for b in range(B + 1):
                    for c in range(CK):
                        if b == 2 and c == 0:
                            act.wait_ge(s["abs_summed"], NW)
                        if b < B:
                            x_hi(b, c)
                        if CK * b + c + 2 < NUNIT:
                            prep_act(act, CK * b + c + 2)
                        if b == 1:
                            sum_abs(4 * c)
                            sum_abs(4 * c + 1)
                        for n in range(cut[c], cut[c + 1]) if b == 0 else ():
                            _, hi, _, rows, cols = pieces[n]
                            act.wait_ge(s[f"piece_in{n % 4}"], 16 * (n // 4 + 1))
                            act.activation(hi, stage[0:rows, n % 4, 0:cols], ACT.Copy).then_inc(s["piece_hi"], 1)
                        for f in tiles_of(b, c):
                            tanh(b - 1, f)
                        for f in tiles_of(b, c):
                            h_hi(b - 1, f)
                        if b == 1:
                            sum_abs(4 * c + 2)
                            sum_abs(4 * c + 3)
                        if b == B - 1 and c == CK - 1:
                            act.wait_ge(s["centred"], 1)
                            act.activation(probs[:], probs[:], ACT.Exp).then_inc(s["exped"], 1)
                        if b and c == CK - 1:
                            for t in range(TT):
                                evict(b - 1, t)

            @block.vector
            def _(dve):
                def hidden(b, f):
                    n = SFT * b + f
                    r = rows_of(f)
                    dve.wait_ge(s["tanh"], n + 1)
                    dve.scalar_tensor_tensor(out=th[0:r, f % 2], in0=th[0:r, f % 2], scalar=1.0, in1=ps_u[0:r, f % 2, 0],
                                             op0=ALU.add, op1=ALU.mult).then_inc(s["silu"], 1)
                    dve.wait_ge(s["silu"], n + 1)
                    wait(dve, s["h_lo"], n - 1)
                    dve.scalar_tensor_tensor(out=hf[0:r, f % 2], in0=th[0:r, f % 2], scalar=0.5, in1=ps_u[0:r, f % 2, 1],
                                             op0=ALU.mult, op1=ALU.mult).then_inc(s["hidden"], 1)

                done = [0]

                def step(ins):
                    ins.then_inc(s["route"], 1)
                    done[0] += 1
                    dve.wait_ge(s["route"], done[0])

                def over_experts(v):
                    return v.unsqueeze(2).to_broadcast([P, NT, E])

                def over_tiles(v):
                    return v.unsqueeze(1).to_broadcast([P, NT, E])

                def choose():
                    step(dve.tensor_reduce(top_[:], probs[:], AX_X, ALU.max))
                    dve.tensor_tensor(probs[:], probs[:], over_experts(top_[:]), ALU.subtract).then_inc(s["centred"], 1)
                    dve.wait_ge(s["exped"], 1)
                    step(dve.tensor_reduce(top_[:], probs[:], AX_X, ALU.add))
                    step(dve.reciprocal(top_[:], top_[:]))
                    step(dve.tensor_tensor(probs[:], probs[:], over_experts(top_[:]), ALU.mult))
                    dve.wait_ge(s["tables"], 5)
                    for k in range(TOPK):
                        step(dve.tensor_reduce(weight[:, k], probs[:], AX_X, ALU.max))
                        step(dve.tensor_tensor(cand[:], probs[:], over_experts(weight[:, k]), ALU.is_equal))
                        step(dve.tensor_tensor(cand[:], cand[:], over_tiles(index16[:]), ALU.mult))
                        step(dve.tensor_reduce(top_[:], cand[:], AX_X, ALU.min))
                        step(dve.tensor_tensor(chosen[:, k], over_tiles(index16[:]), over_experts(top_[:]), ALU.is_equal))
                        if k == 0:
                            step(dve.scalar_tensor_tensor(out=probs[:], in0=chosen[:, k], scalar=-2.0, in1=probs[:],
                                                          op0=ALU.mult, op1=ALU.add))
                    dve.tensor_tensor(mask[:], chosen[:, 0], chosen[:, 1], ALU.add).then_inc(s["mask"], 1)

                def place_rows():
                    dve.wait_ge(s["ranked"], 1)
                    step(dve.tensor_copy(count[:], ps_l[:, 0:E]))
                    step(dve.tensor_tensor(many[:], count[:].unsqueeze(2).to_broadcast([P, E, NT]),
                                           full[:].unsqueeze(1).to_broadcast([P, E, NT]), ALU.is_gt))
                    step(dve.tensor_reduce(blocks[:], many[:], AX_X, ALU.add))
                    step(dve.tensor_tensor_scan(ends[:], ones[:, 0:E], blocks[:], 0.0, ALU.mult, ALU.add))
                    step(dve.tensor_tensor(first_[:], ends[:], blocks[:], ALU.subtract))
                    step(dve.tensor_scalar(first_[:], first_[:], float(P), None, ALU.mult))
                    step(dve.tensor_tensor(rank[:], ps_r, over_tiles(first_[:]), ALU.add))
                    for k in range(TOPK):
                        step(dve.tensor_tensor(cand[:], chosen[:, k], rank[:], ALU.mult))
                        step(dve.tensor_reduce(slotf[:, k], cand[:], AX_X, ALU.add))
                    dve.tensor_copy(slot[:], slotf[:]).then_inc(s["slots"], 1)
                    step(dve.tensor_tensor(past[:], ends[0:1].unsqueeze(1).to_broadcast([1, NBLK + 1, E]),
                                           block_no[:].unsqueeze(2).to_broadcast([1, NBLK + 1, E]), ALU.is_le))
                    step(dve.tensor_reduce(owner[:], past[:], AX_X, ALU.add))
                    step(dve.tensor_scalar(owner[:], owner[:], float(E - 1), None, ALU.min))
                    step(dve.tensor_copy(block_expert[:], owner[:]))
                    dve.memset(change[:, 0:1], 0.0).then_inc(s["change0"], 1)
                    step(dve.tensor_tensor(change[:, 1:], owner[:, 1:], owner[:, 0:NBLK], ALU.is_gt))
                    dve.wait_ge(s["change0"], 1)
                    step(dve.tensor_tensor_scan(changes[:], ones[0:1, 0:NBLK + 1], change[:], 0.0, ALU.mult, ALU.add))
                    step(dve.tensor_copy(fresh[:], change[:]))
                    step(dve.tensor_copy(turn[:], changes[:]))
                    step(dve.tensor_scalar(turn_before[:], changes[:], -1.0, 0.0, ALU.add, ALU.max))

                    step(dve.tensor_reduce(wtotal[:], ps_l[:, 64:64 + NW].rearrange("p (l n) -> p l n", l=2), AX_X, ALU.add))
                    step(dve.tensor_scalar(wscale[:], wtotal[:], 1.0 / (C * INNER), 1e-5, ALU.mult, ALU.max))
                    step(dve.reciprocal(wmean[:], wscale[:]))
                    step(dve.tensor_copy(winv[:], wmean[:].unsqueeze(2).to_broadcast([P, 2, NPIECE])))

                prep_dve(dve, 0)
                prep_dve(dve, 1)
                mix_dve(dve, 0)
                for b in range(B + 1):
                    for c in range(CK):
                        u = CK * b + c
                        if u + 2 < NUNIT:
                            prep_dve(dve, u + 2)
                        if u + 1 < NUNIT:
                            mix_dve(dve, u + 1)
                        for f in tiles_of(b, c):
                            hidden(b - 1, f)
                        if c == CK - 1 and b < B:
                            dve.wait_ge(s["mixed_read"], u + 1)
                            dve.tensor_copy(probs[:, TT * b:TT * (b + 1), :], ps_lg).then_inc(s["logits_read"], 1)
                        if b == B - 1 and c == CK - 1:
                            dve.wait_ge(s["logits_read"], B)
                            choose()
                            place_rows()

            @block.tensor
            def _(pe):
                def turn(b, c):
                    u = CK * b + c
                    m = mixed[:, c % 2]
                    pe.wait_ge(s["mixed_ready"], u + 1)
                    wait(pe, s["tok_ready"], u)
                    for t in range(TT):
                        last = pe.transpose(ps_t[:, t], m[:, t * P:(t + 1) * P], ident[:])
                    last.then_inc(s["turned"], 1)
                    if c == 0:
                        wait(pe, s["logits_read"], b)
                    for t in range(TT):
                        last = pe.matmul(ps_lg[:, t], m[:, t * P:(t + 1) * P], gate_sb[:, c], start=(c == 0 and t == 0),
                                         stop=(c == CK - 1 and t == TT - 1), skip_group_check=True)
                    last.then_inc(s["mixed_read"], 1)

                def up(b, f):
                    n = SFT * b + f
                    r = rows_of(f)
                    wait(pe, s["hidden"], n - 1)
                    if f == 0:
                        pe.wait_ge(s["x_lo"], CK * (b + 1))
                    for w in range(2):
                        for c in range(CK):
                            hi, lo = s13h[:, w, c, f * P:f * P + r], s13l[:, w, c, f * P:f * P + r]
                            for i, (l_, r_) in enumerate(((hi, xh), (hi, xl), (lo, xh))):
                                last = pe.matmul(ps_u[0:r, f % 2, w], l_, r_[:, b % 2, c], start=(c == 0 and i == 0),
                                                 stop=(c == CK - 1 and i == 2))
                    last.then_inc(s["up_done"], 1)

                def down(b, t):
                    y = TT * b + t
                    wait(pe, s["y_evicted"], y - 1)
                    for f in range(SFT):
                        if t == 0:
                            pe.wait_ge(s["h_lo"], SFT * b + f + 1)
                        r = rows_of(f)
                        hi, lo = hh[0:r, f, t * P:(t + 1) * P], hl[0:r, f, t * P:(t + 1) * P]
                        for i, (l_, r_) in enumerate(((hi, s2h[0:r, f]), (hi, s2l[0:r, f]), (lo, s2h[0:r, f]))):
                            last = pe.matmul(ps_y[:, t % 2], l_, r_, start=(f == 0 and i == 0),
                                             stop=(f == SFT - 1 and i == 2))
                    last.then_inc(s["down_done"], 1)

                def count():
                    pe.wait_ge(s["tok_ready"], NUNIT)
                    pe.wait_ge(s["logits_read"], B)
                    pe.wait_ge(s["tables"], 2)
                    pe.wait_ge(s["mask"], 1)
                    pe.wait_ge(s["abs_summed"], NW)
                    pe.matmul(ps_l[:, 64:64 + NW], ones[:], abs_sum, start=True, stop=True)
                    pe.matmul(ps_r, below[:], mask[:], start=True, stop=False, skip_group_check=True)
                    for t in range(NT - 1):
                        last = pe.matmul(ps_r[:, t + 1:NT], ones_b[:], mask[:, t].unsqueeze(1).to_broadcast([P, NT - 1 - t, E]),
                                         start=False, stop=t == NT - 2, skip_group_check=True)
                    for t in range(NT):
                        last = pe.matmul(ps_l[:, 0:E], ones_b[:], mask[:, t], start=t == 0, stop=t == NT - 1)
                    last.then_inc(s["ranked"], 1)

                pe.wait_ge(s["gate_in"], 16)
                for b in range(B + 1):
                    for c in range(CK):
                        if b < B:
                            turn(b, c)
                        if b == 1 and c == 0:
                            pe.wait_ge(s["piece_lo"], len(pieces))
                        for f in tiles_of(b, c):
                            up(b - 1, f)
                        if b and c == CK - 1:
                            for t in range(TT):
                                down(b - 1, t)
                                if b == B - 1 and t == 1:
                                    count()

        with ExitStack() as st:
            shared_out = [s["y_out0"], s["y_out1"]]
            s = Sems("e")
            NU, ND = CK, FT
            NV = 2
            NG = NU - NV + ND
            PER = 3
            (wuh, wul, wdh, wdl), end = place(A, [
                ("wuh", [P, 2, CK, 2 * F], F32R), ("wul", [P, 2, CK, 2 * F], F32R),
                ("wdh", [P, 2, FT, C], F32R), ("wdl", [P, 2, FT, C], F32R)])
            assert end <= Bx
            (rawu, rawd, rows_in, hid, gatev, ah, al, bh, bl, ev, uv, fw, bw, piece0), end = place(Ch, [
                ("rawu", [P, CK, 2 * F], F32), ("rawd", [P, FT, C], F32), ("rows_in", [P, 2, C], F32),
                ("hid", [P, FT * P], F32), ("gatev", [P, F], F32),
                ("ah", [P, 2, CK, P], F32R), ("al", [P, 2, CK, P], F32R),
                ("bh", [P, FT, P], F32R), ("bl", [P, FT, P], F32R),
                ("ev1", [P, 2, T], F32),
                ("uv1", [P, 2, T], F32),
                ("fw1", [P, 2, T], F32), ("bw1", [P, 2, T], F32),
                ("piece0", [P, PIECE], F32)])
            assert end <= W, (end, W)
            (k_in, piece1), end = place(W + 32768, [("k_in1", [P, 2, T], F32), ("piece1", [P, PIECE], F32)])
            piece = (piece0, piece1)
            assert end <= Y
            ps_x = st.enter_context(nc.psum_tensor("ps_x", [P, CK, P], F32))
            ps_h = st.enter_context(nc.psum_tensor("ps_h", [P, 4, P], F32))
            ps_1 = st.enter_context(nc.psum_tensor("ps_1", [P, 512], F32))
            ps_3 = st.enter_context(nc.psum_tensor("ps_3", [P, 512], F32))
            ps_o = st.enter_context(nc.psum_tensor("ps_o", [P, 2, C], F32))
            block = st.enter_context(nc.Block())
            decay1 = decay[:, 1].rearrange("p b c -> p (b c)")
            out1 = unit_out[:].rearrange("p b c -> p (b c)")
            u1 = unit_u[:].rearrange("p b c -> p (b c)")
            winv1 = winv[:].rearrange("p l n -> p (l n)")
            assert NW == NUNIT
            k_units = kT.rearrange("b c p t -> (b c) p t")
            assert PER * NUNIT >= NBLK > PER * (NUNIT - 1)

            def rows(j):
                return min(P, F - j * P)

            def every_block(eng, body):
                R = 2 * PER
                for i in range(R):
                    body(i, i % 2, i // PER, i % PER)
                with eng.Fori(1, NBLK // R) as j:
                    for i in range(R):
                        body(R * j + i, i % 2, 2 * j + i // PER, i % PER)
                for i in range(R * (NBLK // R), NBLK):
                    body(i, i % 2, i // PER, i % PER)

            def is_first(i):
                return type(i) is int and i == 0

            def is_last(i):
                return type(i) is int and i == NBLK - 1

            def lo_count(n, j):
                return (s["vec_lo"], NV * n + j + 1) if j < NV else (s["pool_lo"], NG * n + j - NV + 1)

            def buffer(t, n, j):
                return t[:, ds(n % 2), j].rearrange("p a n -> p (a n)")

            def when_fresh(eng, i, turns, load_):
                changed = eng.value_load(fresh[0:1, ds(i)], min_val=0, max_val=1)
                with eng.If(changed > 0):
                    load_(i, eng.value_load(turns[0:1, ds(i)], min_val=0, max_val=E - 1))

            @block.sync
            def _(sp):
                def weights(i, before):
                    e = sp.value_load(block_expert[0:1, ds(i)], min_val=0, max_val=E - 1)
                    for j in range(NU):
                        if not is_first(i):
                            sp.wait_ge(*lo_count(before, j))
                        sp.dma_start(rawu[:, j], w13[ds(e), j].rearrange("a p n -> p (a n)")).then_inc(s[f"wu_in{j}"], 16)
                    for j in range(ND):
                        if not is_first(i):
                            sp.wait_ge(s["pool_lo"], NG * before + NU - NV + j + 1)
                        sp.dma_start(rawd[0:rows(j), j], w2[ds(e), j * P:j * P + rows(j)].rearrange("a p n -> p (a n)")).then_inc(s[f"wd_in{j}"], 16)

                def rows_load(i, p, first):
                    if not first:
                        sp.wait_ge(s["x_turned"], i - 1)
                    sp.dma_start(rows_in[:, p], xslots[ds(i * P, P)]).then_inc(s[f"rows_in{p}"], 16)

                def k_load(u, p, first):
                    if not first:
                        sp.wait_ge(s["uv_ready"], u - 1)
                    sp.dma_start(k_in[:, p], k_units[ds(u)].rearrange("a p t -> p (a t)")).then_inc(s[f"k_in{p}"], 16)

                def piece_load(m, p, first):
                    if not first:
                        sp.wait_ge(s["ternary"], m - 1)
                    sp.dma_start(piece[p][:], wp[ds(m)].rearrange("a p n -> p (a n)")).then_inc(s[f"w_in{p}"], 16)

                def store(i, p):
                    sp.wait_ge(s["y_evicted"], i + 1)
                    sp.dma_start(yslots[ds(i * P, P)], y_sb[:, p]).then_inc(s[f"y_out{p}"], 16)

                def body(i, p, u, part):
                    ahead = not (type(i) is int and i >= NBLK - 2)
                    if ahead:
                        rows_load(i + 2, p, False)
                    if not (type(i) is int and i < 2):
                        store(i - 2, p)
                    if part == 0 and (type(u) is not int or 1 <= u < NUNIT - 1):
                        k_load(u + 1, (p + 1) % 2, False)
                        piece_load(u + 1, (p + 1) % 2, False)
                    if ahead:
                        when_fresh(sp, i + 2, turn_before, weights)

                for p in range(2):
                    rows_load(p, p, True)
                weights(0, 0)
                for p in range(2):
                    k_load(p, p, True)
                    piece_load(p, p, True)
                when_fresh(sp, 1, turn_before, weights)
                every_block(sp, body)
                for i in (NBLK - 2, NBLK - 1):
                    store(i, i % 2)
                sp.wait_ge(s["y_out0"], 16 * ((NBLK + 1) // 2))
                sp.wait_ge(s["y_out1"], 16 * (NBLK // 2))

            @block.gpsimd
            def _(pool):
                def split(i, n):
                    for j in range(NV, NU):
                        pool.wait_ge(s["wu_hi"], NU * n + j + 1)
                        pool.tensor_tensor(buffer(wul, n, j), rawu[:, j], f32(buffer(wuh, n, j)), ALU.subtract).then_inc(s["pool_lo"], 1)
                    for j in range(ND):
                        r = rows(j)
                        pool.wait_ge(s["wd_hi"], ND * n + j + 1)
                        pool.tensor_tensor(buffer(wdl, n, j)[0:r], rawd[0:r, j], f32(buffer(wdh, n, j)[0:r]), ALU.subtract).then_inc(s["pool_lo"], 1)

                split(0, 0)
                with pool.Fori(1, NBLK) as i:
                    when_fresh(pool, i, turn, split)

            @block.scalar
            def _(act):
                def exps(u):
                    act.wait_ge(s["clipped"], 2 * u + 1)
                    act.activation(ev[:, 1], ev[:, 1], ACT.Exp).then_inc(s["exped"], 1)
                    act.wait_ge(s["clipped"], 2 * u + 2)
                    act.activation(uv[:, 1], uv[:, 1], ACT.Exp).then_inc(s["exped"], 1)

                def a_hi(i, p, two_before):
                    act.wait_ge(s["x_turned"], i + 1)
                    if two_before:
                        act.wait_ge(s["up_done"], i)
                    act.activation(ah[:, p], ps_x[:], ACT.Copy).then_inc(s["a_hi"], 1)

                def b_hi(i):
                    act.wait_ge(s["h_turned"], i + 1)
                    if not is_first(i):
                        act.wait_ge(s["down_done"], i + 1)
                    act.activation(bh[:], ps_h[:, 0:FT], ACT.Copy).then_inc(s["b_hi"], 1)

                def evict(i, p):
                    act.wait_ge(s["down_done"], i + 2)
                    if type(i) is not int or i >= 2:
                        act.wait_ge(s[f"y_out{p}"], 8 * (i - p))
                    else:
                        act.wait_ge(shared_out[p], 16 * NT // 2)
                    act.activation(y_sb[:, p], ps_o[:, p], ACT.Copy).then_inc(s["y_evicted"], 1)

                def split_up(i, n):
                    for j in range(NU):
                        act.wait_ge(s[f"wu_in{j}"], 16 * (n + 1))
                        if j == 0 and not is_first(i):
                            act.wait_ge(s["up_done"], i)
                        act.activation(buffer(wuh, n, j), rawu[:, j], ACT.Copy).then_inc(s["wu_hi"], 1)

                def split_down(i, n):
                    for j in range(ND):
                        r = rows(j)
                        act.wait_ge(s[f"wd_in{j}"], 16 * (n + 1))
                        if j == 0 and not is_first(i):
                            act.wait_ge(s["down_done"], i)
                        act.activation(buffer(wdh, n, j)[0:r], rawd[0:r, j], ACT.Copy).then_inc(s["wd_hi"], 1)

                def body(i, p, u, part):
                    if not is_last(i):
                        changed = act.value_load(fresh[0:1, ds(i + 1)], min_val=0, max_val=1)
                        n = act.value_load(turn[0:1, ds(i + 1)], min_val=0, max_val=E - 1)
                    if not is_first(i):
                        b_hi(i - 1)
                    if not is_last(i):
                        a_hi(i + 1, 1 - p, not is_first(i))
                        with act.If(changed > 0):
                            split_up(i + 1, n)
                    if part == PER - 1:
                        act.wait_ge(s["rounded"], u + 1)
                    act.wait_ge(s["up_done"], i + 2)
                    act.activation(gatev[:], ps_1[:, 0:F], ACT.Tanh, scale=0.5).then_inc(s["tanh"], 1)
                    if not is_first(i):
                        evict(i - 1, 1 - p)
                    if not is_last(i):
                        with act.If(changed > 0):
                            split_down(i + 1, n)
                    if part == PER - 1:
                        ternary(u, part_parity(p, part))
                        exps(u + 1)

                def ternary(m, p):
                    act.activation(wq[:, ds(m)].rearrange("p a n -> p (a n)"), piece[p][:], ACT.Copy,
                                   bias=-ROUND).then_inc(s["ternary"], 1)

                def part_parity(p, part):
                    return (p - part) % 2

                a_hi(0, 0, False)
                split_up(0, 0)
                split_down(0, 0)
                exps(0)
                every_block(act, body)
                b_hi(NBLK - 1)
                act.wait_ge(s["rounded"], NW)
                ternary(NW - 1, (NW - 1) % 2)
                evict(NBLK - 1, (NBLK - 1) % 2)

            @block.vector
            def _(dve):
                def a_lo(i, p):
                    dve.wait_ge(s["a_hi"], i + 1)
                    dve.tensor_tensor(al[:, p], ps_x[:], f32(ah[:, p]), ALU.subtract).then_inc(s["a_lo"], 1)

                def b_lo(i):
                    dve.wait_ge(s["b_hi"], i + 1)
                    dve.tensor_tensor(bl[:], ps_h[:, 0:FT], f32(bh[:]), ALU.subtract).then_inc(s["b_lo"], 1)

                def hidden(i):
                    dve.wait_ge(s["tanh"], i + 1)
                    dve.scalar_tensor_tensor(out=gatev[:], in0=gatev[:], scalar=1.0, in1=ps_1[:, 0:F],
                                             op0=ALU.add, op1=ALU.mult).then_inc(s["silu"], 1)
                    dve.wait_ge(s["silu"], i + 1)
                    if not is_first(i):
                        dve.wait_ge(s["h_turned"], i)
                    dve.scalar_tensor_tensor(out=hid[:, 0:F], in0=gatev[:], scalar=0.5, in1=ps_3[:, 0:F],
                                             op0=ALU.mult, op1=ALU.mult).then_inc(s["hidden"], 1)

                def w_lo(i, n):
                    for j in range(NV):
                        dve.wait_ge(s["wu_hi"], NU * n + j + 1)
                        dve.tensor_tensor(buffer(wul, n, j), rawu[:, j], f32(buffer(wuh, n, j)), ALU.subtract).then_inc(s["vec_lo"], 1)

                STEPS = 8

                def clip(u, p):
                    if not is_first(u):
                        dve.wait_ge(s["step"], STEPS * (u - 1) + 6)
                    dve.wait_ge(s[f"k_in{p}"], 8 * (u - p) + 16)
                    dve.tensor_scalar(ev[:, 1], k_in[:, p], 30.0, None, ALU.min).then_inc(s["clipped"], 1)
                    dve.tensor_scalar(uv[:, 1], k_in[:, p], u1[:, ds(u)], 30.0, ALU.add, ALU.min).then_inc(s["clipped"], 1)

                def scan(u, to, j, back):
                    d = decay1[:, ds(u)].to_broadcast([P, T])
                    o, i_ = (to[:, j, ::-1], ev[:, j, ::-1]) if back else (to[:, j], ev[:, j])
                    dve.tensor_tensor_scan(o, d, i_, 0.0, ALU.mult, ALU.add).then_inc(s["step"], 1)

                def finish(u):
                    dve.wait_ge(s["step"], STEPS * u + 8)
                    dve.scalar_tensor_tensor(out=ratio[:, ds(u)].rearrange("p a t -> p (a t)"), in0=fw[:, 0],
                                             scalar=out1[:, ds(u)], in1=fw[:, 1],
                                             op0=ALU.mult, op1=ALU.mult).then_inc(s["ratio"], 1)

                def early(u, p, part):
                    if part == 0:
                        if not is_first(u):
                            finish(u - 1)
                        dve.wait_ge(s["exped"], 2 * u + 1)
                        dve.tensor_tensor(ev[:, 0], ev[:, 1], k_in[:, p], ALU.mult).then_inc(s["ev_ready"], 1)
                    if part == 1:
                        dve.wait_ge(s["step"], STEPS * u + 4)
                        dve.scalar_tensor_tensor(out=fw[:, :, 0:T - 1], in0=bw[:, :, 1:T], scalar=decay1[:, ds(u)],
                                                 in1=fw[:, :, 0:T - 1], op0=ALU.mult, op1=ALU.add).then_inc(s["step"], 1)
                        dve.wait_ge(s[f"w_in{p}"], 8 * (u - p) + 16)
                        dve.tensor_scalar(piece[p][:], piece[p][:], winv1[:, ds(u)], -1.0, ALU.mult, ALU.max).then_inc(s["scaled"], 1)
                    if part == 2:
                        dve.wait_ge(s["scaled"], u + 1)
                        dve.tensor_scalar(piece[p][:], piece[p][:], 1.0, ROUND, ALU.min, ALU.add).then_inc(s["rounded"], 1)
                        if type(u) is not int or u < NUNIT - 1:
                            clip(u + 1, 1 - p)

                def late(u, p, part):
                    if part == 0:
                        if not is_first(u):
                            dve.wait_ge(s["ratio"], u)
                        dve.wait_ge(s["ev_ready"], u + 1)
                        for to, back in ((fw, False), (bw, True)):
                            for j in range(2):
                                scan(u, to, j, back)
                    if part == 1:
                        dve.wait_ge(s["exped"], 2 * u + 2)
                        dve.tensor_tensor(uv[:, 0], uv[:, 1], k_in[:, p], ALU.mult).then_inc(s["uv_ready"], 1)
                        dve.wait_ge(s["uv_ready"], u + 1)
                        dve.wait_ge(s["step"], STEPS * u + 5)
                        dve.tensor_tensor(fw[:], fw[:], uv[:], ALU.add).then_inc(s["step"], 1)
                        dve.wait_ge(s["step"], STEPS * u + 6)
                        dve.tensor_scalar(fw[:, 1], fw[:, 1], 1e-8, None, ALU.max).then_inc(s["step"], 1)
                    if part == 2:
                        dve.wait_ge(s["step"], STEPS * u + 7)
                        dve.reciprocal(fw[:, 1], fw[:, 1]).then_inc(s["step"], 1)

                def body(i, p, u, part):
                    pu = (p - part) % 2
                    if not is_last(i):
                        changed = dve.value_load(fresh[0:1, ds(i + 1)], min_val=0, max_val=1)
                        n = dve.value_load(turn[0:1, ds(i + 1)], min_val=0, max_val=E - 1)
                    if not is_first(i):
                        b_lo(i - 1)
                    if not is_last(i):
                        a_lo(i + 1, 1 - p)
                        with dve.If(changed > 0):
                            w_lo(i + 1, n)
                    early(u, pu, part)
                    hidden(i)
                    late(u, pu, part)

                dve.memset(hid[:, F:FT * P], 0.0).then_inc(s["up_done"], 1)
                dve.memset(hid[:, 0:F], 0.0).then_inc(s["down_done"], 1)
                a_lo(0, 0)
                w_lo(0, 0)
                clip(0, 0)
                every_block(dve, body)
                b_lo(NBLK - 1)
                early(NUNIT - 1, (NUNIT - 1) % 2, PER - 1)
                late(NUNIT - 1, (NUNIT - 1) % 2, PER - 1)
                finish(NUNIT - 1)

            @block.tensor
            def _(pe):
                def turn_x(i, p):
                    pe.wait_ge(s[f"rows_in{p}"], 8 * (i - p) + 16)
                    if not is_first(i):
                        pe.wait_ge(s["a_lo"], i)
                    for c in range(CK):
                        last = pe.transpose(ps_x[:, c], rows_in[:, p, c * P:(c + 1) * P], ident[:])
                    last.then_inc(s["x_turned"], 1)

                def turn_h(i):
                    pe.wait_ge(s["hidden"], i + 1)
                    if not is_first(i):
                        pe.wait_ge(s["b_lo"], i)
                    for f in range(FT):
                        last = pe.transpose(ps_h[:, f], hid[:, f * P:(f + 1) * P], ident[:])
                    last.then_inc(s["h_turned"], 1)

                def up(i, p, n):
                    pe.wait_ge(s["a_lo"], i + 1)
                    for c in range(CK):
                        pe.wait_ge(*lo_count(n, c))
                        for w, ps in enumerate((ps_1, ps_3)):
                            hi, lo = (buffer(v, n, c)[:, w * F:(w + 1) * F] for v in (wuh, wul))
                            for k, (l_, r_) in enumerate(((ah, hi), (ah, lo), (al, hi))):
                                last = pe.matmul(ps[:, 0:F], l_[:, p, c], r_, start=(c == 0 and k == 0),
                                                 stop=(c == CK - 1 and k == 2))
                    last.then_inc(s["up_done"], 1)

                def down(i, p, n):
                    pe.wait_ge(s["b_lo"], i + 1)
                    pe.wait_ge(s["pool_lo"], NG * n + NG)
                    if type(i) is not int or i >= 2:
                        pe.wait_ge(s["y_evicted"], i - 1)
                    for f in range(FT):
                        r = rows(f)
                        hi, lo = (buffer(v, n, f)[0:r] for v in (wdh, wdl))
                        for k, (l_, r_) in enumerate(((bh, hi), (bh, lo), (bl, hi))):
                            last = pe.matmul(ps_o[:, p], l_[0:r, f], r_, start=(f == 0 and k == 0),
                                             stop=(f == FT - 1 and k == 2))
                    last.then_inc(s["down_done"], 1)

                def turn_of(i):
                    return pe.value_load(turn[0:1, ds(i)], min_val=0, max_val=E - 1)

                def body(i, p, u, part):
                    n = turn_of(i)
                    if not is_first(i):
                        n_before = turn_of(i - 1)
                    if not is_last(i):
                        turn_x(i + 1, 1 - p)
                    if not is_first(i):
                        turn_h(i - 1)
                    up(i, p, n)
                    if not is_first(i):
                        down(i - 1, 1 - p, n_before)

                pe.wait_ge(s["up_done"], 1)
                turn_x(0, 0)
                every_block(pe, body)
                turn_h(NBLK - 1)
                down(NBLK - 1, (NBLK - 1) % 2, turn_of(NBLK - 1))


        (x1, z1), end = place(A, [("x1", [P, NT, C], F32), ("z1", [P, NT, C], F32)])
        assert end <= Bx
        (alpha, quant1, ssq, amax1, half, minus1, consts, halfalpha, ident_b), _ = place(Y, [
            ("alpha", [P, NT], F32), ("quant1", [P, NT], F32), ("ssq", [P, NT], F32),
            ("amax1", [P, NT], F32), ("half", [P, NT], F32), ("minus1", [P, NT], F32),
            ("consts", [P, 6], F32), ("halfalpha", [P, NT], F32), ("ident_b", [P, P], BF16)])
        big, end = place(Bx, [
            ("lng_sb", [P, INNER], F32), ("lnb_sb", [P, INNER], F32), ("b2_sb", [P, C], F32),
            ("pre", [P, INNER], F32), ("hid5", [P, 2, INNER], F32),
            ("moved", [P, INNER], F32), ("junk", [P, INNER], BF16), ("hq", [P, INNER], BF16),
            ("hqT", [P, IK, P], BF16), ("moved1", [P, C], F32), ("xq", [P, C], BF16),
            ("xqT", [P, 2, CK, P], BF16), ("out_sb", [P, 2, C], F32), ("arow", [BR, 2, P], F32R),
            ("arows", [BR, NT, P], F32R), ("brow", [BR, INNER], F32R)])
        lng_sb, lnb_sb, b2_sb, pre, hid5, moved, junk, hq, hqT, moved1, xq, xqT, out_sb, arow, arows, brow = big
        assert end <= W, (end, W)
        with ExitStack() as st:
            s = Sems("g")
            (ya, yb, ysh, xin, sig), end = place(Ch, [
                ("ya", [P, 2, C], F32), ("yb", [P, 2, C], F32), ("ysh", [P, 2, C], F32),
                ("xin", [P, 2, C], F32), ("sig", [P, 2, C], F32)])
            assert end <= D
            (square, inv, rstd1, ia, ia_hi, winv1, acols), end = place(D, [
                ("square", [P, C], F32), ("inv", [P, NT], F32), ("rstd1", [P, NT], F32), ("ia", [P, NT], F32),
                ("ia_hi", [P, NT], F32R), ("winv1", [P, 1], F32), ("acols", [P, NT, BR], F32)])
            assert end <= Bx + (W - Bx) - 4 * (NT * P + INNER), "free of arows and brow"
            braw = at("braw", [BR, INNER], F32, W + 32768)
            ps_r = st.enter_context(nc.psum_tensor("ps_r4", [P, 2, CK, P], F32))
            ps_a = st.enter_context(nc.psum_tensor("ps_a", [BR, NT, P], F32))
            PARTS = (slice(0, NT - 4), slice(NT - 4, NT))
            block = st.enter_context(nc.Block())

            @block.sync
            def _(sp):
                for t in range(NT):
                    p = t % 2
                    if t >= 2:
                        sp.wait_ge(s[f"x_and_shared{p}"], t // 2)
                    if t == 4:
                        sp.wait_ge(s["filled"], 2)
                        for r in (0, 32, 64):
                            sp.dma_start(braw[r:r + 1], b1).then_inc(s["b_in"], 16)
                    sp.dma_start(ysh[:, p], yshared[t]).then_inc(s[f"rows_in{p}"], 16)
                    sp.dma_start(xin[:, p], x[t]).then_inc(s[f"rows_in{p}"], 16)

            @block.gpsimd
            def _(pool):
                for t in range(NT):
                    p = t % 2
                    if t >= 2:
                        pool.wait_ge(s["summed"], 2 * (t - 1))
                    for k, dst in enumerate((ya, yb)):
                        pool.indirect_dma_start(dst[:, p], None, yslots, bass.IndirectOffsetOnAxis(
                            ap=slot[:, k, t:t + 1], axis=0)).then_inc(s[f"gathered{p}"], 16)
                    if p == 0:
                        pool.wait_ge(s["rows_in0"], 32 * (t // 2 + 1))
                        pool.tensor_tensor(x1[:, t], xin[:, 0], ysh[:, 0], ALU.add).then_inc(s["x_and_shared0"], 1)
                    if t == 1:
                        pool.memset(half[:], -0.5).then_inc(s["filled"], 1)
                        pool.memset(braw[:], 0.0).then_inc(s["filled"], 1)
                    if t == 2:
                        pool.memset(acols[:], 0.0).then_inc(s["filled"], 1)
                    if t == 3:
                        pool.tensor_copy(ident_b[:], ident[:]).then_inc(s["filled"], 1)
                pool.wait_ge(s["filled"], 1)
                for n, v in enumerate(PARTS):
                    pool.wait_ge(s["mean_square"], n + 1)
                    pool.tensor_tensor(rstd1[:, v], ssq[:, v], half[:, v], ALU.pow).then_inc(s["rstd"], 1)

            @block.tensor
            def _(pe):
                for t in range(NT):
                    wait(pe, s["mixed"], t - 1)
                    for c in range(CK):
                        last = pe.transpose(ps_r[:, t % 2, c], ratio[:, CK * (t // TT) + c, (t % TT) * P:(t % TT + 1) * P], ident[:])
                    last.then_inc(s["ratio_turned"], 1)
                for n, v in enumerate(PARTS):
                    pe.wait_ge(s["acols"], 3 * n + 3)
                    for t in range(v.start, v.stop):
                        last = pe.transpose(ps_a[:, t], acols[:, t], ident[:])
                    last.then_inc(s["a_turned"], 1)

            @block.scalar
            def _(act):
                for t in range(NT):
                    p = t % 2
                    act.wait_ge(s["summed"], 2 * t + 2)
                    wait(act, s["mixed"], t - 1)
                    act.activation(sig[:, p], x1[:, t], ACT.Sigmoid).then_inc(s["sigmoid"], 1)
                    if t == 8:
                        act.wait_ge(s["b_in"], 48)
                        act.activation(brow[:], braw[:], ACT.Copy).then_inc(s["brow"], 1)
                    if t:
                        act.wait_ge(s["mixed"], t)
                        wait(act, s["squared"], t - 1)
                        act.activation(square[:], z1[:, t - 1], ACT.Square, accum_out=ssq[:, t - 1:t]).then_inc(s["squared"], 1)
                act.wait_ge(s["mixed"], NT)
                act.wait_ge(s["squared"], NT - 1)
                act.activation(square[:], z1[:, NT - 1], ACT.Square, accum_out=ssq[:, NT - 1:NT]).then_inc(s["squared"], 1)
                for n, v in enumerate(PARTS):
                    act.wait_ge(s["a_turned"], n + 1)
                    act.activation(arows[:, v], ps_a[:, v], ACT.Copy).then_inc(s["arows"], 1)

            @block.vector
            def _(dve):
                def mix(t):
                    dve.wait_ge(s["sigmoid"], t + 1)
                    dve.wait_ge(s["ratio_turned"], t + 1)
                    dve.tensor_tensor(z1[:, t], sig[:, t % 2], ps_r[:, t % 2].rearrange("p c n -> p (c n)"), ALU.mult).then_inc(s["mixed"], 1)
                    dve.wait_ge(s["mixed"], t + 1)
                    dve.tensor_reduce(amax1[:, t:t + 1], z1[:, t], AX_X, ALU.max, apply_absolute_value=True).then_inc(s["amax"], 1)

                def mean_square(n):
                    v = PARTS[n]
                    dve.wait_ge(s["squared"], v.stop)
                    dve.tensor_scalar(ssq[:, v], ssq[:, v], 1.0 / C, EPS, ALU.mult, ALU.add).then_inc(s["mean_square"], 1)

                def stats(n):
                    v = PARTS[n]
                    dve.wait_ge(s["rstd"], n + 1)
                    dve.wait_ge(s["amax"], v.stop)
                    dve.tensor_tensor(amax1[:, v], amax1[:, v], rstd1[:, v], ALU.mult).then_inc(s["stat"], 1)
                    dve.wait_ge(s["stat"], 6 * n + 1)
                    dve.tensor_scalar(amax1[:, v], amax1[:, v], 1e-5, None, ALU.max).then_inc(s["stat"], 1)
                    dve.wait_ge(s["stat"], 6 * n + 2)
                    dve.reciprocal(inv[:, v], amax1[:, v]).then_inc(s["stat"], 1)
                    dve.tensor_scalar(alpha[:, v], amax1[:, v], wscale[:, 0:1], 1.0 / 127.0, ALU.mult, ALU.mult).then_inc(s["stat"], 1)
                    if n == 0:
                        dve.reciprocal(winv1[:], wscale[:, 0:1]).then_inc(s["winv1"], 1)
                        dve.wait_ge(s["winv1"], 1)
                    dve.wait_ge(s["stat"], 6 * n + 3)
                    dve.tensor_scalar(ia[:, v], inv[:, v], winv1[:], 127.0, ALU.mult, ALU.mult).then_inc(s["ia"], 1)
                    dve.wait_ge(s["ia"], 2 * n + 1)
                    dve.tensor_copy(ia_hi[:, v], ia[:, v]).then_inc(s["ia"], 1)
                    dve.wait_ge(s["ia"], 2 * n + 2)
                    dve.wait_ge(s["filled"], 3)
                    dve.tensor_copy(acols[:, v, 0], f32(ia_hi[:, v])).then_inc(s["acols"], 1)
                    dve.tensor_tensor(acols[:, v, 32], ia[:, v], f32(ia_hi[:, v]), ALU.subtract).then_inc(s["acols"], 1)
                    dve.tensor_copy(acols[:, v, 64], f32(ia_hi[:, v])).then_inc(s["acols"], 1)
                    dve.wait_ge(s["stat"], 6 * n + 4)
                    dve.tensor_scalar(halfalpha[:, v], alpha[:, v], 0.5, None, ALU.mult).then_inc(s["stat"], 1)
                    dve.scalar_tensor_tensor(out=quant1[:, v], in0=inv[:, v], scalar=127.0, in1=rstd1[:, v],
                                             op0=ALU.mult, op1=ALU.mult).then_inc(s["stat"], 1)

                for t in range(NT):
                    p = t % 2
                    if p:
                        dve.wait_ge(s["rows_in1"], 32 * (t // 2 + 1))
                        dve.tensor_tensor(x1[:, t], xin[:, 1], ysh[:, 1], ALU.add).then_inc(s["x_and_shared1"], 1)
                    dve.wait_ge(s[f"x_and_shared{p}"], t // 2 + 1)
                    dve.wait_ge(s[f"gathered{p}"], 32 * (t // 2 + 1))
                    for k, rows_ in enumerate((ya, yb)):
                        wait(dve, s["summed"], 2 * t + k)
                        dve.scalar_tensor_tensor(out=x1[:, t], in0=rows_[:, p], scalar=weight[:, k, t:t + 1], in1=x1[:, t],
                                                 op0=ALU.mult, op1=ALU.add).then_inc(s["summed"], 1)
                    if t:
                        mix(t - 1)
                    if t == NT - 2:
                        mean_square(0)
                    if t == NT - 4:
                        dve.wait_ge(s["brow"], 1)
                        dve.tensor_tensor(brow[64:65], braw[64:65], f32(brow[64:65]), ALU.subtract).then_inc(s["brow_lo"], 1)
                mix(NT - 1)
                mean_square(1)
                stats(0)
                stats(1)

        with ExitStack() as st:
            s = Sems("f")
            (gsum, negmu, vsum, rstd, hsum, r2, amax2, m2, inv2, quant2, beta, factor), end = place(W + 32768, [
                (n, [P, 2], F32) for n in ("gsum", "negmu", "vsum", "rstd", "hsum", "r2", "amax2", "m2", "inv2",
                                            "quant2", "beta", "factor")])
            ps_q = st.enter_context(nc.psum_tensor("ps_q", [P, CK, P], BF16))
            ps_i = st.enter_context(nc.psum_tensor("ps_i", [P, INNER], F32))
            ps_k = st.enter_context(nc.psum_tensor("ps_k", [P, 2, IK // 2, P], BF16))
            ps_z = st.enter_context(nc.psum_tensor("ps_z", [P, C], F32))
            block = st.enter_context(nc.Block())
            FIRST, LAST = -2, NT + 2

            def there(t):
                return type(t) is not int or 0 <= t < NT

            def every_step(eng, step):
                for t in range(FIRST, 4):
                    step(t, t % 2)
                with eng.Fori(2, NT // 2 - 1) as j:
                    step(2 * j, 0)
                    step(2 * j + 1, 1)
                for t in range(NT - 2, LAST + 1):
                    step(t, t % 2)

            @block.sync
            def _(sp):
                for dst, src, n in ((lng_sb, lng, INNER), (lnb_sb, lnb, INNER), (b2_sb, b2, C)):
                    sp.dma_start(dst[:], src.to_broadcast([P, n])).then_inc(s["rows_in"], 16)

                def store(t, p):
                    sp.wait_ge(s["out_ready"], t + 1)
                    sp.dma_start(out[ds(t)].rearrange("a p n -> p (a n)"), out_sb[:, p]).then_inc(s[f"out{p}"], 16)

                with sp.Fori(0, NT // 2) as j:
                    store(2 * j, 0)
                    store(2 * j + 1, 1)
                for p in range(2):
                    sp.wait_ge(s[f"out{p}"], 16 * NT // 2)

            @block.gpsimd
            def _(pool):
                def tiny(out_, a, b, op, name):
                    pool.tensor_tensor(out_, a, b, op).then_inc(s[name], 1)

                def const(n):
                    return consts[:, n:n + 1]

                def after_square(t, p):
                    def col(v):
                        return v[:, p:p + 1]

                    pool.wait_ge(s["hsq"], t + 1)
                    tiny(col(hsum), col(hsum), const(1), ALU.mult, "tiny_h")
                    pool.wait_ge(s["tiny_h"], 3 * t + 1)
                    tiny(col(hsum), col(hsum), const(2), ALU.add, "tiny_h")
                    pool.wait_ge(s["tiny_h"], 3 * t + 2)
                    tiny(col(r2), col(hsum), half[:, 0:1], ALU.pow, "r2")
                    pool.wait_ge(s["peak"], t + 1)
                    tiny(col(inv2), col(m2), minus1[:, 0:1], ALU.pow, "tiny_h")
                    wait(pool, s["out_ready"], t - 1)
                    tiny(col(beta), col(m2), const(3), ALU.mult, "beta")
                    pool.wait_ge(s["tiny_h"], 3 * t + 3)
                    tiny(col(inv2), col(inv2), const(4), ALU.mult, "inv2")
                    pool.wait_ge(s["inv2"], t + 1)
                    tiny(col(quant2), col(r2), col(inv2), ALU.mult, "quant2")

                def after_variance(t, p):
                    def col(v):
                        return v[:, p:p + 1]

                    pool.wait_ge(s["var"], t + 1)
                    tiny(col(vsum), col(vsum), const(1), ALU.mult, "tiny_v")
                    pool.wait_ge(s["tiny_v"], 2 * t + 1)
                    tiny(col(vsum), col(vsum), const(2), ALU.add, "tiny_v")
                    pool.wait_ge(s["tiny_v"], 2 * t + 2)
                    tiny(col(rstd), col(vsum), half[:, 0:1], ALU.pow, "rstd")

                def step(t, p):
                    if there(t - 1):
                        after_square(t - 1, 1 - p)
                    if there(t):
                        if type(t) is int and t == 0:
                            pool.wait_ge(s["rows_in"], 48)
                        x_ = x1[:, ds(t)].rearrange("p a n -> p (a n)")
                        pool.tensor_tensor(x_, x_, b2_sb[:], ALU.add).then_inc(s["x_bias"], 1)
                        after_variance(t, p)

                pool.memset(minus1[:], -1.0).then_inc(s["consts"], 1)
                for n, value in ((1, 1.0 / INNER), (2, EPS), (4, 127.0)):
                    pool.memset(const(n), value).then_inc(s["consts"], 1)
                pool.tensor_scalar(const(3), wscale[:, 1:2], 1.0 / 127.0, None, ALU.mult).then_inc(s["consts"], 1)
                pool.wait_ge(s["consts"], 5)
                every_step(pool, step)

            @block.scalar
            def _(act):
                def step(t, p):
                    if there(t):
                        act.wait_ge(s["up_done"], t + 1)
                        wait(act, s["moved"], t - 1)
                        act.wait_ge(s["factor"], t + 1)
                        act.activation(hid5[:, p], ps_i[:], ACT.Tanh, scale=factor[:, p:p + 1]).then_inc(s["tanh"], 1)
                    if there(t - 2):
                        act.wait_ge(s["h_turned"], t - 1)
                        wait(act, s["down_done"], t - 2)
                        act.activation(hqT[:], ps_k[:].rearrange("p a k n -> p (a k) n"), ACT.Copy).then_inc(s["hqT"], 1)
                    if there(t - 1):
                        act.wait_ge(s["normed"], t)
                        act.wait_ge(s["var"], t)
                        act.activation(junk[:], hid5[:, 1 - p], ACT.Square, accum_out=hsum[:, 1 - p:2 - p]).then_inc(s["hsq"], 1)
                    if there(t):
                        act.wait_ge(s["silu2"], t + 1)
                        act.activation(hid5[:, p], pre[:], ACT.Gelu, scale=factor[:, p:p + 1], accum_out=gsum[:, p:p + 1]).then_inc(s["gelu"], 1)
                    if there(t):
                        act.wait_ge(s["gelu"], t + 1)
                        act.activation(negmu[:, p:p + 1], gsum[:, p:p + 1], ACT.Copy, scale=-1.0 / INNER).then_inc(s["negmu"], 1)
                        act.wait_ge(s["negmu"], t + 1)
                        wait(act, s["hsq"], t)
                        act.activation(junk[:], hid5[:, p], ACT.Square, bias=negmu[:, p:p + 1], accum_out=vsum[:, p:p + 1]).then_inc(s["var"], 1)
                    if there(t + 1):
                        act.activation(factor[:, 1 - p:2 - p], halfalpha[:, ds(t + 1)], ACT.Copy).then_inc(s["factor"], 1)
                    if there(t - 1):
                        act.wait_ge(s["quant2"], t)
                        wait(act, s["hq"], t - 1)
                        act.activation(moved[:], hid5[:, 1 - p], ACT.Copy, bias=ROUND, scale=quant2[:, 1 - p:2 - p]).then_inc(s["moved"], 1)
                    if there(t + 2):
                        wait(act, s["xq"], t + 2)
                        act.activation(moved1[:], z1[:, ds(t + 2)].rearrange("p a n -> p (a n)"), ACT.Copy, bias=ROUND,
                                       scale=quant1[:, ds(t + 2)]).then_inc(s["moved1"], 1)
                        act.activation(arow[:, p], f32(arows[:, ds(t + 2)].rearrange("r a n -> r (a n)")), ACT.Copy).then_inc(s["arow"], 1)

                every_step(act, step)

            @block.vector
            def _(dve):
                def step(t, p):
                    if there(t - 1):
                        dve.wait_ge(s["rstd"], t)
                        dve.wait_ge(s["centred"], t)
                        dve.scalar_tensor_tensor(out=hid5[:, 1 - p], in0=hid5[:, 1 - p], scalar=rstd[:, 1 - p:2 - p], in1=lnb_sb[:],
                                                 op0=ALU.mult, op1=ALU.add).then_inc(s["normed"], 1)
                    if there(t):
                        dve.wait_ge(s["tanh"], t + 1)
                        wait(dve, s["gelu"], t)
                        dve.scalar_tensor_tensor(out=pre[:], in0=hid5[:, p], scalar=1.0, in1=ps_i[:],
                                                 op0=ALU.add, op1=ALU.mult).then_inc(s["silu2"], 1)
                    if there(t + 1):
                        dve.wait_ge(s["x_turned"], t + 2)
                        wait(dve, s["up_done"], t)
                        dve.tensor_copy(xqT[:, 1 - p], ps_q[:]).then_inc(s["xqT"], 1)
                    if there(t - 1):
                        dve.wait_ge(s["normed"], t)
                        dve.tensor_reduce(amax2[:, 1 - p:2 - p], hid5[:, 1 - p], AX_X, ALU.max, apply_absolute_value=True).then_inc(s["amax"], 1)
                    if there(t - 3):
                        q = 1 - p
                        wait(dve, s[f"out{q}"], 8 * (t - 3 - q))
                        dve.wait_ge(s["beta"], t - 2)
                        dve.wait_ge(s["x_bias"], t - 2)
                        dve.wait_ge(s["down_done"], t - 2)
                        dve.scalar_tensor_tensor(out=out_sb[:, q], in0=ps_z[:], scalar=beta[:, q:q + 1],
                                                 in1=x1[:, ds(t - 3)].rearrange("p a n -> p (a n)"),
                                                 op0=ALU.mult, op1=ALU.add).then_inc(s["out_ready"], 1)
                    if there(t - 1):
                        dve.wait_ge(s["r2"], t)
                        dve.wait_ge(s["amax"], t)
                        dve.tensor_scalar(m2[:, 1 - p:2 - p], amax2[:, 1 - p:2 - p], r2[:, 1 - p:2 - p], 1e-5,
                                          ALU.mult, ALU.max).then_inc(s["peak"], 1)
                    if there(t):
                        if type(t) is int and t == 0:
                            dve.wait_ge(s["rows_in"], 48)
                        dve.wait_ge(s["var"], t + 1)
                        dve.scalar_tensor_tensor(out=hid5[:, p], in0=hid5[:, p], scalar=negmu[:, p:p + 1], in1=lng_sb[:],
                                                 op0=ALU.add, op1=ALU.mult).then_inc(s["centred"], 1)
                    if there(t - 1):
                        dve.wait_ge(s["moved"], t)
                        wait(dve, s["h_turned"], t - 1)
                        dve.tensor_scalar(hq[:], moved[:], ROUND, None, ALU.subtract).then_inc(s["hq"], 1)
                    if there(t + 2):
                        dve.wait_ge(s["moved1"], t + 3)
                        wait(dve, s["x_turned"], t + 2)
                        dve.tensor_scalar(xq[:], moved1[:], ROUND, None, ALU.subtract).then_inc(s["xq"], 1)

                every_step(dve, step)

            @block.tensor
            def _(pe):
                def step(t, p):
                    if there(t + 1):
                        pe.wait_ge(s["xqT"], t + 2)
                        wait(pe, s["silu2"], t + 1)
                        pe.wait_ge(s["arow"], t + 2)
                        for n in range(INNER // C):
                            for c in range(CK):
                                last = pe.matmul(ps_i[:, n * C:(n + 1) * C], xqT[:, 1 - p, c],
                                                 w1q[:, 2 * c + n // 2, (n % 2) * C:(n % 2 + 1) * C], start=c == 0, stop=False)
                            last = pe.matmul(ps_i[:, n * C:(n + 1) * C], arow[:, 1 - p], brow[:, n * C:(n + 1) * C],
                                             start=False, stop=True)
                        last.then_inc(s["up_done"], 1)
                    if there(t - 2):
                        pe.wait_ge(s["hqT"], t - 1)
                        wait(pe, s["out_ready"], t - 2)
                        for k in range(IK):
                            last = pe.matmul(ps_z[:], hqT[:, k], w2q[:, k // 2, (k % 2) * C:(k % 2 + 1) * C],
                                             start=k == 0, stop=k == IK - 1)
                        last.then_inc(s["down_done"], 1)
                    if there(t - 1):
                        pe.wait_ge(s["hq"], t)
                        wait(pe, s["hqT"], t - 1)
                        for k in range(IK):
                            last = pe.transpose(ps_k[:, k // 8, k % 8], hq[:, k * P:(k + 1) * P], ident_b[:])
                        last.then_inc(s["h_turned"], 1)
                    if there(t + 2):
                        pe.wait_ge(s["xq"], t + 3)
                        wait(pe, s["xqT"], t + 2)
                        for c in range(CK):
                            last = pe.transpose(ps_q[:, c], xq[:, c * P:(c + 1) * P], ident_b[:])
                        last.then_inc(s["x_turned"], 1)

                every_step(pe, step)




def laid_out(inputs):
    import numpy as np

    def a(name):
        return np.asarray(inputs[name])

    def by_channel(v):
        return v.reshape(B, T, CK, P).transpose(0, 2, 3, 1)

    def column(v):
        return v.reshape(CK, P).T

    def up_weights(w1, w3):
        return np.concatenate([w1, w3], axis=-2).swapaxes(-1, -2).reshape(*w1.shape[:-2], CK, P, -1)

    arrays = {
        "xT": by_channel(a("x")),
        "kT": by_channel(a("fside_BxSxS_0")),
        "x": a("x").reshape(NT, P, C),
        "cond": a("cond_512").T,
        "wu": np.stack([column(a(n)) for n in ("L0_cond_w", "L0_cond_u", "L1_cond_w", "L1_cond_u")], axis=1),
        "gate": a("L0_ffn_gate_w").T.reshape(CK, P, E).transpose(1, 0, 2),
        "sw13": np.stack([a("L0_ffn_sw1").T.reshape(CK, P, SF), a("L0_ffn_sw3").T.reshape(CK, P, SF)]),
        "sw2": a("L0_ffn_sw2").T,
        "w13": up_weights(a("L0_ffn_w1"), a("L0_ffn_w3")),
        "w2": a("L0_ffn_w2").swapaxes(1, 2),
        "wp": np.concatenate([
            a("L1_ffn_w1").T.reshape(CK, P, 2, PIECE).transpose(0, 2, 1, 3).reshape(NPIECE, P, PIECE),
            a("L1_ffn_w2").T.reshape(NPIECE, 2, P, C).transpose(0, 2, 1, 3).reshape(NPIECE, P, PIECE)]),
        "b1": a("L1_ffn_b1").reshape(1, INNER),
        "lng": a("L1_ffn_ln_g").reshape(1, INNER),
        "lnb": a("L1_ffn_ln_b").reshape(1, INNER),
        "b2": a("L1_ffn_b2").reshape(1, C),
    }
    return {n: np.ascontiguousarray(v) for n, v in arrays.items()}


def kernel(**inputs):
    import concourse.bacc as bacc
    from concourse.bass_utils import run_bass_kernel_spmd

    nc = bacc.Bacc("TRN2", target_bir_lowering=False, num_devices=1)
    arrays = laid_out(inputs)
    args = [nc.dram_tensor(n, v.shape, F32, kind="ExternalInput").ap() for n, v in arrays.items()]
    args.append(nc.dram_tensor("out", (NT, P, C), F32, kind="ExternalOutput").ap())
    args.append(nc.dram_tensor("xslots", (SLOTS, C), F32, kind="Internal").ap())
    args.append(nc.dram_tensor("yslots", (SLOTS, C), F32, kind="Internal").ap())
    args.append(nc.dram_tensor("yshared", (NT, P, C), F32, kind="Internal").ap())
    build(nc, *args)
    got = run_bass_kernel_spmd(nc, [arrays], core_ids=[0])
    return got.results[0]["out"].reshape(B, T, C)
```
